# Optimizing a Trainium2 kernel written in Bass

```python
import numpy as np
import jax
import jax.numpy as jnp

def _softmax(x, axis=-1):
    return jax.nn.softmax(x, axis=axis)

def _gelu(x):
    return jax.nn.gelu(x, approximate=True)

def _silu(x):
    return jax.nn.silu(x)

def _sigmoid(x):
    return jax.nn.sigmoid(x)

def _layernorm(x, axis=-1, eps=1e-05):
    m = jnp.mean(x, axis=axis, keepdims=True)
    v = jnp.var(x, axis=axis, keepdims=True)
    return (x - m) / jnp.sqrt(v + eps)

def _scatter_add(tgt, idx, src, axis=0):
    return tgt.at[idx].add(src)

def _segment_sum(src, seg, n):
    return jax.ops.segment_sum(src, seg, n)
kernel_name = 'mk_gnn_preln_d2_gnn_r64_84b6fc'

def setup_inputs(seed: int=0):
    np.random.seed(seed)
    _w = jnp.asarray

    def _rec_inputs():
        import jax
        import jax.numpy as jnp
        _gk = jax.random.key(seed)
        x = -0.0003713 + 1 * jax.random.normal(jax.random.fold_in(_gk, 1), (50000, 256), jnp.float32)
        src = jax.random.randint(jax.random.fold_in(_gk, 2), (12500,), 0, 50000, jnp.int32)
        dst = jax.random.randint(jax.random.fold_in(_gk, 3), (12500,), 0, 50000, jnp.int32)
        _o = jnp.argsort(dst, stable=True)
        src = src[_o]
        dst = dst[_o]
        edge_attr_16 = 0.000130101 + 1.00012 * jax.random.normal(jax.random.fold_in(_gk, 12), (12500, 16), jnp.float32)
        return (x, src, dst, edge_attr_16)
    x, src, dst, edge_attr_16 = _rec_inputs()

    def _L0_gnn_setup():
        import jax, jax.numpy as jnp
        import numpy as np
        NEG_SLOPE = 0.2
        N_NODES = 50000
        N_EDGES = 12500

        def gat_conv(h, src, dst, W, al, ar, residual):
            N = h.shape[0]
            H, D = al.shape
            feat = (h @ W).reshape(N, H, D)
            el = jnp.sum(feat * al, axis=-1)
            er = jnp.sum(feat * ar, axis=-1)
            e = jax.nn.leaky_relu(el[src] + er[dst], NEG_SLOPE)
            emax = jax.ops.segment_max(e, dst, num_segments=N)
            ex = jnp.exp(e - emax[dst])
            denom = jax.ops.segment_sum(ex, dst, num_segments=N)
            a = ex / denom[dst]
            msg = feat[src] * a[:, :, None]
            rst = jax.ops.segment_sum(msg, dst, num_segments=N)
            if residual:
                rst = rst + h.reshape(N, H, D)
            return jax.nn.elu(rst).reshape(N, H * D)
        key = jax.random.key(seed)
        ks = jax.random.split(key, 9)
        features = jax.random.normal(ks[0], (N_NODES, 256), dtype=jnp.float32)
        src = jax.random.randint(ks[1], (N_EDGES,), 0, N_NODES, dtype=jnp.int32)
        dst = jax.random.randint(ks[2], (N_EDGES,), 0, N_NODES, dtype=jnp.int32)
        s1 = 1.0 / np.sqrt(256.0)
        W1 = jax.random.normal(ks[3], (256, 256), dtype=jnp.float32) * s1
        al1 = jax.random.normal(ks[4], (4, 64), dtype=jnp.float32) * 0.1
        ar1 = jax.random.normal(ks[5], (4, 64), dtype=jnp.float32) * 0.1
        W2 = jax.random.normal(ks[6], (256, 256), dtype=jnp.float32) * s1
        al2 = jax.random.normal(ks[7], (4, 64), dtype=jnp.float32) * 0.1
        ar2 = jax.random.normal(ks[8], (4, 64), dtype=jnp.float32) * 0.1
        return {'features': features, 'src': src, 'dst': dst, 'W1': W1, 'al1': al1, 'ar1': ar1, 'W2': W2, 'al2': al2, 'ar2': ar2}
    _L0_gnn_all = _L0_gnn_setup()
    _L0_gnn_in = {k: v for k, v in _L0_gnn_all.items() if k in ('W1', 'al1', 'ar1', 'W2', 'al2', 'ar2')}
    del _L0_gnn_all

    def _L1_gnn_setup():
        import jax, jax.numpy as jnp
        import numpy as np
        N, NODE_DIM, EDGE_DIM, HIDDEN, E = (10000, 256, 16, 512, 5000)
        key = jax.random.key(seed)
        ks = jax.random.split(key, 12)

        def lin(kw, kb, fan_in, fan_out):
            bound = 1.0 / np.sqrt(fan_in)
            W = jax.random.uniform(kw, (fan_in, fan_out), jnp.float32, -bound, bound)
            b = jax.random.uniform(kb, (fan_out,), jnp.float32, -bound, bound)
            return (W, b)
        node_features = jax.random.normal(ks[0], (N, NODE_DIM), jnp.float32)
        edge_index = jax.random.randint(ks[1], (2, E), 0, N, jnp.int32)
        edge_features = jax.random.normal(ks[2], (E, EDGE_DIM), jnp.float32)
        mW1, mb1 = lin(ks[3], ks[4], 2 * NODE_DIM + EDGE_DIM, HIDDEN)
        mW2, mb2 = lin(ks[5], ks[6], HIDDEN, NODE_DIM)
        uW1, ub1 = lin(ks[7], ks[8], 2 * NODE_DIM, HIDDEN)
        uW2, ub2 = lin(ks[9], ks[10], HIDDEN, NODE_DIM)
        return {'node_features': node_features, 'edge_index': edge_index, 'edge_features': edge_features, 'mW1': mW1, 'mb1': mb1, 'mW2': mW2, 'mb2': mb2, 'uW1': uW1, 'ub1': ub1, 'uW2': uW2, 'ub2': ub2}
    _L1_gnn_all = _L1_gnn_setup()
    _L1_gnn_in = {k: v for k, v in _L1_gnn_all.items() if k in ('mW1', 'mb1', 'mW2', 'mb2', 'uW1', 'ub1', 'uW2', 'ub2')}
    del _L1_gnn_all
    return {'x': x, 'src': src, 'dst': dst, 'edge_attr_16': edge_attr_16, 'L0_gnn_W1': _L0_gnn_in['W1'], 'L0_gnn_al1': _L0_gnn_in['al1'], 'L0_gnn_ar1': _L0_gnn_in['ar1'], 'L0_gnn_W2': _L0_gnn_in['W2'], 'L0_gnn_al2': _L0_gnn_in['al2'], 'L0_gnn_ar2': _L0_gnn_in['ar2'], 'L1_gnn_mW1': _L1_gnn_in['mW1'], 'L1_gnn_mb1': _L1_gnn_in['mb1'], 'L1_gnn_mW2': _L1_gnn_in['mW2'], 'L1_gnn_mb2': _L1_gnn_in['mb2'], 'L1_gnn_uW1': _L1_gnn_in['uW1'], 'L1_gnn_ub1': _L1_gnn_in['ub1'], 'L1_gnn_uW2': _L1_gnn_in['uW2'], 'L1_gnn_ub2': _L1_gnn_in['ub2']}

def reference(x, src, dst, edge_attr_16, L0_gnn_W1, L0_gnn_al1, L0_gnn_ar1, L0_gnn_W2, L0_gnn_al2, L0_gnn_ar2, L1_gnn_mW1, L1_gnn_mb1, L1_gnn_mW2, L1_gnn_mb2, L1_gnn_uW1, L1_gnn_ub1, L1_gnn_uW2, L1_gnn_ub2):
    import jax
    import jax.numpy as jnp

    def _L0_gnn_ref(features, src, dst, W1, al1, ar1, W2, al2, ar2):
        import jax, jax.numpy as jnp
        import numpy as np
        NEG_SLOPE = 0.2
        N_NODES = 50000
        N_EDGES = 12500

        def gat_conv(h, src, dst, W, al, ar, residual):
            N = h.shape[0]
            H, D = al.shape
            feat = (h @ W).reshape(N, H, D)
            el = jnp.sum(feat * al, axis=-1)
            er = jnp.sum(feat * ar, axis=-1)
            e = jax.nn.leaky_relu(el[src] + er[dst], NEG_SLOPE)
            emax = jax.ops.segment_max(e, dst, num_segments=N)
            ex = jnp.exp(e - emax[dst])
            denom = jax.ops.segment_sum(ex, dst, num_segments=N)
            a = ex / denom[dst]
            msg = feat[src] * a[:, :, None]
            rst = jax.ops.segment_sum(msg, dst, num_segments=N)
            if residual:
                rst = rst + h.reshape(N, H, D)
            return jax.nn.elu(rst).reshape(N, H * D)
        h = gat_conv(features, src, dst, W1, al1, ar1, residual=False)
        h = gat_conv(h, src, dst, W2, al2, ar2, residual=True)
        return h

    def _L1_gnn_ref(node_features, edge_index, edge_features, mW1, mb1, mW2, mb2, uW1, ub1, uW2, ub2):
        import jax, jax.numpy as jnp
        import numpy as np
        N, NODE_DIM, EDGE_DIM, HIDDEN, E = (10000, 256, 16, 512, 5000)
        i_idx = edge_index[0]
        j_idx = edge_index[1]
        node_i = node_features[i_idx]
        node_j = node_features[j_idx]
        msg_input = jnp.concatenate([node_i, node_j, edge_features], axis=-1)
        h = jax.nn.relu(msg_input @ mW1 + mb1)
        messages = h @ mW2 + mb2
        aggregated = jax.ops.segment_sum(messages, i_idx, num_segments=node_features.shape[0])
        update_input = jnp.concatenate([node_features, aggregated], axis=-1)
        u = jax.nn.relu(update_input @ uW1 + ub1)
        updated = u @ uW2 + ub2
        return node_features + updated
    edge_index = jnp.stack([src, dst])
    h = jnp.maximum(_layernorm(x, axis=-1), 0.0)
    x = x + _L0_gnn_ref(h, src, dst, L0_gnn_W1, L0_gnn_al1, L0_gnn_ar1, L0_gnn_W2, L0_gnn_al2, L0_gnn_ar2)
    h = jnp.maximum(_layernorm(x, axis=-1), 0.0)
    x = x + _L1_gnn_ref(h, edge_index, edge_attr_16, L1_gnn_mW1, L1_gnn_mb1, L1_gnn_mW2, L1_gnn_mb2, L1_gnn_uW1, L1_gnn_ub1, L1_gnn_uW2, L1_gnn_ub2)
    return x

_drawn_inputs = setup_inputs


def setup_inputs(seed=0):
    import zlib

    import numpy as np

    out = dict(_drawn_inputs(seed))
    spreads = {}
    factors = {'edge_attr_16': 8.0,
     'L0_gnn_al1': 5.712,
     'L0_gnn_ar1': 41.96,
     'L0_gnn_al2': 38.804,
     'L0_gnn_ar2': 64.0,
     'L1_gnn_mW1': 7.811,
     'L1_gnn_mb1': 24.775,
     'L1_gnn_mW2': 6.377,
     'L1_gnn_mb2': 49.887,
     'L1_gnn_ub1': 8.0,
     'L1_gnn_ub2': 3.47}
    for name, (base, spread) in spreads.items():
        noise = np.random.default_rng([zlib.crc32(name.encode()), seed]).standard_normal(out[name].shape)
        drawn = base * np.exp(spread * noise) if base else spread * noise
        out[name] = jnp.asarray(drawn.astype(out[name].dtype))
    for name, factor in factors.items():
        out[name] = (out[name] * factor).astype(out[name].dtype)
    return out
```

```python
from contextlib import ExitStack

import numpy as np
import concourse.bass as bass
from concourse import mybir

F32 = mybir.dt.float32
F16 = mybir.dt.float16
I32 = mybir.dt.int32
ALU = mybir.AluOpType
ACT = mybir.ActivationFunctionType
AX = mybir.AxisListType

P = 128
N_NODES, D = 50000, 256
N_EDGES, D_EDGE = 12500, 16
HEADS = 4
D_HEAD = D // HEADS
HIDDEN = 512
KD = D // P
KH = HIDDEN // P
TILES = 100
EDGES = P * TILES
PARTS_USED = N_EDGES // TILES
assert PARTS_USED * TILES == N_EDGES and PARTS_USED < P
NODE_TILES = -(-N_NODES // P)
LAST_ROWS = N_NODES - (NODE_TILES - 1) * P
PAD_KEY = NODE_TILES * P - 1
assert PAD_KEY >= N_NODES
NO_ROW = EDGES
G = 256
GT = G // P
GROUPS = EDGES // G
ROW_INTS = 4
EPS = 1e-5
NEG_SLOPE = 0.2
FAR = 1e30


def build(nc, x, src, dst, attr, W1, al1, ar1, W2, al2, ar2, mW1, mb1, mW2, mb2, uW1, ub1, uW2, ub2, out):
    ctx = ExitStack()

    def dram(name, shape, dt):
        return nc.dram_tensor(name, shape, dt, kind="Internal").ap()

    by_dst = dram("by_dst", [EDGES + 1, ROW_INTS], I32)
    by_src = dram("by_src", [EDGES + 1, ROW_INTS], I32)
    by_src_attr = dram("by_src_attr", [EDGES + 1, D_EDGE], F32)
    end_of = dram("end_of", [P * NODE_TILES, 1], I32)
    H1 = dram("H1", [EDGES + 1, D], F32)
    X1 = dram("X1", [EDGES + 1, D], F32)
    GS = dram("GS", [EDGES, HIDDEN], F32)

    with ctx:
        def sb(name, shape, dt=F32):
            return ctx.enter_context(nc.sbuf_tensor(name, shape, dt))

        def sem(name):
            return ctx.enter_context(nc.semaphore(name))

        ident = sb("ident", [P, P])
        ident16 = sb("ident16", [P, P], F16)
        tri = sb("tri", [P, P])
        trilow = sb("trilow", [P, P])
        ones = sb("ones", [P, P])
        iota_t = sb("iota_t", [P, NODE_TILES], F16)
        eps = sb("eps", [P, 1])
        headsel = sb("headsel", [HEADS, KD, P])
        w1 = sb("w1", [P, KD, D])
        w2 = sb("w2", [P, KD, D])
        wa = sb("wa", [P, 4, KD, HEADS])
        mw1 = sb("mw1", [P, 2 * KD, HIDDEN])
        mw1e = sb("mw1e", [D_EDGE, HIDDEN])
        mw2 = sb("mw2", [P, KH, D])
        uw1 = sb("uw1", [P, 2 * KD, HIDDEN])
        uw2 = sb("uw2", [P, KH, D])
        mb1c = sb("mb1c", [P, KH])
        mb2c = sb("mb2c", [P, KD])
        ub1r = sb("ub1r", [P, HIDDEN])
        ub2r = sb("ub2r", [P, D])
        end_d = sb("end_d", [P, NODE_TILES], I32)
        end_s = sb("end_s", [P, NODE_TILES], I32)

        def wait(eng, signal, n):
            if not (isinstance(n, int) and n <= 0):
                eng.wait_ge(signal, n)

        def wait_apart(pool, signal, n):
            if not (isinstance(n, int) and n <= 0):
                pool.wait_ge(signal, n)
                pool.sem_inc(apart, 1)

        def overlapped(eng, front, back, n):
            def two_steps(i):
                front(2 * i + 1, 1, i)
                back(2 * i, 0, i)
                front(2 * i + 2, 0, i + 1)
                back(2 * i + 1, 1, i)

            front(0, 0, 0)
            two_steps(0)
            with eng.Fori(1, (n - 2) // 2) as i:
                two_steps(i)
            front(n - 1, 1, n // 2 - 1)
            back(n - 2, 0, n // 2 - 1)
            back(n - 1, 1, n // 2 - 1)

        def nothing(g, s, i):
            pass

        apart = sem("apart")

        with ExitStack() as c0:
            def sb0(name, shape, dt=F32):
                return c0.enter_context(nc.sbuf_tensor(name, shape, dt))

            av = sb0("av", [P, 4, D])
            prod = sb0("prod", [P, 4, KD, D])
            key = sb0("key", [P, 2, TILES], I32)
            hi_i = sb0("hi_i", [P, 2, TILES], I32)
            lo_i = sb0("lo_i", [P, 2, TILES], I32)
            keyf = sb0("keyf", [P, 2, TILES])
            hi = sb0("hi", [P, 2, TILES])
            lo = sb0("lo", [P, 2, TILES])
            flat = sb0("flat", [P, 2, TILES], I32)
            attrs = sb0("attrs", [P, TILES, D_EDGE])
            zrow = sb0("zrow", [1, D])
            sentinel = sb0("sentinel", [1, ROW_INTS], I32)
            ohH = sb0("ohH", [P, 2, 2, NODE_TILES], F16)
            ohL = sb0("ohL", [P, 2, 2, P], F16)
            cnt = sb0("cnt", [P, 2, NODE_TILES])
            tot = sb0("tot", [P, 2, NODE_TILES])
            cum = sb0("cum", [P, 2, NODE_TILES])
            first = sb0("first", [P, 2, NODE_TILES])
            has = sb0("has", [P, 2, NODE_TILES])
            onesr = sb0("onesr", [P, NODE_TILES])

            w_in, k_in, a_in, cst, prodd, wad = (sem(n) for n in ("weights_in", "keys_in", "attr_in", "consts_made", "prod_made", "wa_made"))
            keyset, keysplit, z_out, z_set = (sem(n) for n in ("keys_preset", "keys_split", "zeros_out", "zeros_set"))
            with nc.Block() as block:
                @block.sync
                def _(sp):
                    sp.wait_ge(keyset, 1)
                    sp.dma_start(key[0:PARTS_USED, 0, :], dst.rearrange("(p t) -> p t", t=TILES)).then_inc(k_in, 16)
                    sp.dma_start(key[0:PARTS_USED, 1, :], src.rearrange("(p t) -> p t", t=TILES)).then_inc(k_in, 16)
                    sp.dma_start(attrs[0:PARTS_USED, :, :], attr.rearrange("(p t) f -> p t f", t=TILES)).then_inc(a_in, 16)
                    sp.dma_start(w1[:, :, :], W1.rearrange("(k p) n -> p k n", p=P)).then_inc(w_in, 16)
                    sp.dma_start(w2[:, :, :], W2.rearrange("(k p) n -> p k n", p=P)).then_inc(w_in, 16)
                    for i, a in enumerate((al1, ar1, al2, ar2)):
                        sp.dma_start(av[:, i, :], a.rearrange("h d -> (h d)").partition_broadcast(P)).then_inc(w_in, 16)
                    sp.dma_start(mw1[:, :, :], mW1[0:2 * D, :].rearrange("(k p) n -> p k n", p=P)).then_inc(w_in, 16)
                    sp.dma_start(mw1e[:, :], mW1[2 * D:2 * D + D_EDGE, :]).then_inc(w_in, 16)
                    sp.dma_start(mw2[:, :, :], mW2.rearrange("(k p) n -> p k n", p=P)).then_inc(w_in, 16)
                    sp.dma_start(uw1[:, :, :], uW1.rearrange("(k p) n -> p k n", p=P)).then_inc(w_in, 16)
                    sp.dma_start(uw2[:, :, :], uW2.rearrange("(k p) n -> p k n", p=P)).then_inc(w_in, 16)
                    with nc.allow_non_contiguous_dma(reason="bias columns, once"):
                        sp.dma_start(mb1c[:, :], mb1.rearrange("(k p) -> p k", p=P)).then_inc(w_in, 16)
                        sp.dma_start(mb2c[:, :], mb2.rearrange("(k p) -> p k", p=P)).then_inc(w_in, 16)
                    sp.dma_start(ub1r[:, :], ub1.partition_broadcast(P)).then_inc(w_in, 16)
                    sp.dma_start(ub2r[:, :], ub2.partition_broadcast(P)).then_inc(w_in, 16)
                    sp.wait_ge(z_set, 2)
                    sp.dma_start(H1[NO_ROW:NO_ROW + 1, :], zrow[:, :]).then_inc(z_out, 16)
                    sp.dma_start(X1[NO_ROW:NO_ROW + 1, :], zrow[:, :]).then_inc(z_out, 16)
                    sp.dma_start(by_dst[0:1, :], sentinel[:, :]).then_inc(z_out, 16)
                    sp.dma_start(by_src[0:1, :], sentinel[:, :]).then_inc(z_out, 16)
                    sp.wait_ge(z_out, 64)
                    sp.wait_ge(w_in, 16 * 15)
                    sp.wait_ge(a_in, 16)

                @block.gpsimd
                def _(pool):
                    pool.memset(ident[:, :], 0.0)
                    pool.memset(tri[:, :], 1.0)
                    pool.memset(trilow[:, :], 1.0)
                    pool.memset(headsel[:, :, :], 1.0)
                    pool.iota(iota_t[:, :], pattern=[[1, NODE_TILES]], base=0, channel_multiplier=0,
                              allow_small_or_imprecise_dtypes=True)
                    pool.drain()
                    pool.affine_select(out=ident[:, :], in_=ident[:, :], compare_op=ALU.not_equal, fill=1.0,
                                       base=0, pattern=[[-1, P]], channel_multiplier=1)
                    pool.affine_select(out=tri[:, :], in_=tri[:, :], compare_op=ALU.is_ge, fill=0.0,
                                       base=-1, pattern=[[1, P]], channel_multiplier=-1)
                    pool.affine_select(out=trilow[:, :], in_=trilow[:, :], compare_op=ALU.is_ge, fill=0.0,
                                       base=-1, pattern=[[-1, P]], channel_multiplier=1)
                    pool.affine_select(out=headsel[:, :, :], in_=headsel[:, :, :], compare_op=ALU.is_ge, fill=0.0,
                                       base=0, pattern=[[P, KD], [1, P]], channel_multiplier=-D_HEAD)
                    pool.drain()
                    pool.affine_select(out=headsel[:, :, :], in_=headsel[:, :, :], compare_op=ALU.is_ge, fill=0.0,
                                       base=D_HEAD - 1, pattern=[[-P, KD], [-1, P]], channel_multiplier=D_HEAD)
                    pool.tensor_copy(ident16[:, :], ident[:, :])

                @block.vector
                def _(dve):
                    dve.memset(attrs[:, :, :], 0.0)
                    dve.memset(key[:, :, :], PAD_KEY)
                    dve.drain().then_inc(keyset, 1)
                    dve.memset(zrow[:, :], 0.0).then_inc(z_set, 1)
                    dve.memset(sentinel[:, :], -1).then_inc(z_set, 1)
                    dve.memset(ones[:, :], 1.0)
                    dve.memset(onesr[:, :], 1.0)
                    dve.memset(eps[:, :], EPS)
                    dve.wait_ge(k_in, 32)
                    dve.tensor_scalar(hi_i[:, :, :], key[:, :, :], 7, None, ALU.arith_shift_right)
                    dve.tensor_scalar(lo_i[:, :, :], key[:, :, :], P - 1, None, ALU.bitwise_and)
                    dve.tensor_copy(keyf[:, :, :], key[:, :, :])
                    dve.drain()
                    dve.tensor_copy(hi[:, :, :], hi_i[:, :, :])
                    dve.tensor_copy(lo[:, :, :], lo_i[:, :, :])
                    dve.drain()
                    dve.scalar_tensor_tensor(flat[:, :, :], lo[:, :, :], float(NODE_TILES), hi[:, :, :], ALU.mult, ALU.add)
                    dve.wait_ge(w_in, 16 * 15)
                    for i in range(4):
                        w = (w1, w1, w2, w2)[i]
                        for k in range(KD):
                            dve.tensor_tensor(prod[:, i, k, :], w[:, k, :], av[:, i, :], ALU.mult)
                    dve.drain()
                    dve.tensor_reduce(wa[:, :, :, :].rearrange("p i k h -> p (i k h)"),
                                      prod[:, :, :, :].rearrange("p i k (h d) -> p (i k h) d", h=HEADS), AX.X, ALU.add)

            cnt_ps = [c0.enter_context(nc.psum_tensor(f"cnt_ps{k}", [P, 512], F32)) for k in range(2)]
            onehot, counted, slot_free, table_up = (sem(n) for n in ("onehot_made", "tile_counted", "onehot_free", "tables_stored"))
            cum_ps, cnt_done, seeded = (sem(n) for n in ("sums_made", "cnt_copied", "starts_seeded"))
            first_done = sem("first_made")
            tot_ps = [c0.enter_context(nc.psum_tensor(f"tot_ps{k}", [P, 512], F32)) for k in range(2)]
            pre_ps = [c0.enter_context(nc.psum_tensor(f"pre_ps{k}", [P, 512], F32)) for k in range(2)]

            def make_onehots(dve, t, slot):
                for k in range(2):
                    dve.tensor_scalar(ohH[:, slot, k, :], iota_t[:, :], hi[:, k, bass.ds(t, 1)], None, ALU.is_equal)
                    last = dve.tensor_scalar(ohL[:, slot, k, :], iota_t[:, 0:P], lo[:, k, bass.ds(t, 1)], None, ALU.is_equal)
                return last

            with nc.Block() as block:
                @block.vector
                def _(dve):
                    with dve.Fori(0, TILES // 2) as i:
                        for slot in range(2):
                            dve.wait_ge(slot_free, 2 * i + slot + 1)
                            make_onehots(dve, 2 * i + slot, slot).then_inc(onehot, 1)
                    dve.wait_ge(counted, 1)
                    for k in range(2):
                        dve.tensor_copy(cnt[:, k, :], cnt_ps[k][:, 0:NODE_TILES])
                    dve.drain().then_inc(cnt_done, 1)
                    dve.wait_ge(cum_ps, 1)
                    for k in range(2):
                        dve.tensor_copy(tot[:, k, :], tot_ps[k][:, 0:NODE_TILES])
                    dve.drain()
                    for k in range(2):
                        dve.tensor_tensor_scan(cum[:, k, :], onesr[:, :], tot[:, k, :], 0.0, ALU.mult, ALU.add)
                    dve.drain()
                    dve.tensor_tensor(cum[:, :, :], cum[:, :, :], tot[:, :, :], ALU.subtract)
                    dve.tensor_scalar(has[:, :, :], cnt[:, :, :], 0.5, None, ALU.is_gt)
                    dve.drain()
                    for k in range(2):
                        dve.tensor_tensor(first[:, k, :], cum[:, k, :], pre_ps[k][:, 0:NODE_TILES], ALU.add)
                    dve.drain().then_inc(first_done, 1)
                    dve.scalar_tensor_tensor(tot[:, :, :], first[:, :, :], float(-1 - NO_ROW), cnt[:, :, :], ALU.add, ALU.add)
                    dve.drain()
                    dve.tensor_tensor(tot[:, :, :], tot[:, :, :], has[:, :, :], ALU.mult)
                    dve.drain()
                    dve.tensor_scalar(end_d[:, :], tot[:, 0, :], float(NO_ROW), None, ALU.add)
                    dve.tensor_scalar(end_s[:, :], tot[:, 1, :], float(NO_ROW), None, ALU.add)
                    dve.drain().then_inc(table_up, 1)

                @block.tensor
                def _(pe):
                    pe.sem_inc(slot_free, 2)
                    pe.wait_ge(onehot, 1)
                    for k in range(2):
                        pe.matmul(cnt_ps[k][:, 0:NODE_TILES], ohL[:, 0, k, :], ohH[:, 0, k, :], start=True, stop=False,
                                  skip_group_check=True)
                    pe.drain().then_inc(slot_free, 1)
                    pe.wait_ge(onehot, 2)
                    for k in range(2):
                        pe.matmul(cnt_ps[k][:, 0:NODE_TILES], ohL[:, 1, k, :], ohH[:, 1, k, :], start=False, stop=False,
                                  skip_group_check=True)
                    pe.drain().then_inc(slot_free, 1)
                    with pe.Fori(1, TILES // 2) as i:
                        for slot in range(2):
                            pe.wait_ge(onehot, 2 * i + slot + 1)
                            for k in range(2):
                                mm = pe.matmul(cnt_ps[k][:, 0:NODE_TILES], ohL[:, slot, k, :], ohH[:, slot, k, :],
                                               start=False, stop=False, skip_group_check=True)
                            mm.then_inc(slot_free, 1)
                    pe.drain().then_inc(counted, 1)
                    pe.wait_ge(cnt_done, 1)
                    for k in range(2):
                        pe.matmul(pre_ps[k][:, 0:NODE_TILES], tri[:, :], cnt[:, k, :], start=True, stop=True)
                        mm = pe.matmul(tot_ps[k][:, 0:NODE_TILES], ones[:, :], cnt[:, k, :], start=True, stop=True)
                    mm.then_inc(cum_ps, 1)
                    pe.wait_ge(first_done, 1)
                    for k in range(2):
                        pe.matmul(cnt_ps[k][:, 0:NODE_TILES], ident[:, :], first[:, k, :], start=True, stop=False,
                                  skip_group_check=True)

                @block.sync
                def _(sp):
                    sp.wait_ge(table_up, 1)
                    sp.dma_start(end_of.rearrange("(p n) o -> p (n o)", p=P), end_d[:, :]).then_inc(table_up, 16)
                    sp.wait_ge(table_up, 17)

            snap = sb0("snap", [P, 2, 2, NODE_TILES])
            diag = sb0("diag", [P, 2, 2, P])
            lT = sb0("lT", [P, 2, 2, P])
            before = sb0("before", [P, 2, TILES])
            within = sb0("within", [P, 2, TILES])
            place = sb0("place", [P, 2, TILES], I32)
            junk = sb0("junk", [P, 2, NODE_TILES])
            junk2 = sb0("junk2", [P, 2, P])
            pick_ps = tot_ps
            keyrow_ps = [p[:, 0:2 * P].rearrange("p (k n) -> p k n", k=2) for p in pre_ps]
            lT_ps = [c0.enter_context(nc.psum_tensor(f"lT_ps{s}", [P, 1024], F16))[:, 0:2 * P] for s in range(2)]
            oh2, rows_up, lT_up, snapped, advanced, picked = (sem(n) for n in (
                "p2_onehot", "p2_keyrows", "p2_lT", "p2_snapped", "p2_advanced", "p2_picked"))
            lTc, tile_done, placed = (sem(n) for n in ("p2_lT_copied", "p2_tile_done", "placed"))
            with nc.Block() as block:
                @block.vector
                def _(dve):
                    def finish(t, slot):
                        dve.wait_ge(picked, t + 1)
                        for k in range(2):
                            dve.scalar_tensor_tensor(junk[:, k, :], pick_ps[k][:, 0:NODE_TILES], 1.0,
                                                     ohH[:, slot, k, :], ALU.mult, ALU.mult,
                                                     accum_out=before[:, k, bass.ds(t, 1)])
                            dve.scalar_tensor_tensor(junk2[:, k, :], keyrow_ps[slot][:, k, :], keyf[:, k, bass.ds(t, 1)],
                                                            trilow[:, :], ALU.is_equal, ALU.mult,
                                                            accum_out=within[:, k, bass.ds(t, 1)])
                        dve.drain().then_inc(tile_done, 1)

                    def begin(t, slot):
                        make_onehots(dve, t, slot)
                        for k in range(2):
                            dve.tensor_scalar(diag[:, slot, k, :], ident[:, :], keyf[:, k, bass.ds(t, 1)], None, ALU.mult)
                        dve.drain().then_inc(oh2, 1)

                    dve.sem_inc(tile_done, 1)
                    begin(0, 0)
                    with dve.Fori(0, TILES // 2 - 1) as i:
                        begin(2 * i + 1, 1)
                        finish(2 * i, 0)
                        begin(2 * i + 2, 0)
                        finish(2 * i + 1, 1)
                    begin(TILES - 1, 1)
                    finish(TILES - 2, 0)
                    finish(TILES - 1, 1)
                    dve.tensor_tensor(before[:, :, :], before[:, :, :], within[:, :, :], ALU.add)
                    dve.drain()
                    dve.tensor_scalar(place[:, :, :], before[:, :, :], 1.0, None, ALU.add).then_inc(placed, 1)

                @block.tensor
                def _(pe):
                    with pe.Fori(0, TILES // 2) as i:
                        for slot in range(2):
                            pe.wait_ge(oh2, 2 * i + slot + 1)
                            for k in range(2):
                                mm = pe.transpose(lT_ps[slot][:, k * P:(k + 1) * P], ohL[:, slot, k, :], ident16[:, :])
                            mm.then_inc(lT_up, 1)
                            for k in range(2):
                                mm = pe.matmul(keyrow_ps[slot][:, k, :], ones[:, :], diag[:, slot, k, :], start=True, stop=True)
                            pe.wait_ge(lTc, 2 * i + slot + 1)
                            for k in range(2):
                                mm = pe.matmul(cnt_ps[k][:, 0:NODE_TILES], ohL[:, slot, k, :], ohH[:, slot, k, :],
                                               start=False, stop=False, skip_group_check=True)
                            mm.then_inc(advanced, 1)
                            pe.wait_ge(tile_done, 2 * i + slot + 1)
                            for k in range(2):
                                mm = pe.matmul(pick_ps[k][:, 0:NODE_TILES], lT[:, slot, k, :], snap[:, slot, k, :],
                                               start=True, stop=True)
                            mm.then_inc(picked, 1)

                @block.scalar
                def _(act):
                    act.sem_inc(advanced, 1)
                    with act.Fori(0, TILES // 2) as i:
                        for slot in range(2):
                            act.wait_ge(advanced, 2 * i + slot + 1)
                            for k in range(2):
                                act.activation(snap[:, slot, k, :], cnt_ps[k][:, 0:NODE_TILES], ACT.Copy)
                            act.wait_ge(lT_up, 2 * i + slot + 1)
                            act.activation(lT[:, slot, :, :].rearrange("p k n -> p (k n)"),
                                           lT_ps[slot], ACT.Copy).then_inc(lTc, 1)

            SC = 4
            row4 = sb0("row4", [P, SC, ROW_INTS], I32)
            rowa = sb0("rowa", [P, SC, D_EDGE])
            flat4 = sb0("flat4", [P, SC, 2], I32)
            place4 = sb0("place4", [P, SC, 2], I32)
            ends = [sem(f"ends_in{s}") for s in range(SC)]
            outs = [sem(f"rows_out{s}") for s in range(SC)]
            staged, staged2 = sem("rows_staged"), sem("rows_free")
            with nc.Block() as block:
                @block.vector
                def _(dve):
                    def stage(i):
                        for s in range(SC):
                            t = SC * i + s
                            wait(dve, outs[s], 48 * i)
                            dve.tensor_copy(row4[:, s, 0:1], key[:, 1, bass.ds(t, 1)])
                            dve.tensor_copy(row4[:, s, 1:2], key[:, 0, bass.ds(t, 1)])
                            dve.tensor_copy(rowa[:, s, :], attrs[:, bass.ds(t, 1), :].rearrange("p o f -> p (o f)"))
                            dve.tensor_copy(flat4[:, s, 0:1], flat[:, 1, bass.ds(t, 1)])
                            dve.tensor_copy(flat4[:, s, 1:2], flat[:, 0, bass.ds(t, 1)])
                            dve.tensor_copy(place4[:, s, 0:1], place[:, 0, bass.ds(t, 1)])
                            dve.tensor_copy(place4[:, s, 1:2], place[:, 1, bass.ds(t, 1)])
                            dve.drain().then_inc(staged, 1)

                    stage(0)
                    with dve.Fori(1, TILES // SC) as i:
                        stage(i)

                @block.gpsimd
                def _(pool):
                    with pool.Fori(0, TILES // SC) as i:
                        for s in range(SC):
                            wait_apart(pool, staged, SC * i + s + 1)
                            for c in range(2):
                                pool.indirect_dma_start(
                                    out=row4[:, s, 2 + c:3 + c], out_offset=None, in_=end_of,
                                    in_offset=bass.IndirectOffsetOnAxis(ap=flat4[:, s, c:c + 1], axis=0)).then_inc(ends[s], 16)
                        for s in range(SC):
                            wait_apart(pool, ends[s], 32 * i + 32)
                            for table, source, c in ((by_dst, row4, 0), (by_src, row4, 1), (by_src_attr, rowa, 1)):
                                pool.indirect_dma_start(
                                    out=table, out_offset=bass.IndirectOffsetOnAxis(ap=place4[:, s, c:c + 1], axis=0),
                                    in_=source[:, s, :], in_offset=None).then_inc(outs[s], 16)
                    for s in range(SC):
                        pool.wait_ge(outs[s], 48 * (TILES // SC))

        def gat(layer):
            nm = f"g{layer}_"
            first_layer = layer == 1
            w = w1 if first_layer else w2
            wal, war = (wa[:, 2 * (layer - 1), :, :], wa[:, 2 * layer - 1, :, :])
            n_in = 2 if first_layer else 3
            with ExitStack() as c:
                def t(name, shape, dt=F32):
                    return c.enter_context(nc.sbuf_tensor(nm + name, shape, dt))

                def ps(name, dt=F32):
                    return c.enter_context(nc.psum_tensor(nm + name, [P, 512], dt))

                def sm(name):
                    return c.enter_context(nc.semaphore(nm + name))

                rows = t("rows", [P, 2, GT, ROW_INTS], I32)
                keys = t("keys", [HEADS, 2, G + 1, ROW_INTS], I32)
                idx = t("idx", [P, 2, GT, ROW_INTS], I32)
                same = t("same", [HEADS, 2, G])
                neg = t("neg", [HEADS, 2, G])
                xin = t("xin", [P, 2, GT, n_in, D])
                st = t("st", [P, 2 * GT, 6])
                mv = t("mv", [P, 2 * GT, 2])
                sd = t("sd", [P, 2 * GT])
                rstd = t("rstd", [P, 2 * GT])
                hT = t("hT", [P, 2, KD, G])
                score = t("score", [HEADS, G])
                top = t("top", [HEADS, 2, G + 1])
                dd = t("dd", [HEADS, 2, G])
                ew = t("ew", [HEADS, 2, G])
                den = t("den", [HEADS, 2, G])
                feat = t("feat", [P, 2, KD, G])
                val = t("val", [P, KD, G])
                acc = t("acc", [P, 2, KD, G])
                rden = t("rden", [P, GT * HEADS])
                r = t("r", [P, GT, D])
                neg_r = t("neg_r", [P, GT, D])
                res = t("res", [P, 2, GT, D])
                hT_ps = [ps(f"hT_ps{q}") for q in range(2)]
                F_ps = ps("F_ps")
                S_ps = ps("S_ps")
                B_ps = [ps(f"B_ps{b}") for b in range(2)]
                O_ps = ps("O_ps")
                DT = S_ps[:, 256:256 + GT * HEADS]

                rows_in = [sm(f"rows_in{s}") for s in range(2)]
                x_in = [sm(f"x_in{s}") for s in range(2)]
                stored = [sm(f"stored{s}") for s in range(2)]
                (idx_made, stats_made, root_made, normed, turned, hT_made, scored, score_read, dd_made, ew_made,
                 spread, scanned, out_turned, out_read, neg_made, exp_made, res_made, f_summed, feat_made) = (sm(n) for n in (
                     "idx_made", "stats_made", "root_made", "normed", "turned", "hT_made", "scored", "score_read",
                     "dd_made", "ew_made", "spread", "scanned", "out_turned", "out_read", "neg_made", "exp_made",
                     "res_made", "f_summed", "feat_made"))
                table = x if first_layer else H1
                target = H1 if first_layer else X1

                with nc.Block() as block:
                    @block.sync
                    def _(sp):
                        def front(g, s, i):
                            wait(sp, idx_made, g - 1)
                            sp.dma_start(rows[:, s, :, :], by_dst[bass.ds(g * G + 1, G), :].rearrange("(j p) w -> p j w", p=P)).then_inc(rows_in[s], 16)
                            sp.dma_start(keys[:, s, :, :].rearrange("h e w -> h (e w)"),
                                         by_dst[bass.ds(g * G, G + 1), :].rearrange("e w -> (e w)").partition_broadcast(HEADS)).then_inc(rows_in[s], 16)

                        def back(g, s, i):
                            wait(sp, res_made, g + 1)
                            sp.dma_start(target[bass.ds(g * G, G), :].rearrange("(j p) d -> p j d", p=P), res[:, s, :, :]).then_inc(stored[s], 16)

                        overlapped(sp, front, back, GROUPS)
                        for s in range(2):
                            sp.wait_ge(stored[s], 16 * (GROUPS // 2))

                    @block.gpsimd
                    def _(pool):
                        def front(g, s, i):
                            wait_apart(pool, idx_made, g + 1)
                            wait_apart(pool, normed if first_layer else res_made, g - 1)
                            for j in range(GT):
                                for q in range(n_in):
                                    col = (0, 1)[q] if first_layer else (2, 3, 1)[q]
                                    pool.indirect_dma_start(
                                        out=xin[:, s, j, q, :], out_offset=None, in_=x if q == 2 else table,
                                        in_offset=bass.IndirectOffsetOnAxis(ap=idx[:, s, j, col:col + 1], axis=0)).then_inc(x_in[s], 16)

                        overlapped(pool, front, nothing, GROUPS)

                    @block.vector
                    def _(dve):
                        def prepare(g, s, i):
                            wait(dve, rows_in[s], 32 * i + 32)
                            dve.tensor_scalar(idx[:, s, :, :], rows[:, s, :, :], float(N_NODES - 1), None, ALU.min)
                            dve.tensor_tensor(same[:, s, :], keys[:, s, 1:G + 1, 1], keys[:, s, 0:G, 1], ALU.is_equal)
                            dve.drain()
                            dve.tensor_scalar(neg[:, s, :], same[:, s, :], -1.0, FAR, ALU.add, ALU.mult).then_inc(idx_made, 1)

                        def front(g, s, i):
                            prepare(g, s, i)
                            if not first_layer:
                                return
                            wait(dve, x_in[s], 16 * GT * n_in * (i + 1))
                            for j in range(GT):
                                for q in range(2):
                                    dve.bn_stats(st[:, 2 * j + q, :], xin[:, s, j, q, :])
                            dve.drain()
                            for a in range(2 * GT):
                                last = dve.bn_aggr(mv[:, a, :], st[:, a, :])
                            last.then_inc(stats_made, 1)
                            wait(dve, root_made, g + 1)
                            dve.reciprocal(rstd[:, :], sd[:, :])
                            dve.drain()
                            for j in range(GT):
                                for q in range(2):
                                    a = 2 * j + q
                                    last = dve.tensor_scalar(xin[:, s, j, q, :], xin[:, s, j, q, :], mv[:, a, 0:1],
                                                             rstd[:, a:a + 1], ALU.subtract, ALU.mult)
                            last.then_inc(normed, 1)

                        def back(g, s, i):
                            wait(dve, scored, g + 1)
                            dve.tensor_scalar(score[:, :], S_ps[0:HEADS, 0:G], NEG_SLOPE, None, ALU.mult)
                            dve.tensor_copy(top[:, s, 0:1], top[:, 1 - s, G:G + 1])
                            dve.drain()
                            dve.tensor_tensor(score[:, :], score[:, :], S_ps[0:HEADS, 0:G], ALU.max).then_inc(score_read, 1)
                            dve.drain()
                            dve.tensor_tensor_scan(top[:, s, 1:G + 1], neg[:, s, :], score[:, :], top[:, s, 0:1], ALU.add, ALU.max)
                            dve.drain()
                            dve.tensor_tensor(dd[:, 0, :], top[:, s, 0:G], top[:, s, 1:G + 1], ALU.subtract)
                            dve.tensor_tensor(dd[:, 1, :], score[:, :], top[:, s, 1:G + 1], ALU.subtract)
                            dve.drain()
                            dve.tensor_tensor(dd[:, 0, :], dd[:, 0, :], neg[:, s, :], ALU.min).then_inc(dd_made, 1)
                            wait(dve, ew_made, g + 1)
                            dve.tensor_tensor_scan(den[:, s, :], ew[:, 0, :], ew[:, 1, :], den[:, 1 - s, G - 1:G], ALU.mult, ALU.add)
                            wait(dve, spread, g + 1)
                            wait(dve, feat_made, g + 1)
                            for b in range(KD):
                                dve.tensor_tensor(val[:, b, :], feat[:, s, b, :], B_ps[b][:, G:2 * G], ALU.mult)
                            dve.drain()
                            for b in range(KD):
                                last = dve.tensor_tensor_scan(acc[:, s, b, :], B_ps[b][:, 0:G], val[:, b, :],
                                                              acc[:, 1 - s, b, G - 1:G], ALU.mult, ALU.add)
                            last.then_inc(scanned, 1)
                            wait(dve, out_turned, g + 1)
                            dve.reciprocal(rden[:, :], DT)
                            dve.drain()
                            dve.tensor_tensor(r[:, :, :].rearrange("p j (h d) -> p (j h) d", h=HEADS),
                                              O_ps[:, :].rearrange("p (a d) -> p a d", d=D_HEAD),
                                              rden[:, :].unsqueeze(2).to_broadcast([P, GT * HEADS, D_HEAD]), ALU.mult).then_inc(out_read, 1)
                            dve.drain()
                            if not first_layer:
                                dve.tensor_tensor(r[:, :, :], r[:, :, :], xin[:, s, :, 1, :], ALU.add)
                                dve.drain()
                            dve.tensor_scalar(neg_r[:, :, :], r[:, :, :], 0.0, None, ALU.min).then_inc(neg_made, 1)
                            wait(dve, exp_made, g + 1)
                            wait(dve, stored[s], 16 * i)
                            ins = dve.scalar_tensor_tensor(res[:, s, :, :], neg_r[:, :, :], -1.0, r[:, :, :], ALU.add, ALU.max)
                            if not first_layer:
                                dve.drain()
                                ins = dve.tensor_tensor(res[:, s, :, :], res[:, s, :, :], xin[:, s, :, 2, :], ALU.add)
                            ins.then_inc(res_made, 1)

                        dve.memset(top[:, :, :], 0.0)
                        dve.memset(den[:, :, :], 0.0)
                        dve.memset(acc[:, :, :, :], 0.0)
                        dve.drain()
                        overlapped(dve, front, back, GROUPS)

                    @block.scalar
                    def _(act):
                        def front(g, s, i):
                            if first_layer:
                                wait(act, stats_made, g + 1)
                                act.activation(sd[:, :], mv[:, :, 1], ACT.Sqrt, bias=eps[:, :]).then_inc(root_made, 1)
                            wait(act, turned, g + 1)
                            for q in range(2):
                                last = act.activation(hT[:, q, :, :].rearrange("p k e -> p (k e)"), hT_ps[q][:, :],
                                                      ACT.Relu if first_layer else ACT.Copy)
                            last.then_inc(hT_made, 1)
                            wait(act, f_summed, g + 1)
                            wait(act, scanned, g - 1)
                            act.activation(feat[:, s, :, :].rearrange("p k e -> p (k e)"), F_ps[:, :], ACT.Copy).then_inc(feat_made, 1)

                        def back(g, s, i):
                            wait(act, dd_made, g + 1)
                            act.activation(ew[:, :, :], dd[:, :, :], ACT.Exp).then_inc(ew_made, 1)
                            wait(act, neg_made, g + 1)
                            act.activation(neg_r[:, :, :], neg_r[:, :, :], ACT.Exp).then_inc(exp_made, 1)

                        overlapped(act, front, back, GROUPS)

                    @block.tensor
                    def _(pe):
                        def front(g, s, i):
                            if first_layer:
                                wait(pe, normed, g + 1)
                            else:
                                wait(pe, x_in[s], 16 * GT * n_in * (i + 1))
                            for q in range(2):
                                for j in range(GT):
                                    for k in range(KD):
                                        mm = pe.transpose(hT_ps[q][:, k * G + j * P:k * G + (j + 1) * P],
                                                          xin[:, s, j, q, k * P:(k + 1) * P], ident[:, :])
                            mm.then_inc(turned, 1)
                            wait(pe, hT_made, g + 1)
                            wait(pe, feat_made, g)
                            for m in range(KD):
                                for k in range(KD):
                                    mm = pe.matmul(F_ps[:, m * G:(m + 1) * G], w[:, k, m * P:(m + 1) * P], hT[:, 0, k, :],
                                                   start=(k == 0), stop=(k == KD - 1))
                            mm.then_inc(f_summed, 1)
                            wait(pe, score_read, g)
                            for q in range(2):
                                for k in range(KD):
                                    mm = pe.matmul(S_ps[0:HEADS, 0:G], (wal, war)[q][:, k, :], hT[:, q, k, :],
                                                   start=(q == 0 and k == 0), stop=(q == 1 and k == KD - 1))
                            mm.then_inc(scored, 1)

                        def back(g, s, i):
                            wait(pe, ew_made, g + 1)
                            for b in range(KD):
                                mm = pe.matmul(B_ps[b][:, :], headsel[:, b, :], ew[:, :, :].rearrange("h q e -> h (q e)"),
                                               start=True, stop=True)
                            mm.then_inc(spread, 1)
                            wait(pe, scanned, g + 1)
                            wait(pe, out_read, g)
                            for j in range(GT):
                                for b in range(KD):
                                    pe.transpose(O_ps[:, j * D + b * P:j * D + (b + 1) * P],
                                                 acc[:, s, b, j * P:(j + 1) * P], ident[:, :])
                                mm = pe.transpose(DT[:, j * HEADS:(j + 1) * HEADS], den[:, s, j * P:(j + 1) * P], ident[0:HEADS, 0:HEADS])
                            mm.then_inc(out_turned, 1)

                        overlapped(pe, front, back, GROUPS)

        gat(1)
        gat(2)

        with ExitStack() as c:
            def t(name, shape, dt=F32):
                return c.enter_context(nc.sbuf_tensor("m_" + name, shape, dt))

            def ps(name):
                return c.enter_context(nc.psum_tensor("m_" + name, [P, 512], F32))

            def sm(name):
                return c.enter_context(nc.semaphore("m_" + name))

            rows = t("rows", [P, 2, GT, ROW_INTS], I32)
            keys = t("keys", [1, 2, G + 1, ROW_INTS], I32)
            att = t("att", [P, 2, GT, D_EDGE])
            attT = t("attT", [D_EDGE, G])
            idx = t("idx", [P, 2, GT, ROW_INTS], I32)
            same = t("same", [1, 2, G])
            xin = t("xin", [P, 2, GT, 2, D])
            st = t("st", [P, 2 * GT, 6])
            mv = t("mv", [P, 2 * GT, 2])
            sd = t("sd", [P, 2 * GT])
            rstd = t("rstd", [P, 2 * GT])
            hT = t("hT", [P, 2, KD, G])
            hid = t("hid", [P, KH, G])
            msg = t("msg", [P, KD, G])
            agg = t("agg", [P, 2, KD, G])
            gs = t("gs", [P, 2, GT, HIDDEN])
            hT_ps = [ps(f"hT_ps{q}") for q in range(2)]
            misc_ps = ps("misc_ps")
            hid_ps = [ps(f"hid_ps{b}") for b in range(2)]
            msg_ps = ps("msg_ps")
            gs_ps = [ps(f"gs_ps{j}") for j in range(GT)]
            rows_in = [sm(f"rows_in{s}") for s in range(2)]
            x_in = [sm(f"x_in{s}") for s in range(2)]
            x1_in = [sm(f"x1_in{s}") for s in range(2)]
            stored = [sm(f"stored{s}") for s in range(2)]
            (idx_made, stats_made, root_made, normed, turned, hT_made, attT_made, hid_summed, hid_made, msg_summed, msg_made,
             spread, scanned, gs_summed, gs_made) = (sm(n) for n in (
                 "idx_made", "stats_made", "root_made", "normed", "turned", "hT_made", "attT_made", "hid_summed", "hid_made",
                 "msg_summed", "msg_made", "spread", "scanned", "gs_summed", "gs_made"))
            with nc.Block() as block:
                @block.sync
                def _(sp):
                    def front(g, s, i):
                        wait(sp, idx_made, g - 1)
                        wait(sp, turned, g - 1)
                        wait(sp, spread, g - 1)
                        sp.dma_start(rows[:, s, :, :], by_src[bass.ds(g * G + 1, G), :].rearrange("(j p) w -> p j w", p=P)).then_inc(rows_in[s], 16)
                        sp.dma_start(keys[:, s, :, :].rearrange("h e w -> h (e w)"),
                                     by_src[bass.ds(g * G, G + 1), :].rearrange("(o e) w -> o (e w)", o=1)).then_inc(rows_in[s], 16)
                        sp.dma_start(att[:, s, :, :], by_src_attr[bass.ds(g * G + 1, G), :].rearrange("(j p) w -> p j w", p=P)).then_inc(rows_in[s], 16)

                    def back(g, s, i):
                        wait(sp, gs_made, g + 1)
                        sp.dma_start(GS[bass.ds(g * G, G), :].rearrange("(j p) d -> p j d", p=P), gs[:, s, :, :]).then_inc(stored[s], 16)

                    overlapped(sp, front, back, GROUPS)
                    for s in range(2):
                        sp.wait_ge(stored[s], 16 * (GROUPS // 2))

                @block.gpsimd
                def _(pool):
                    def front(g, s, i):
                        wait_apart(pool, idx_made, g + 1)
                        wait_apart(pool, turned, g - 1)
                        for j in range(GT):
                            pool.indirect_dma_start(
                                out=xin[:, s, j, 0, :], out_offset=None, in_=x,
                                in_offset=bass.IndirectOffsetOnAxis(ap=idx[:, s, j, 0:1], axis=0)).then_inc(x_in[s], 16)
                            pool.indirect_dma_start(
                                out=xin[:, s, j, 1, :], out_offset=None, in_=X1,
                                in_offset=bass.IndirectOffsetOnAxis(ap=idx[:, s, j, 3:4], axis=0)).then_inc(x_in[s], 16)

                    def back(g, s, i):
                        wait_apart(pool, x_in[s], 32 * GT * (i + 1))
                        for j in range(GT):
                            pool.indirect_dma_start(
                                out=xin[:, s, j, 0, :], out_offset=None, in_=X1,
                                in_offset=bass.IndirectOffsetOnAxis(ap=idx[:, s, j, 2:3], axis=0),
                                bounds_check=NO_ROW - 1, oob_is_err=False).then_inc(x1_in[s], 16)

                    overlapped(pool, front, back, GROUPS)

                @block.vector
                def _(dve):
                    def prepare(g, s, i):
                        wait(dve, rows_in[s], 48 * i + 48)
                        wait(dve, x1_in[s], 16 * GT * i)
                        dve.tensor_scalar(idx[:, s, :, :], rows[:, s, :, :], float(N_NODES - 1), None, ALU.min)
                        dve.tensor_tensor(same[:, s, :], keys[:, s, 1:G + 1, 0], keys[:, s, 0:G, 0], ALU.is_equal).then_inc(idx_made, 1)

                    def norm(g, s, i):
                        wait(dve, x1_in[s], 16 * GT * (i + 1))
                        for j in range(GT):
                            for q in range(2):
                                dve.bn_stats(st[:, 2 * j + q, :], xin[:, s, j, q, :])
                        dve.drain()
                        for a in range(2 * GT):
                            last = dve.bn_aggr(mv[:, a, :], st[:, a, :])
                        last.then_inc(stats_made, 1)
                        wait(dve, root_made, g + 1)
                        dve.reciprocal(rstd[:, :], sd[:, :])
                        dve.drain()
                        for j in range(GT):
                            for q in range(2):
                                a = 2 * j + q
                                last = dve.tensor_scalar(xin[:, s, j, q, :], xin[:, s, j, q, :], mv[:, a, 0:1],
                                                         rstd[:, a:a + 1], ALU.subtract, ALU.mult)
                        last.then_inc(normed, 1)

                    def front(g, s, i):
                        prepare(g, s, i)

                    def back(g, s, i):
                        norm(g, s, i)
                        wait(dve, turned, g + 1)
                        dve.tensor_copy(attT[:, :], misc_ps[0:D_EDGE, 0:G]).then_inc(attT_made, 1)
                        wait(dve, msg_made, g + 1)
                        wait(dve, spread, g + 1)
                        for b in range(KD):
                            last = dve.tensor_tensor_scan(agg[:, s, b, :], misc_ps[:, G:2 * G], msg[:, b, :],
                                                          agg[:, 1 - s, b, G - 1:G], ALU.mult, ALU.add)
                        last.then_inc(scanned, 1)
                        wait(dve, gs_summed, g + 1)
                        wait(dve, stored[s], 16 * i)
                        for j in range(GT):
                            last = dve.tensor_tensor(gs[:, s, j, :], gs_ps[j][:, :], ub1r[:, :], ALU.add)
                        last.then_inc(gs_made, 1)

                    dve.memset(agg[:, :, :, :], 0.0)
                    dve.drain()
                    overlapped(dve, front, back, GROUPS)

                @block.scalar
                def _(act):
                    def back(g, s, i):
                        wait(act, stats_made, g + 1)
                        act.activation(sd[:, :], mv[:, :, 1], ACT.Sqrt, bias=eps[:, :]).then_inc(root_made, 1)
                        wait(act, turned, g + 1)
                        for q in range(2):
                            last = act.activation(hT[:, q, :, :].rearrange("p k e -> p (k e)"), hT_ps[q][:, :], ACT.Relu)
                        last.then_inc(hT_made, 1)
                        wait(act, hid_summed, g + 1)
                        for m in range(KH):
                            last = act.activation(hid[:, m, :], hid_ps[m // 2][:, (m % 2) * G:(m % 2 + 1) * G], ACT.Relu,
                                                  bias=mb1c[:, m:m + 1])
                        last.then_inc(hid_made, 1)
                        wait(act, msg_summed, g + 1)
                        for m in range(KD):
                            last = act.activation(msg[:, m, :], msg_ps[:, m * G:(m + 1) * G], ACT.Identity, bias=mb2c[:, m:m + 1])
                        last.then_inc(msg_made, 1)

                    overlapped(act, nothing, back, GROUPS)

                @block.tensor
                def _(pe):
                    def back(g, s, i):
                        wait(pe, normed, g + 1)
                        wait(pe, scanned, g)
                        for j in range(GT):
                            pe.transpose(misc_ps[0:D_EDGE, j * P:(j + 1) * P], att[:, s, j, :], ident[:, :])
                        for q in range(2):
                            for j in range(GT):
                                for k in range(KD):
                                    mm = pe.transpose(hT_ps[q][:, k * G + j * P:k * G + (j + 1) * P],
                                                      xin[:, s, j, q, k * P:(k + 1) * P], ident[:, :])
                        mm.then_inc(turned, 1)
                        wait(pe, hT_made, g + 1)
                        wait(pe, attT_made, g + 1)
                        pe.matmul(misc_ps[:, G:2 * G], ones[0:1, :], same[:, s, :], start=True, stop=True).then_inc(spread, 1)
                        for m in range(KH):
                            o = hid_ps[m // 2][:, (m % 2) * G:(m % 2 + 1) * G]
                            for q in range(2):
                                for k in range(KD):
                                    pe.matmul(o, mw1[:, q * KD + k, m * P:(m + 1) * P], hT[:, q, k, :],
                                              start=(q == 0 and k == 0), stop=False)
                            mm = pe.matmul(o, mw1e[:, m * P:(m + 1) * P], attT[:, :], start=False, stop=True)
                        mm.then_inc(hid_summed, 1)
                        wait(pe, hid_made, g + 1)
                        for m in range(KD):
                            for k in range(KH):
                                mm = pe.matmul(msg_ps[:, m * G:(m + 1) * G], mw2[:, k, m * P:(m + 1) * P], hid[:, k, :],
                                               start=(k == 0), stop=(k == KH - 1))
                        mm.then_inc(msg_summed, 1)
                        wait(pe, scanned, g + 1)
                        wait(pe, gs_made, g)
                        for j in range(GT):
                            for k in range(KD):
                                mm = pe.matmul(gs_ps[j][:, :], agg[:, s, k, j * P:(j + 1) * P], uw1[:, KD + k, :],
                                               start=(k == 0), stop=(k == KD - 1))
                        mm.then_inc(gs_summed, 1)

                    overlapped(pe, nothing, back, GROUPS)

        NT = 2
        STEPS = (NODE_TILES + NT - 1) // NT
        with ExitStack() as c:
            def t(name, shape, dt=F32):
                return c.enter_context(nc.sbuf_tensor("u_" + name, shape, dt))

            def ps(name):
                return c.enter_context(nc.psum_tensor("u_" + name, [P, 512], F32))

            def sm(name):
                return c.enter_context(nc.semaphore("u_" + name))

            idx = t("idx", [P, 2, 2, NT], I32)
            xt = t("xt", [P, 2, NT, D])
            gb = t("gb", [P, 2, NT, HIDDEN])
            xn = t("xn", [P, NT, D])
            st = t("st", [P, NT, 6])
            mv = t("mv", [P, NT, 2])
            sd = t("sd", [P, NT])
            rstd = t("rstd", [P, NT])
            res = t("res", [P, 2, NT, D])
            hT = t("hT", [P, KD, NT * P])
            ua = t("ua", [P, 2, NT, HIDDEN])
            uT = t("uT", [P, NT, KH, P])
            ot = t("ot", [P, 2, NT, D])
            hT_ps = ps("hT_ps")
            U_ps = [[ps(f"U_ps{s}{j}") for j in range(NT)] for s in range(2)]
            uT_ps = [ps(f"uT_ps{j}") for j in range(NT)]
            O_ps = ps("O_ps")
            x_in, x1_in, gs_in, stored = ([sm(f"{n}{s}") for s in range(2)] for n in ("x_in", "x1_in", "gs_in", "stored"))
            (idx_made, filled, stats_made, root_made, normed, res_made, turned, hT_made, u_summed, u_made, u_turned, uT_made,
             o_summed, o_made) = (sm(n) for n in (
                 "idx_made", "filled", "stats_made", "root_made", "normed", "res_made", "turned", "hT_made", "u_summed",
                 "u_made", "u_turned", "uT_made", "o_summed", "o_made"))
            last_step = STEPS - 1
            n_last = NODE_TILES - last_step * NT
            assert n_last == 1

            def tiles(g):
                return n_last if isinstance(g, int) and g == last_step else NT

            with nc.Block() as block:
                @block.sync
                def _(sp):
                    def front(g, s, i):
                        wait(sp, res_made, g - 1)
                        if tiles(g) == NT:
                            sp.dma_start(xt[:, s, :, :], x[bass.ds(g * (NT * P), NT * P), :].rearrange("(j p) d -> p j d", p=P)).then_inc(x_in[s], 16)
                        else:
                            sp.dma_start(xt[0:LAST_ROWS, s, 0, :], x[g * NT * P:N_NODES, :]).then_inc(x_in[s], 16)

                    def back(g, s, i):
                        wait(sp, o_made, g + 1)
                        if tiles(g) == NT:
                            sp.dma_start(out[bass.ds(g * (NT * P), NT * P), :].rearrange("(j p) d -> p j d", p=P), ot[:, s, :, :]).then_inc(stored[s], 16)
                        else:
                            sp.dma_start(out[g * NT * P:N_NODES, :], ot[0:LAST_ROWS, s, 0, :]).then_inc(stored[s], 16)

                    overlapped(sp, front, back, STEPS)
                    for s in range(2):
                        sp.wait_ge(stored[s], 16 * (STEPS // 2))

                @block.gpsimd
                def _(pool):
                    def front(g, s, i):
                        wait_apart(pool, idx_made, g + 1)
                        wait_apart(pool, x_in[s], 16 * i + 16)
                        for j in range(tiles(g)):
                            pool.indirect_dma_start(
                                out=xt[:, s, j, :], out_offset=None, in_=X1,
                                in_offset=bass.IndirectOffsetOnAxis(ap=idx[:, s, 0, j:j + 1], axis=0),
                                bounds_check=NO_ROW - 1, oob_is_err=False).then_inc(x1_in[s], 16)
                        wait_apart(pool, filled, g + 1)
                        for j in range(tiles(g)):
                            pool.indirect_dma_start(
                                out=gb[:, s, j, :], out_offset=None, in_=GS,
                                in_offset=bass.IndirectOffsetOnAxis(ap=idx[:, s, 1, j:j + 1], axis=0),
                                bounds_check=NO_ROW - 1, oob_is_err=False).then_inc(gs_in[s], 16)

                    overlapped(pool, front, nothing, STEPS)

                def arrived(eng, signals, g, s, i):
                    wait(eng, signals[s], 16 * NT * i + 16 * tiles(g))

                @block.vector
                def _(dve):
                    def indices(g, s, i):
                        n = tiles(g)
                        dve.tensor_copy(idx[:, s, 0, 0:n], end_d[:, bass.ds(g * NT, n)])
                        dve.tensor_copy(idx[:, s, 1, 0:n], end_s[:, bass.ds(g * NT, n)]).then_inc(idx_made, 1)

                    def front(g, s, i):
                        n = tiles(g)
                        indices(g, s, i)
                        arrived(dve, x1_in, g, s, i)
                        for j in range(n):
                            dve.bn_stats(st[:, j, :], xt[:, s, j, :])
                        dve.drain()
                        for j in range(n):
                            last = dve.bn_aggr(mv[:, j, :], st[:, j, :])
                        last.then_inc(stats_made, 1)
                        wait(dve, root_made, g + 1)
                        dve.reciprocal(rstd[:, 0:n], sd[:, 0:n])
                        dve.drain()
                        for j in range(n):
                            last = dve.tensor_scalar(xn[:, j, :], xt[:, s, j, :], mv[:, j, 0:1], rstd[:, j:j + 1], ALU.subtract, ALU.mult)
                        last.then_inc(normed, 1)
                        dve.drain()
                        dve.scalar_tensor_tensor(res[:, s, 0:n, :], xn[:, 0:n, :], 0.0, xt[:, s, 0:n, :], ALU.max, ALU.add).then_inc(res_made, 1)
                        dve.drain()
                        for j in range(n):
                            dve.tensor_tensor(res[:, s, j, :], res[:, s, j, :], ub2r[:, :], ALU.add)
                        wait(dve, u_summed, g + 1)
                        arrived(dve, gs_in, g, s, i)
                        for j in range(n):
                            last = dve.tensor_tensor(ua[:, s, j, :], U_ps[s][j][:, :], gb[:, s, j, :], ALU.add)
                        last.then_inc(u_made, 1)

                    def back(g, s, i):
                        n = tiles(g)
                        wait(dve, o_summed, g + 1)
                        wait(dve, stored[s], 16 * i)
                        dve.tensor_tensor(ot[:, s, 0:n, :], O_ps[:, 0:n * D].rearrange("p (j d) -> p j d", d=D), res[:, s, 0:n, :],
                                          ALU.add).then_inc(o_made, 1)

                    overlapped(dve, front, back, STEPS)

                @block.scalar
                def _(act):
                    def front(g, s, i):
                        n = tiles(g)
                        wait(act, u_made, g - 1)
                        for j in range(n):
                            last = act.activation(gb[:, s, j, :], ub1r[:, :], ACT.Copy)
                        last.then_inc(filled, 1)
                        wait(act, stats_made, g + 1)
                        act.activation(sd[:, 0:n], mv[:, 0:n, 1], ACT.Sqrt, bias=eps[:, :]).then_inc(root_made, 1)
                        wait(act, turned, g + 1)
                        act.activation(hT[:, :, 0:n * P], hT_ps[:, :].rearrange("p (k e) -> p k e", k=KD)[:, :, 0:n * P],
                                       ACT.Relu).then_inc(hT_made, 1)

                    def back(g, s, i):
                        wait(act, u_turned, g + 1)
                        for j in range(tiles(g)):
                            last = act.activation(uT[:, j, :, :].rearrange("p k e -> p (k e)"), uT_ps[j][:, :], ACT.Relu)
                        last.then_inc(uT_made, 1)

                    overlapped(act, front, back, STEPS)

                @block.tensor
                def _(pe):
                    def front(g, s, i):
                        wait(pe, normed, g + 1)
                        for j in range(tiles(g)):
                            for k in range(KD):
                                mm = pe.transpose(hT_ps[:, k * NT * P + j * P:k * NT * P + (j + 1) * P], xn[:, j, k * P:(k + 1) * P],
                                                  ident[:, :])
                        mm.then_inc(turned, 1)
                        wait(pe, hT_made, g + 1)
                        for j in range(tiles(g)):
                            for k in range(KD):
                                mm = pe.matmul(U_ps[s][j][:, :], hT[:, k, j * P:(j + 1) * P], uw1[:, k, :],
                                               start=(k == 0), stop=(k == KD - 1))
                        mm.then_inc(u_summed, 1)

                    def back(g, s, i):
                        wait(pe, u_made, g + 1)
                        for j in range(tiles(g)):
                            for m in range(KH):
                                mm = pe.transpose(uT_ps[j][:, m * P:(m + 1) * P], ua[:, s, j, m * P:(m + 1) * P], ident[:, :])
                        mm.then_inc(u_turned, 1)
                        wait(pe, uT_made, g + 1)
                        wait(pe, o_made, g)
                        for j in range(tiles(g)):
                            for m in range(KH):
                                mm = pe.matmul(O_ps[:, j * D:(j + 1) * D], uT[:, j, m, :], uw2[:, m, :],
                                               start=(m == 0), stop=(m == KH - 1))
                        mm.then_inc(o_summed, 1)

                    overlapped(pe, front, back, STEPS)


_INS = ["x", "src", "dst", "edge_attr_16", "L0_gnn_W1", "L0_gnn_al1", "L0_gnn_ar1", "L0_gnn_W2", "L0_gnn_al2",
        "L0_gnn_ar2", "L1_gnn_mW1", "L1_gnn_mb1", "L1_gnn_mW2", "L1_gnn_mb2", "L1_gnn_uW1", "L1_gnn_ub1",
        "L1_gnn_uW2", "L1_gnn_ub2"]


def kernel(**inputs):
    import numpy as _np
    import concourse.bacc as _bacc
    from concourse import mybir as _mybir
    from concourse.bass_utils import run_bass_kernel_spmd as _run

    nc = _bacc.Bacc("TRN2", target_bir_lowering=False, num_devices=1)
    arrays, args = {}, []
    for name in _INS:
        a = _np.ascontiguousarray(inputs[name])
        arrays[f"in_{name}"] = a
        args.append(nc.dram_tensor(f"in_{name}", a.shape, _mybir.dt.from_np(a.dtype), kind="ExternalInput").ap())
    out = nc.dram_tensor("out_dram", (N_NODES, D), _mybir.dt.float32, kind="ExternalOutput").ap()
    build(nc, *args, out)
    r = _run(nc, [arrays], core_ids=[0])
    return r.results[0]["out_dram"]
```

```python
from contextlib import ExitStack

import numpy as np
import concourse.bass as bass
from concourse import mybir

F32 = mybir.dt.float32
F16 = mybir.dt.float16
I32 = mybir.dt.int32
ALU = mybir.AluOpType
ACT = mybir.ActivationFunctionType
AX = mybir.AxisListType

P = 128
N_NODES, D = 50000, 256
N_EDGES, D_EDGE = 12500, 16
HEADS = 4
D_HEAD = D // HEADS
HIDDEN = 512
KD = D // P
KH = HIDDEN // P
TILES = 100
EDGES = P * TILES
PARTS_USED = N_EDGES // TILES
assert PARTS_USED * TILES == N_EDGES and PARTS_USED < P
NODE_TILES = -(-N_NODES // P)
LAST_ROWS = N_NODES - (NODE_TILES - 1) * P
PAD_KEY = NODE_TILES * P - 1
assert PAD_KEY >= N_NODES
NO_ROW = EDGES
G = 256
GT = G // P
GROUPS = EDGES // G
ROW = 2 + D_EDGE
UN = 4
EPS = 1e-5
NEG_SLOPE = 0.2
FAR = 1e30


def build(nc, x, src, dst, attr, W1, al1, ar1, W2, al2, ar2, mW1, mb1, mW2, mb2, uW1, ub1, uW2, ub2, out):
    ctx = ExitStack()

    def dram(name, shape, dt):
        return nc.dram_tensor(name, shape, dt, kind="Internal").ap()

    by_dst = dram("by_dst", [EDGES + 1, 2], I32)
    by_src = dram("by_src", [EDGES + 1, ROW], I32)
    end_of = dram("end_of", [P * NODE_TILES, 1], I32)
    H1 = dram("H1", [EDGES + 1, D], F32)
    X1 = dram("X1", [EDGES + 1, D], F32)
    GS = dram("GS", [EDGES, HIDDEN], F32)

    with ctx:
        def sb(name, shape, dt=F32):
            return ctx.enter_context(nc.sbuf_tensor(name, shape, dt))

        def sem(name):
            return ctx.enter_context(nc.semaphore(name))

        ident = sb("ident", [P, P])
        ident16 = sb("ident16", [P, P], F16)
        tri = sb("tri", [P, P])
        trilow = sb("trilow", [P, P])
        ones = sb("ones", [P, P])
        iota_t = sb("iota_t", [P, NODE_TILES], F16)
        eps = sb("eps", [P, 1])
        headsel = sb("headsel", [HEADS, KD, P])
        w1 = sb("w1", [P, KD, D])
        w2 = sb("w2", [P, KD, D])
        wa = sb("wa", [P, 4, KD, HEADS])
        mw1 = sb("mw1", [P, 2 * KD, HIDDEN])
        mw1e = sb("mw1e", [D_EDGE, HIDDEN])
        mw2 = sb("mw2", [P, KH, D])
        uw1 = sb("uw1", [P, 2 * KD, HIDDEN])
        uw2 = sb("uw2", [P, KH, D])
        mb1c = sb("mb1c", [P, KH])
        mb2c = sb("mb2c", [P, KD])
        ub1r = sb("ub1r", [P, HIDDEN])
        ub2r = sb("ub2r", [P, D])
        end_d = sb("end_d", [P, NODE_TILES], I32)
        end_s = sb("end_s", [P, NODE_TILES], I32)
        ends = sb("ends", [P, TILES, 3], I32)

        def reached(v, n):
            return not isinstance(v, int) or v >= n

        def pipelined(eng, stages, n):
            lags = [lag for _, lag in stages]

            def step(i, c):
                for stage, lag in stages:
                    g = UN * i + c - lag
                    if not isinstance(g, int) or 0 <= g < n:
                        stage(g, (c - lag) % UN, i + (c - lag) // UN)

            first = -(-(max(lags) + UN) // UN)
            for T in range(first * UN):
                step(T // UN, T % UN)
            with eng.Fori(first, (n - 1) // UN) as i:
                for c in range(UN):
                    step(i, c)
            for T in range((n - 1) // UN * UN, n + max(lags)):
                step(T // UN, T % UN)

        apart = sem("apart")
        phase_sems = []

        def phase_sem(name):
            phase_sems.append(nc.alloc_semaphore(name))
            return phase_sems[-1]

        def end_phase():
            nc.clear_and_free_semaphores(list(phase_sems))
            nc.all_engine_barrier()
            phase_sems.clear()


        with ExitStack() as c0:
            def sb0(name, shape, dt=F32):
                return c0.enter_context(nc.sbuf_tensor(name, shape, dt))

            av = sb0("av", [P, 4, D])
            prod = sb0("prod", [P, 4, KD, D])
            key = sb0("key", [P, 2, TILES], I32)
            hi_i = sb0("hi_i", [P, 2, TILES], I32)
            lo_i = sb0("lo_i", [P, 2, TILES], I32)
            keyf = sb0("keyf", [P, 2, TILES])
            hi = sb0("hi", [P, 2, TILES])
            lo = sb0("lo", [P, 2, TILES])
            pay = sb0("pay", [P, TILES, ROW], I32)
            zrow = sb0("zrow", [1, D])
            sentinel = sb0("sentinel", [1, ROW], I32)
            ohH = sb0("ohH", [P, 2, 2, NODE_TILES], F16)
            ohL = sb0("ohL", [P, 2, 2, P], F16)
            cnt = sb0("cnt", [P, 2, NODE_TILES])
            tot = sb0("tot", [P, 2, NODE_TILES])
            cum = sb0("cum", [P, 2, NODE_TILES])
            first = sb0("first", [P, 2, NODE_TILES])
            has = sb0("has", [P, 2, NODE_TILES])
            onesr = sb0("onesr", [P, NODE_TILES])

            w_in, k_in, a_in, cst, prodd, wad = (sem(n) for n in ("weights_in", "keys_in", "attr_in", "consts_made", "prod_made", "wa_made"))
            keyset, keysplit, z_out, z_set = (sem(n) for n in ("keys_preset", "keys_split", "zeros_out", "zeros_set"))
            with nc.Block() as block:
                @block.sync
                def _(sp):
                    sp.wait_ge(keyset, 1)
                    sp.dma_start(key[0:PARTS_USED, 0, :], dst.rearrange("(p t) -> p t", t=TILES)).then_inc(k_in, 16)
                    sp.dma_start(key[0:PARTS_USED, 1, :], src.rearrange("(p t) -> p t", t=TILES)).then_inc(k_in, 16)
                    sp.dma_start(pay[0:PARTS_USED, :, 2:ROW], attr.bitcast(I32).rearrange("(p t) f -> p t f", t=TILES)).then_inc(a_in, 16)
                    sp.dma_start(w1[:, :, :], W1.rearrange("(k p) n -> p k n", p=P)).then_inc(w_in, 16)
                    sp.dma_start(w2[:, :, :], W2.rearrange("(k p) n -> p k n", p=P)).then_inc(w_in, 16)
                    for i, a in enumerate((al1, ar1, al2, ar2)):
                        sp.dma_start(av[:, i, :], a.rearrange("h d -> (h d)").partition_broadcast(P)).then_inc(w_in, 16)
                    sp.dma_start(mw1[:, :, :], mW1[0:2 * D, :].rearrange("(k p) n -> p k n", p=P)).then_inc(w_in, 16)
                    sp.dma_start(mw1e[:, :], mW1[2 * D:2 * D + D_EDGE, :]).then_inc(w_in, 16)
                    sp.dma_start(mw2[:, :, :], mW2.rearrange("(k p) n -> p k n", p=P)).then_inc(w_in, 16)
                    sp.dma_start(uw1[:, :, :], uW1.rearrange("(k p) n -> p k n", p=P)).then_inc(w_in, 16)
                    sp.dma_start(uw2[:, :, :], uW2.rearrange("(k p) n -> p k n", p=P)).then_inc(w_in, 16)
                    with nc.allow_non_contiguous_dma(reason="bias columns, once"):
                        sp.dma_start(mb1c[:, :], mb1.rearrange("(k p) -> p k", p=P)).then_inc(w_in, 16)
                        sp.dma_start(mb2c[:, :], mb2.rearrange("(k p) -> p k", p=P)).then_inc(w_in, 16)
                    sp.dma_start(ub1r[:, :], ub1.partition_broadcast(P)).then_inc(w_in, 16)
                    sp.dma_start(ub2r[:, :], ub2.partition_broadcast(P)).then_inc(w_in, 16)
                    sp.wait_ge(z_set, 2)
                    sp.dma_start(H1[NO_ROW:NO_ROW + 1, :], zrow[:, :]).then_inc(z_out, 16)
                    sp.dma_start(X1[NO_ROW:NO_ROW + 1, :], zrow[:, :]).then_inc(z_out, 16)
                    sp.dma_start(by_dst[0:1, :], sentinel[:, 0:2]).then_inc(z_out, 16)
                    sp.dma_start(by_src[0:1, :], sentinel[:, :]).then_inc(z_out, 16)
                    sp.wait_ge(z_out, 64)
                    sp.wait_ge(w_in, 16 * 15)
                    sp.wait_ge(a_in, 16)

                @block.gpsimd
                def _(pool):
                    pool.memset(ident[:, :], 0.0)
                    pool.memset(tri[:, :], 1.0)
                    pool.memset(trilow[:, :], 1.0)
                    pool.memset(headsel[:, :, :], 1.0)
                    pool.iota(iota_t[:, :], pattern=[[1, NODE_TILES]], base=0, channel_multiplier=0,
                              allow_small_or_imprecise_dtypes=True)
                    pool.drain()
                    pool.affine_select(out=ident[:, :], in_=ident[:, :], compare_op=ALU.not_equal, fill=1.0,
                                       base=0, pattern=[[-1, P]], channel_multiplier=1)
                    pool.affine_select(out=tri[:, :], in_=tri[:, :], compare_op=ALU.is_ge, fill=0.0,
                                       base=-1, pattern=[[1, P]], channel_multiplier=-1)
                    pool.affine_select(out=trilow[:, :], in_=trilow[:, :], compare_op=ALU.is_ge, fill=0.0,
                                       base=-1, pattern=[[-1, P]], channel_multiplier=1)
                    pool.affine_select(out=headsel[:, :, :], in_=headsel[:, :, :], compare_op=ALU.is_ge, fill=0.0,
                                       base=0, pattern=[[P, KD], [1, P]], channel_multiplier=-D_HEAD)
                    pool.drain()
                    pool.affine_select(out=headsel[:, :, :], in_=headsel[:, :, :], compare_op=ALU.is_ge, fill=0.0,
                                       base=D_HEAD - 1, pattern=[[-P, KD], [-1, P]], channel_multiplier=D_HEAD)
                    pool.tensor_copy(ident16[:, :], ident[:, :])

                @block.vector
                def _(dve):
                    dve.memset(pay[:, :, :], 0)
                    dve.memset(key[:, :, :], PAD_KEY)
                    dve.drain().then_inc(keyset, 1)
                    dve.memset(zrow[:, :], 0.0).then_inc(z_set, 1)
                    dve.memset(sentinel[:, :], -1).then_inc(z_set, 1)
                    dve.memset(ones[:, :], 1.0)
                    dve.memset(onesr[:, :], 1.0)
                    dve.memset(eps[:, :], EPS)
                    dve.wait_ge(k_in, 32)
                    dve.tensor_scalar(hi_i[:, :, :], key[:, :, :], 7, None, ALU.arith_shift_right)
                    dve.tensor_scalar(lo_i[:, :, :], key[:, :, :], P - 1, None, ALU.bitwise_and)
                    dve.tensor_copy(keyf[:, :, :], key[:, :, :])
                    dve.drain()
                    dve.tensor_copy(hi[:, :, :], hi_i[:, :, :])
                    dve.tensor_copy(lo[:, :, :], lo_i[:, :, :])
                    dve.tensor_copy(pay[:, :, 0], key[:, 1, :])
                    dve.tensor_copy(pay[:, :, 1], key[:, 0, :])
                    dve.wait_ge(w_in, 16 * 15)
                    for i in range(4):
                        w = (w1, w1, w2, w2)[i]
                        for k in range(KD):
                            dve.tensor_tensor(prod[:, i, k, :], w[:, k, :], av[:, i, :], ALU.mult)
                    dve.drain()
                    dve.tensor_reduce(wa[:, :, :, :].rearrange("p i k h -> p (i k h)"),
                                      prod[:, :, :, :].rearrange("p i k (h d) -> p (i k h) d", h=HEADS), AX.X, ALU.add)

            cnt_ps = [c0.enter_context(nc.psum_tensor(f"cnt_ps{k}", [P, 512], F32)) for k in range(2)]
            onehot, counted, slot_free, table_up = (sem(n) for n in ("onehot_made", "tile_counted", "onehot_free", "tables_stored"))
            cum_ps, cnt_done, seeded = (sem(n) for n in ("sums_made", "cnt_copied", "starts_seeded"))
            first_done = sem("first_made")
            tot_ps = [c0.enter_context(nc.psum_tensor(f"tot_ps{k}", [P, 512], F32)) for k in range(2)]
            pre_ps = [c0.enter_context(nc.psum_tensor(f"pre_ps{k}", [P, 512], F32)) for k in range(2)]

            def make_onehots(dve, t, slot):
                for k in range(2):
                    dve.tensor_scalar(ohH[:, slot, k, :], iota_t[:, :], hi[:, k, bass.ds(t, 1)], None, ALU.is_equal)
                    last = dve.tensor_scalar(ohL[:, slot, k, :], iota_t[:, 0:P], lo[:, k, bass.ds(t, 1)], None, ALU.is_equal)
                return last

            with nc.Block() as block:
                @block.vector
                def _(dve):
                    with dve.Fori(0, TILES // 2) as i:
                        for slot in range(2):
                            dve.wait_ge(slot_free, 2 * i + slot + 1)
                            make_onehots(dve, 2 * i + slot, slot).then_inc(onehot, 1)
                    dve.wait_ge(counted, 1)
                    for k in range(2):
                        dve.tensor_copy(cnt[:, k, :], cnt_ps[k][:, 0:NODE_TILES])
                    dve.drain().then_inc(cnt_done, 1)
                    dve.wait_ge(cum_ps, 1)
                    for k in range(2):
                        dve.tensor_copy(tot[:, k, :], tot_ps[k][:, 0:NODE_TILES])
                    dve.drain()
                    for k in range(2):
                        dve.tensor_tensor_scan(cum[:, k, :], onesr[:, :], tot[:, k, :], 0.0, ALU.mult, ALU.add)
                    dve.drain()
                    dve.tensor_tensor(cum[:, :, :], cum[:, :, :], tot[:, :, :], ALU.subtract)
                    dve.tensor_scalar(has[:, :, :], cnt[:, :, :], 0.5, None, ALU.is_gt)
                    dve.drain()
                    for k in range(2):
                        dve.tensor_tensor(first[:, k, :], cum[:, k, :], pre_ps[k][:, 0:NODE_TILES], ALU.add)
                    dve.drain().then_inc(first_done, 1)
                    dve.scalar_tensor_tensor(tot[:, :, :], first[:, :, :], float(-1 - NO_ROW), cnt[:, :, :], ALU.add, ALU.add)
                    dve.drain()
                    dve.tensor_tensor(tot[:, :, :], tot[:, :, :], has[:, :, :], ALU.mult)
                    dve.drain()
                    dve.tensor_scalar(end_d[:, :], tot[:, 0, :], float(NO_ROW), None, ALU.add)
                    dve.tensor_scalar(end_s[:, :], tot[:, 1, :], float(NO_ROW), None, ALU.add)
                    dve.drain().then_inc(table_up, 1)

                @block.tensor
                def _(pe):
                    pe.sem_inc(slot_free, 2)
                    pe.wait_ge(onehot, 1)
                    for k in range(2):
                        pe.matmul(cnt_ps[k][:, 0:NODE_TILES], ohL[:, 0, k, :], ohH[:, 0, k, :], start=True, stop=False,
                                  skip_group_check=True)
                    pe.drain().then_inc(slot_free, 1)
                    pe.wait_ge(onehot, 2)
                    for k in range(2):
                        pe.matmul(cnt_ps[k][:, 0:NODE_TILES], ohL[:, 1, k, :], ohH[:, 1, k, :], start=False, stop=False,
                                  skip_group_check=True)
                    pe.drain().then_inc(slot_free, 1)
                    with pe.Fori(1, TILES // 2) as i:
                        for slot in range(2):
                            pe.wait_ge(onehot, 2 * i + slot + 1)
                            for k in range(2):
                                mm = pe.matmul(cnt_ps[k][:, 0:NODE_TILES], ohL[:, slot, k, :], ohH[:, slot, k, :],
                                               start=False, stop=False, skip_group_check=True)
                            mm.then_inc(slot_free, 1)
                    pe.drain().then_inc(counted, 1)
                    pe.wait_ge(cnt_done, 1)
                    for k in range(2):
                        pe.matmul(pre_ps[k][:, 0:NODE_TILES], tri[:, :], cnt[:, k, :], start=True, stop=True)
                        mm = pe.matmul(tot_ps[k][:, 0:NODE_TILES], ones[:, :], cnt[:, k, :], start=True, stop=True)
                    mm.then_inc(cum_ps, 1)
                    pe.wait_ge(first_done, 1)
                    for k in range(2):
                        pe.matmul(cnt_ps[k][:, 0:NODE_TILES], ident[:, :], first[:, k, :], start=True, stop=False,
                                  skip_group_check=True)

                @block.sync
                def _(sp):
                    sp.wait_ge(table_up, 1)
                    sp.dma_start(end_of.rearrange("(p n) o -> p (n o)", p=P), end_d[:, :]).then_inc(table_up, 16)
                    sp.wait_ge(table_up, 17)

            snap = sb0("snap", [P, 2, 2, NODE_TILES])
            diag = sb0("diag", [P, 2, 2, P])
            lT = sb0("lT", [P, 2, 2, P])
            bw = sb0("bw", [P, 2, 2])
            place = sb0("place", [P, UN, 2], I32)
            row = sb0("row", [P, UN, ROW], I32)
            junk = sb0("junk", [P, 2, NODE_TILES])
            junk2 = sb0("junk2", [P, 2, P])
            pick_ps = tot_ps
            keyrow_ps = [p[:, 0:2 * P].rearrange("p (k n) -> p k n", k=2) for p in pre_ps]
            lT_ps = [c0.enter_context(nc.psum_tensor(f"lT_ps{s}", [P, 1024], F16))[:, 0:2 * P] for s in range(2)]
            onehot2, diag_made, lT_made, lT_copied, advanced, picked, tile_read, placed = (sem(n) for n in (
                "p2_onehot_made", "p2_diag_made", "p2_lT_made", "p2_lT_copied", "p2_advanced", "p2_picked", "p2_tile_read",
                "p2_placed"))
            row_out = [sem(f"p2_row_out{s}") for s in range(UN)]
            with nc.Block() as block:
                @block.vector
                def _(dve):
                    def onehots(t, s, i):
                        make_onehots(dve, t, s % 2).then_inc(onehot2, 1)

                    def places(t, s, i):
                        dve.wait_ge(picked, t + 1)
                        for k in range(2):
                            dve.scalar_tensor_tensor(junk[:, k, :], pick_ps[k][:, 0:NODE_TILES], 1.0,
                                                     ohH[:, s % 2, k, :], ALU.mult, ALU.mult, accum_out=bw[:, 0, k:k + 1])
                            dve.scalar_tensor_tensor(junk2[:, k, :], keyrow_ps[s % 2][:, k, :], keyf[:, k, bass.ds(t, 1)],
                                                     trilow[:, :], ALU.is_equal, ALU.mult, accum_out=bw[:, 1, k:k + 1])
                        dve.drain().then_inc(tile_read, 1)
                        if reached(i, 1):
                            dve.wait_ge(row_out[s], 32 * i)
                        dve.scalar_tensor_tensor(place[:, s, :], bw[:, 0, :], 1.0, bw[:, 1, :], ALU.add, ALU.add)
                        dve.tensor_copy(row[:, s, :], pay[:, bass.ds(t, 1), :].rearrange("p o w -> p (o w)"))
                        dve.drain().then_inc(placed, 1)

                    pipelined(dve, [(onehots, 0), (places, 1)], TILES)

                @block.gpsimd
                def _(pool):
                    def write_rows(t, s, i):
                        pool.wait_ge(placed, t + 1)
                        pool.sem_inc(apart, 1)
                        for table, words, k in ((by_dst, 2, 0), (by_src, ROW, 1)):
                            pool.indirect_dma_start(
                                out=table, out_offset=bass.IndirectOffsetOnAxis(ap=place[:, s, k:k + 1], axis=0),
                                in_=row[:, s, 0:words], in_offset=None).then_inc(row_out[s], 16)

                    pipelined(pool, [(write_rows, 0)], TILES)
                    for s in range(UN):
                        pool.wait_ge(row_out[s], 32 * (TILES // UN))

                @block.tensor
                def _(pe):
                    def tile(t, s, i):
                        s = s % 2
                        pe.wait_ge(onehot2, t + 1)
                        for k in range(2):
                            mm = pe.transpose(lT_ps[s][:, k * P:(k + 1) * P], ohL[:, s, k, :], ident16[:, :])
                        mm.then_inc(lT_made, 1)
                        pe.wait_ge(diag_made, t + 1)
                        if reached(t, 2):
                            pe.wait_ge(tile_read, t - 1)
                        for k in range(2):
                            pe.matmul(keyrow_ps[s][:, k, :], ones[:, :], diag[:, s, k, :], start=True, stop=True)
                        pe.wait_ge(lT_copied, t + 1)
                        for k in range(2):
                            mm = pe.matmul(cnt_ps[k][:, 0:NODE_TILES], ohL[:, s, k, :], ohH[:, s, k, :],
                                           start=False, stop=False, skip_group_check=True)
                        mm.then_inc(advanced, 1)
                        if reached(t, 1):
                            pe.wait_ge(tile_read, t)
                        for k in range(2):
                            mm = pe.matmul(pick_ps[k][:, 0:NODE_TILES], lT[:, s, k, :], snap[:, s, k, :],
                                           start=True, stop=True)
                        mm.then_inc(picked, 1)

                    pipelined(pe, [(tile, 0)], TILES)

                @block.scalar
                def _(act):
                    def tile(t, s, i):
                        s = s % 2
                        if reached(t, 2):
                            act.wait_ge(tile_read, t - 1)
                        for k in range(2):
                            last = act.activation(diag[:, s, k, :], ident[:, :], ACT.Copy, scale=keyf[:, k, bass.ds(t, 1)])
                        last.then_inc(diag_made, 1)
                        if reached(t, 1):
                            act.wait_ge(advanced, t)
                        for k in range(2):
                            act.activation(snap[:, s, k, :], cnt_ps[k][:, 0:NODE_TILES], ACT.Copy)
                        act.wait_ge(lT_made, t + 1)
                        act.activation(lT[:, s, :, :].rearrange("p k n -> p (k n)"), lT_ps[s], ACT.Copy).then_inc(lT_copied, 1)

                    pipelined(act, [(tile, 0)], TILES)

        def gat(layer):
            nm = f"g{layer}_"
            first_layer = layer == 1
            w = w1 if first_layer else w2
            wal, war = (wa[:, 2 * (layer - 1), :, :], wa[:, 2 * layer - 1, :, :])
            n_in = 2 if first_layer else 3
            with ExitStack() as c:
                def t(name, shape, dt=F32):
                    return c.enter_context(nc.sbuf_tensor(nm + name, shape, dt))

                def ps(name, dt=F32):
                    return c.enter_context(nc.psum_tensor(nm + name, [P, 512], dt))

                def sm(name):
                    return phase_sem(nm + name)

                rows = t("rows", [P, UN, GT, 2], I32)
                keys = t("keys", [HEADS, UN, G + 1, 2], I32)
                parts = t("parts", [P, UN, GT, 2, 2], I32)
                flat = t("flat", [P, UN, GT, 2], I32)
                found = t("found", [P, UN, GT, 2], I32)
                idx = t("idx", [P, UN, GT, 3], I32)
                same = t("same", [HEADS, G])
                neg = t("neg", [HEADS, UN, G])
                xin = t("xin", [P, UN, GT, n_in, D])
                st = t("st", [P, 2 * GT, 6])
                mv = t("mv", [P, 2 * GT, 2])
                sd = t("sd", [P, 2 * GT])
                rstd = t("rstd", [P, 2 * GT])
                hT = t("hT", [P, 2, KD, G])
                score = t("score", [HEADS, G])
                top = t("top", [HEADS, 2, G + 1])
                dd = t("dd", [HEADS, 2, G])
                ew = t("ew", [HEADS, 2, G])
                den = t("den", [HEADS, 2, G])
                feat = t("feat", [P, 2, KD, G])
                val = t("val", [P, KD, G])
                acc = t("acc", [P, 2, KD, G])
                rden = t("rden", [P, GT * HEADS])
                r = t("r", [P, GT, D])
                neg_r = t("neg_r", [P, GT, D])
                res = t("res", [P, 2, GT, D])
                hT_ps = [ps(f"hT_ps{q}") for q in range(2)]
                F_ps = ps("F_ps")
                S_ps = ps("S_ps")
                B_ps = [ps(f"B_ps{b}") for b in range(2)]
                O_ps = ps("O_ps")
                DT_ps = ps("DT_ps")
                DT = DT_ps[:, 0:GT * HEADS]

                rows_in, x_in, found_in, stored = ([sm(f"{n}{s}") for s in range(UN)] for n in ("rows_in", "x_in", "found_in", "stored"))
                (idx_made, stats_made, root_made, normed, turned, hT_made, scored, score_read, dd_made, ew_made,
                 spread, scanned, out_turned, out_read, neg_made, exp_made, res_made, f_summed, feat_made) = (sm(n) for n in (
                     "idx_made", "stats_made", "root_made", "normed", "turned", "hT_made", "scored", "score_read",
                     "dd_made", "ew_made", "spread", "scanned", "out_turned", "out_read", "neg_made", "exp_made",
                     "res_made", "f_summed", "feat_made"))
                n_rows = 2 if first_layer else 1
                target = H1 if first_layer else X1

                with nc.Block() as block:
                    @block.sync
                    def _(sp):
                        def load(g, s, i):
                            if reached(g, UN):
                                sp.wait_ge(idx_made, g - UN + 1)
                            if first_layer:
                                sp.dma_start(rows[:, s, :, :], by_dst[bass.ds(g * G + 1, G), :].rearrange("(j p) w -> p j w", p=P)).then_inc(rows_in[s], 16)
                            sp.dma_start(keys[:, s, :, :].rearrange("h e w -> h (e w)"),
                                         by_dst[bass.ds(g * G, G + 1), :].rearrange("e w -> (e w)").partition_broadcast(HEADS)).then_inc(rows_in[s], 16)

                        def store(g, s, i):
                            sp.wait_ge(res_made, g + 1)
                            sp.dma_start(target[bass.ds(g * G, G), :].rearrange("(j p) d -> p j d", p=P), res[:, s % 2, :, :]).then_inc(stored[s], 16)

                        pipelined(sp, [(load, 0), (store, 6)], GROUPS)
                        for s in range(UN):
                            sp.wait_ge(stored[s], 16 * len(range(s, GROUPS, UN)))

                    @block.gpsimd
                    def _(pool):
                        def gathers(g, s, i):
                            pool.wait_ge(idx_made, g + 1)
                            pool.sem_inc(apart, 1)
                            if reached(g, UN):
                                pool.wait_ge(normed if first_layer else res_made, g - UN + 1)
                                pool.sem_inc(apart, 1)
                            if first_layer:
                                if reached(g, UN):
                                    pool.wait_ge(turned, g - UN + 1)
                                    pool.sem_inc(apart, 1)
                            for j in range(GT):
                                for q in range(n_in):
                                    source = x if first_layer or q == 2 else H1
                                    pool.indirect_dma_start(
                                        out=xin[:, s, j, q, :], out_offset=None, in_=source,
                                        in_offset=bass.IndirectOffsetOnAxis(ap=idx[:, s, j, q:q + 1], axis=0)).then_inc(x_in[s], 16)
                            if first_layer:
                                for j in range(GT):
                                    for q in range(2):
                                        pool.indirect_dma_start(
                                            out=found[:, s, j, q:q + 1], out_offset=None, in_=end_of,
                                            in_offset=bass.IndirectOffsetOnAxis(ap=flat[:, s, j, q:q + 1], axis=0)).then_inc(found_in[s], 16)

                        pipelined(pool, [(gathers, 0)], GROUPS)

                    @block.vector
                    def _(dve):
                        def prepare(g, s, i):
                            dve.wait_ge(rows_in[s], 16 * n_rows * (i + 1))
                            if reached(i, 1):
                                dve.wait_ge(x_in[s], 16 * GT * n_in * i)
                            dve.tensor_tensor(same[:, :], keys[:, s, 1:G + 1, 1], keys[:, s, 0:G, 1], ALU.is_equal)
                            if first_layer:
                                if reached(i, 1):
                                    dve.wait_ge(found_in[s], 16 * GT * 2 * i)
                                dve.tensor_scalar(idx[:, s, :, 0:2], rows[:, s, :, :], float(N_NODES - 1), None, ALU.min)
                                dve.tensor_scalar(parts[:, s, :, :, 0], rows[:, s, :, :], 7, None, ALU.arith_shift_right)
                                dve.tensor_scalar(parts[:, s, :, :, 1], rows[:, s, :, :], P - 1, None, ALU.bitwise_and)
                                dve.drain()
                                dve.scalar_tensor_tensor(flat[:, s, :, :], parts[:, s, :, :, 1], float(NODE_TILES),
                                                         parts[:, s, :, :, 0], ALU.mult, ALU.add)
                            else:
                                dve.tensor_copy(idx[:, s, :, :], ends[:, bass.ds(g * GT, GT), :])
                                dve.drain()
                            dve.tensor_scalar(neg[:, s, :], same[:, :], -1.0, FAR, ALU.add, ALU.mult)
                            dve.drain().then_inc(idx_made, 1)

                        def norm(g, s, i):
                            dve.wait_ge(x_in[s], 16 * GT * n_in * (i + 1))
                            for j in range(GT):
                                for q in range(2):
                                    dve.bn_stats(st[:, 2 * j + q, :], xin[:, s, j, q, :])
                            dve.drain()
                            for a in range(2 * GT):
                                last = dve.bn_aggr(mv[:, a, :], st[:, a, :])
                            last.then_inc(stats_made, 1)
                            dve.wait_ge(root_made, g + 1)
                            dve.reciprocal(rstd[:, :], sd[:, :])
                            dve.drain()
                            for j in range(GT):
                                for q in range(2):
                                    a = 2 * j + q
                                    last = dve.tensor_scalar(xin[:, s, j, q, :], xin[:, s, j, q, :], mv[:, a, 0:1],
                                                             rstd[:, a:a + 1], ALU.subtract, ALU.mult)
                            last.then_inc(normed, 1)

                        def weigh(g, s, i):
                            s2 = s % 2
                            dve.wait_ge(scored, g + 1)
                            dve.tensor_scalar(score[:, :], S_ps[0:HEADS, 0:G], NEG_SLOPE, None, ALU.mult)
                            dve.tensor_copy(top[:, s2, 0:1], top[:, 1 - s2, G:G + 1])
                            dve.drain()
                            dve.tensor_tensor(score[:, :], score[:, :], S_ps[0:HEADS, 0:G], ALU.max).then_inc(score_read, 1)
                            dve.drain()
                            dve.tensor_tensor_scan(top[:, s2, 1:G + 1], neg[:, s, :], score[:, :], top[:, s2, 0:1], ALU.add, ALU.max)
                            dve.drain()
                            dve.tensor_tensor(dd[:, 0, :], top[:, s2, 0:G], top[:, s2, 1:G + 1], ALU.subtract)
                            dve.tensor_tensor(dd[:, 1, :], score[:, :], top[:, s2, 1:G + 1], ALU.subtract)
                            dve.drain()
                            dve.tensor_tensor(dd[:, 0, :], dd[:, 0, :], neg[:, s, :], ALU.min).then_inc(dd_made, 1)

                        def sums(g, s, i):
                            s2 = s % 2
                            dve.wait_ge(ew_made, g + 1)
                            dve.tensor_tensor_scan(den[:, s2, :], ew[:, 0, :], ew[:, 1, :], den[:, 1 - s2, G - 1:G], ALU.mult, ALU.add)
                            dve.wait_ge(spread, g + 1)
                            dve.wait_ge(feat_made, g + 1)
                            for b in range(KD):
                                dve.tensor_tensor(val[:, b, :], feat[:, s2, b, :], B_ps[b][:, G:2 * G], ALU.mult)
                            dve.drain()
                            for b in range(KD):
                                last = dve.tensor_tensor_scan(acc[:, s2, b, :], B_ps[b][:, 0:G], val[:, b, :],
                                                              acc[:, 1 - s2, b, G - 1:G], ALU.mult, ALU.add)
                            last.then_inc(scanned, 1)

                        def divide(g, s, i):
                            dve.wait_ge(out_turned, g + 1)
                            dve.reciprocal(rden[:, :], DT)
                            dve.drain()
                            dve.tensor_tensor(r[:, :, :].rearrange("p j (h d) -> p (j h) d", h=HEADS),
                                              O_ps[:, :].rearrange("p (a d) -> p a d", d=D_HEAD),
                                              rden[:, :].unsqueeze(2).to_broadcast([P, GT * HEADS, D_HEAD]), ALU.mult).then_inc(out_read, 1)
                            dve.drain()
                            if not first_layer:
                                dve.tensor_tensor(r[:, :, :], r[:, :, :], xin[:, s, :, 1, :], ALU.add)
                                dve.drain()
                            dve.tensor_scalar(neg_r[:, :, :], r[:, :, :], 0.0, None, ALU.min).then_inc(neg_made, 1)

                        def elu(g, s, i):
                            s2 = s % 2
                            dve.wait_ge(exp_made, g + 1)
                            if reached(g, 2):
                                dve.wait_ge(stored[(s + 2) % UN], 16 * (i + (s + 2) // UN))
                            ins = dve.scalar_tensor_tensor(res[:, s2, :, :], neg_r[:, :, :], -1.0, r[:, :, :], ALU.add, ALU.max)
                            if not first_layer:
                                dve.drain()
                                ins = dve.tensor_tensor(res[:, s2, :, :], res[:, s2, :, :], xin[:, s, :, 2, :], ALU.add)
                            ins.then_inc(res_made, 1)

                        def keep(g, s, i):
                            dve.wait_ge(found_in[s], 16 * GT * 2 * (i + 1))
                            dve.tensor_copy(ends[:, bass.ds(g * GT, GT), 0:2], found[:, s, :, :])
                            dve.tensor_copy(ends[:, bass.ds(g * GT, GT), 2:3], idx[:, s, :, 1:2])

                        dve.memset(top[:, :, :], 0.0)
                        dve.memset(den[:, :, :], 0.0)
                        dve.memset(acc[:, :, :, :], 0.0)
                        dve.drain()
                        if first_layer:
                            pipelined(dve, [(weigh, 4), (norm, 2), (divide, 5), (sums, 4), (elu, 5), (keep, 3), (prepare, 0)], GROUPS)
                        else:
                            pipelined(dve, [(weigh, 3), (divide, 4), (sums, 3), (elu, 4), (prepare, 0)], GROUPS)

                    @block.scalar
                    def _(act):
                        def root(g, s, i):
                            act.wait_ge(stats_made, g + 1)
                            act.activation(sd[:, :], mv[:, :, 1], ACT.Sqrt, bias=eps[:, :]).then_inc(root_made, 1)

                        def evac_h(g, s, i):
                            act.wait_ge(turned, g + 1)
                            for q in range(2):
                                last = act.activation(hT[:, q, :, :].rearrange("p k e -> p (k e)"), hT_ps[q][:, :],
                                                      ACT.Relu if first_layer else ACT.Copy)
                            last.then_inc(hT_made, 1)

                        def evac_f(g, s, i):
                            act.wait_ge(f_summed, g + 1)
                            if reached(g, 2):
                                act.wait_ge(scanned, g - 1)
                            act.activation(feat[:, s % 2, :, :].rearrange("p k e -> p (k e)"), F_ps[:, :], ACT.Copy).then_inc(feat_made, 1)

                        def weights(g, s, i):
                            act.wait_ge(dd_made, g + 1)
                            act.activation(ew[:, :, :], dd[:, :, :], ACT.Exp).then_inc(ew_made, 1)

                        def exp_r(g, s, i):
                            act.wait_ge(neg_made, g + 1)
                            act.activation(neg_r[:, :, :], neg_r[:, :, :], ACT.Exp).then_inc(exp_made, 1)

                        if first_layer:
                            pipelined(act, [(evac_h, 1), (weights, 2), (root, 0), (evac_f, 1), (exp_r, 3)], GROUPS)
                        else:
                            pipelined(act, [(evac_h, 0), (weights, 1), (evac_f, 0), (exp_r, 2)], GROUPS)

                    @block.tensor
                    def _(pe):
                        def turn(g, s, i):
                            if first_layer:
                                pe.wait_ge(normed, g + 1)
                            else:
                                pe.wait_ge(x_in[s], 16 * GT * n_in * (i + 1))
                            for q in range(2):
                                for j in range(GT):
                                    for k in range(KD):
                                        mm = pe.transpose(hT_ps[q][:, k * G + j * P:k * G + (j + 1) * P],
                                                          xin[:, s, j, q, k * P:(k + 1) * P], ident[:, :])
                            mm.then_inc(turned, 1)

                        def products(g, s, i):
                            pe.wait_ge(hT_made, g + 1)
                            if reached(g, 1):
                                pe.wait_ge(feat_made, g)
                            for m in range(KD):
                                for k in range(KD):
                                    mm = pe.matmul(F_ps[:, m * G:(m + 1) * G], w[:, k, m * P:(m + 1) * P], hT[:, 0, k, :],
                                                   start=(k == 0), stop=(k == KD - 1))
                            mm.then_inc(f_summed, 1)
                            if reached(g, 1):
                                pe.wait_ge(score_read, g)
                            for q in range(2):
                                for k in range(KD):
                                    mm = pe.matmul(S_ps[0:HEADS, 0:G], (wal, war)[q][:, k, :], hT[:, q, k, :],
                                                   start=(q == 0 and k == 0), stop=(q == 1 and k == KD - 1))
                            mm.then_inc(scored, 1)

                        def spread_weights(g, s, i):
                            pe.wait_ge(ew_made, g + 1)
                            if reached(g, 1):
                                pe.wait_ge(scanned, g)
                            for b in range(KD):
                                mm = pe.matmul(B_ps[b][:, :], headsel[:, b, :], ew[:, :, :].rearrange("h q e -> h (q e)"),
                                               start=True, stop=True)
                            mm.then_inc(spread, 1)

                        def turn_back(g, s, i):
                            pe.wait_ge(scanned, g + 1)
                            if reached(g, 1):
                                pe.wait_ge(out_read, g)
                            for j in range(GT):
                                for b in range(KD):
                                    pe.transpose(O_ps[:, j * D + b * P:j * D + (b + 1) * P],
                                                 acc[:, s % 2, b, j * P:(j + 1) * P], ident[:, :])
                                mm = pe.transpose(DT[:, j * HEADS:(j + 1) * HEADS], den[:, s % 2, j * P:(j + 1) * P], ident[0:HEADS, 0:HEADS])
                            mm.then_inc(out_turned, 1)

                        pipelined(pe, [(turn, 0), (turn_back, 2), (products, 0), (spread_weights, 1)], GROUPS)

        gat(1)
        end_phase()
        gat(2)
        end_phase()

        with ExitStack() as c:
            def t(name, shape, dt=F32):
                return c.enter_context(nc.sbuf_tensor("m_" + name, shape, dt))

            def ps(name):
                return c.enter_context(nc.psum_tensor("m_" + name, [P, 512], F32))

            def sm(name):
                return phase_sem("m_" + name)

            rows = t("rows", [P, UN, GT, ROW], I32)
            keys = t("keys", [1, UN, G + 1], I32)
            parts = t("parts", [P, UN, GT, 2, 2], I32)
            flat = t("flat", [P, UN, GT, 2], I32)
            found = t("found", [P, UN, GT, 2], I32)
            idx = t("idx", [P, UN, GT], I32)
            attT = t("attT", [D_EDGE, G])
            same = t("same", [1, 2, G])
            xin = t("xin", [P, UN, GT, 2, D])
            st = t("st", [P, 2 * GT, 6])
            mv = t("mv", [P, 2 * GT, 2])
            sd = t("sd", [P, 2 * GT])
            rstd = t("rstd", [P, 2 * GT])
            hT = t("hT", [P, 2, KD, G])
            hid = t("hid", [P, KH, G])
            msg = t("msg", [P, KD, G])
            agg = t("agg", [P, 2, KD, G])
            gs = t("gs", [P, 2, GT, HIDDEN])
            hT_ps = [ps(f"hT_ps{q}") for q in range(2)]
            misc_ps = ps("misc_ps")
            hid_ps = [ps(f"hid_ps{b}") for b in range(2)]
            msg_ps = ps("msg_ps")
            gs_ps = [ps(f"gs_ps{j}") for j in range(GT)]
            rows_in, found_in, x_in, x1_in, stored = ([sm(f"{n}{s}") for s in range(UN)] for n in (
                "rows_in", "found_in", "x_in", "x1_in", "stored"))
            (idx_made, stats_made, root_made, normed, turned, hT_made, attT_made, hid_summed, hid_made, msg_summed, msg_made,
             spread, scanned, gs_summed, gs_made) = (sm(n) for n in (
                 "idx_made", "stats_made", "root_made", "normed", "turned", "hT_made", "attT_made", "hid_summed", "hid_made",
                 "msg_summed", "msg_made", "spread", "scanned", "gs_summed", "gs_made"))
            with nc.Block() as block:
                @block.sync
                def _(sp):
                    def load(g, s, i):
                        if reached(g, UN):
                            sp.wait_ge(attT_made, g - UN + 1)
                        sp.dma_start(rows[:, s, :, :], by_src[bass.ds(g * G + 1, G), :].rearrange("(j p) w -> p j w", p=P)).then_inc(rows_in[s], 16)
                        with nc.allow_non_contiguous_dma(reason="the sources alone, of rows"):
                            sp.dma_start(keys[:, s, :], by_src[bass.ds(g * G, G + 1), 0:1].rearrange("e o -> o e")).then_inc(rows_in[s], 16)

                    def store(g, s, i):
                        sp.wait_ge(gs_made, g + 1)
                        sp.dma_start(GS[bass.ds(g * G, G), :].rearrange("(j p) d -> p j d", p=P), gs[:, s % 2, :, :]).then_inc(stored[s], 16)

                    pipelined(sp, [(load, 0), (store, 6)], GROUPS)
                    for s in range(UN):
                        sp.wait_ge(stored[s], 16 * len(range(s, GROUPS, UN)))

                @block.gpsimd
                def _(pool):
                    def first_gathers(g, s, i):
                        pool.wait_ge(idx_made, g + 1)
                        pool.sem_inc(apart, 1)
                        if reached(g, UN):
                            pool.wait_ge(turned, g - UN + 1)
                            pool.sem_inc(apart, 1)
                        for j in range(GT):
                            for q in range(2):
                                pool.indirect_dma_start(
                                    out=found[:, s, j, q:q + 1], out_offset=None, in_=end_of,
                                    in_offset=bass.IndirectOffsetOnAxis(ap=flat[:, s, j, q:q + 1], axis=0)).then_inc(found_in[s], 16)
                        for j in range(GT):
                            pool.indirect_dma_start(
                                out=xin[:, s, j, 0, :], out_offset=None, in_=x,
                                in_offset=bass.IndirectOffsetOnAxis(ap=idx[:, s, j:j + 1], axis=0)).then_inc(x_in[s], 16)

                    def second_gathers(g, s, i):
                        pool.wait_ge(found_in[s], 16 * GT * 2 * (i + 1))
                        pool.sem_inc(apart, 1)
                        for j in range(GT):
                            pool.indirect_dma_start(
                                out=xin[:, s, j, 1, :], out_offset=None, in_=X1,
                                in_offset=bass.IndirectOffsetOnAxis(ap=found[:, s, j, 1:2], axis=0)).then_inc(x1_in[s], 16)
                        pool.wait_ge(x_in[s], 16 * GT * (i + 1))
                        pool.sem_inc(apart, 1)
                        for j in range(GT):
                            pool.indirect_dma_start(
                                out=xin[:, s, j, 0, :], out_offset=None, in_=X1,
                                in_offset=bass.IndirectOffsetOnAxis(ap=found[:, s, j, 0:1], axis=0),
                                bounds_check=NO_ROW - 1, oob_is_err=False).then_inc(x1_in[s], 16)

                    pipelined(pool, [(first_gathers, 0), (second_gathers, 1)], GROUPS)

                @block.vector
                def _(dve):
                    def prepare(g, s, i):
                        dve.wait_ge(rows_in[s], 32 * i + 32)
                        if reached(i, 1):
                            dve.wait_ge(x1_in[s], 32 * GT * i)
                        dve.tensor_scalar(idx[:, s, :], rows[:, s, :, 0], float(N_NODES - 1), None, ALU.min)
                        dve.tensor_scalar(parts[:, s, :, :, 0], rows[:, s, :, 0:2], 7, None, ALU.arith_shift_right)
                        dve.tensor_scalar(parts[:, s, :, :, 1], rows[:, s, :, 0:2], P - 1, None, ALU.bitwise_and)
                        dve.drain()
                        dve.scalar_tensor_tensor(flat[:, s, :, :], parts[:, s, :, :, 1], float(NODE_TILES),
                                                 parts[:, s, :, :, 0], ALU.mult, ALU.add).then_inc(idx_made, 1)

                    def norm(g, s, i):
                        dve.wait_ge(x1_in[s], 32 * GT * (i + 1))
                        for j in range(GT):
                            for q in range(2):
                                dve.bn_stats(st[:, 2 * j + q, :], xin[:, s, j, q, :])
                        dve.drain()
                        for a in range(2 * GT):
                            last = dve.bn_aggr(mv[:, a, :], st[:, a, :])
                        last.then_inc(stats_made, 1)
                        dve.wait_ge(root_made, g + 1)
                        dve.reciprocal(rstd[:, :], sd[:, :])
                        dve.drain()
                        for j in range(GT):
                            for q in range(2):
                                a = 2 * j + q
                                last = dve.tensor_scalar(xin[:, s, j, q, :], xin[:, s, j, q, :], mv[:, a, 0:1],
                                                         rstd[:, a:a + 1], ALU.subtract, ALU.mult)
                        last.then_inc(normed, 1)

                    def flags(g, s, i):
                        if reached(g, 2):
                            dve.wait_ge(spread, g - 1)
                        dve.tensor_tensor(same[:, s % 2, :], keys[:, s, 1:G + 1], keys[:, s, 0:G], ALU.is_equal)

                    def evac_att(g, s, i):
                        dve.wait_ge(turned, g + 1)
                        dve.tensor_copy(attT[:, :], misc_ps[0:D_EDGE, 0:G]).then_inc(attT_made, 1)

                    def scan(g, s, i):
                        dve.wait_ge(msg_made, g + 1)
                        dve.wait_ge(spread, g + 1)
                        for b in range(KD):
                            last = dve.tensor_tensor_scan(agg[:, s % 2, b, :], misc_ps[:, G:2 * G], msg[:, b, :],
                                                          agg[:, 1 - s % 2, b, G - 1:G], ALU.mult, ALU.add)
                        last.then_inc(scanned, 1)

                    def add_bias(g, s, i):
                        dve.wait_ge(gs_summed, g + 1)
                        if reached(g, 2):
                            dve.wait_ge(stored[(s + 2) % UN], 16 * (i + (s + 2) // UN))
                        for j in range(GT):
                            last = dve.tensor_tensor(gs[:, s % 2, j, :], gs_ps[j][:, :], ub1r[:, :], ALU.add)
                        last.then_inc(gs_made, 1)

                    dve.memset(agg[:, :, :, :], 0.0)
                    dve.drain()
                    pipelined(dve, [(flags, 4), (evac_att, 4), (add_bias, 6), (norm, 3), (scan, 5), (prepare, 0)], GROUPS)

                @block.scalar
                def _(act):
                    def root(g, s, i):
                        act.wait_ge(stats_made, g + 1)
                        act.activation(sd[:, :], mv[:, :, 1], ACT.Sqrt, bias=eps[:, :]).then_inc(root_made, 1)

                    def evac_h(g, s, i):
                        act.wait_ge(turned, g + 1)
                        for q in range(2):
                            last = act.activation(hT[:, q, :, :].rearrange("p k e -> p (k e)"), hT_ps[q][:, :], ACT.Relu)
                        last.then_inc(hT_made, 1)

                    def evac_hid(g, s, i):
                        act.wait_ge(hid_summed, g + 1)
                        for m in range(KH):
                            last = act.activation(hid[:, m, :], hid_ps[m // 2][:, (m % 2) * G:(m % 2 + 1) * G], ACT.Relu,
                                                  bias=mb1c[:, m:m + 1])
                        last.then_inc(hid_made, 1)

                    def evac_msg(g, s, i):
                        act.wait_ge(msg_summed, g + 1)
                        if reached(g, 1):
                            act.wait_ge(scanned, g)
                        for m in range(KD):
                            last = act.activation(msg[:, m, :], msg_ps[:, m * G:(m + 1) * G], ACT.Identity, bias=mb2c[:, m:m + 1])
                        last.then_inc(msg_made, 1)

                    pipelined(act, [(evac_hid, 2), (evac_h, 1), (root, 0), (evac_msg, 2)], GROUPS)

                @block.tensor
                def _(pe):
                    def turn(g, s, i):
                        pe.wait_ge(normed, g + 1)
                        if reached(g, 2):
                            pe.wait_ge(scanned, g - 1)
                        for q in range(2):
                            for j in range(GT):
                                for k in range(KD):
                                    pe.transpose(hT_ps[q][:, k * G + j * P:k * G + (j + 1) * P],
                                                 xin[:, s, j, q, k * P:(k + 1) * P], ident[:, :])
                        for j in range(GT):
                            mm = pe.transpose(misc_ps[0:D_EDGE, j * P:(j + 1) * P], rows[:, s, j, 2:ROW].bitcast(F32), ident[:, :])
                        mm.then_inc(turned, 1)

                    def hidden(g, s, i):
                        pe.wait_ge(hT_made, g + 1)
                        pe.wait_ge(attT_made, g + 1)
                        if reached(g, 1):
                            pe.wait_ge(hid_made, g)
                        for m in range(KH):
                            o = hid_ps[m // 2][:, (m % 2) * G:(m % 2 + 1) * G]
                            for q in range(2):
                                for k in range(KD):
                                    pe.matmul(o, mw1[:, q * KD + k, m * P:(m + 1) * P], hT[:, q, k, :],
                                              start=(q == 0 and k == 0), stop=False)
                            mm = pe.matmul(o, mw1e[:, m * P:(m + 1) * P], attT[:, :], start=False, stop=True)
                        mm.then_inc(hid_summed, 1)

                    def messages(g, s, i):
                        pe.wait_ge(hid_made, g + 1)
                        if reached(g, 1):
                            pe.wait_ge(msg_made, g)
                        for m in range(KD):
                            for k in range(KH):
                                mm = pe.matmul(msg_ps[:, m * G:(m + 1) * G], mw2[:, k, m * P:(m + 1) * P], hid[:, k, :],
                                               start=(k == 0), stop=(k == KH - 1))
                        mm.then_inc(msg_summed, 1)
                        pe.wait_ge(attT_made, g + 2 if not isinstance(g, int) else min(g + 2, GROUPS))
                        pe.matmul(misc_ps[:, G:2 * G], ones[0:1, :], same[:, s % 2, :], start=True, stop=True).then_inc(spread, 1)

                    def aggregate(g, s, i):
                        pe.wait_ge(scanned, g + 1)
                        if reached(g, 1):
                            pe.wait_ge(gs_made, g)
                        for j in range(GT):
                            for k in range(KD):
                                mm = pe.matmul(gs_ps[j][:, :], agg[:, s % 2, k, j * P:(j + 1) * P], uw1[:, KD + k, :],
                                               start=(k == 0), stop=(k == KD - 1))
                        mm.then_inc(gs_summed, 1)

                    pipelined(pe, [(turn, 0), (aggregate, 2), (messages, 1), (hidden, 0)], GROUPS)

        end_phase()

        NT = 2
        STEPS = (NODE_TILES + NT - 1) // NT
        with ExitStack() as c:
            def t(name, shape, dt=F32):
                return c.enter_context(nc.sbuf_tensor("u_" + name, shape, dt))

            def ps(name):
                return c.enter_context(nc.psum_tensor("u_" + name, [P, 512], F32))

            def sm(name):
                return phase_sem("u_" + name)

            idx = t("idx", [P, UN, 2, NT], I32)
            xt = t("xt", [P, UN, NT, D])
            gb = t("gb", [P, UN, NT, HIDDEN])
            xn = t("xn", [P, 2, NT, D])
            st = t("st", [P, NT, 6])
            mv = t("mv", [P, NT, 2])
            sd = t("sd", [P, NT])
            rstd = t("rstd", [P, NT])
            res = t("res", [P, UN, NT, D])
            hT = t("hT", [P, KD, NT * P])
            ua = t("ua", [P, NT, HIDDEN])
            uT = t("uT", [P, NT, KH, P])
            ot = t("ot", [P, 2, NT, D])
            hT_ps = ps("hT_ps")
            U_ps = [ps(f"U_ps{j}") for j in range(NT)]
            uT_ps = [ps(f"uT_ps{j}") for j in range(NT)]
            O_ps = ps("O_ps")
            x_in, x1_in, gs_in, stored = ([sm(f"{n}{s}") for s in range(UN)] for n in ("x_in", "x1_in", "gs_in", "stored"))
            (idx_made, filled, stats_made, root_made, normed, res_made, turned, hT_made, u_summed, u_made, u_turned, uT_made,
             o_summed, o_made) = (sm(n) for n in (
                 "idx_made", "filled", "stats_made", "root_made", "normed", "res_made", "turned", "hT_made", "u_summed",
                 "u_made", "u_turned", "uT_made", "o_summed", "o_made"))
            last_step = STEPS - 1
            assert NODE_TILES - last_step * NT == 1

            def tiles(g):
                return 1 if isinstance(g, int) and g == last_step else NT

            with nc.Block() as block:
                @block.sync
                def _(sp):
                    def load(g, s, i):
                        if reached(g, UN):
                            sp.wait_ge(res_made, g - UN + 1)
                        if tiles(g) == NT:
                            sp.dma_start(xt[:, s, :, :], x[bass.ds(g * (NT * P), NT * P), :].rearrange("(j p) d -> p j d", p=P)).then_inc(x_in[s], 16)
                        else:
                            sp.dma_start(xt[0:LAST_ROWS, s, 0, :], x[g * NT * P:N_NODES, :]).then_inc(x_in[s], 16)

                    def store(g, s, i):
                        sp.wait_ge(o_made, g + 1)
                        if tiles(g) == NT:
                            sp.dma_start(out[bass.ds(g * (NT * P), NT * P), :].rearrange("(j p) d -> p j d", p=P), ot[:, s % 2, :, :]).then_inc(stored[s], 16)
                        else:
                            sp.dma_start(out[g * NT * P:N_NODES, :], ot[0:LAST_ROWS, s % 2, 0, :]).then_inc(stored[s], 16)

                    pipelined(sp, [(load, 0), (store, 6)], STEPS)
                    for s in range(UN):
                        sp.wait_ge(stored[s], 16 * len(range(s, STEPS, UN)))

                @block.gpsimd
                def _(pool):
                    def gathers(g, s, i):
                        pool.wait_ge(idx_made, g + 1)
                        pool.sem_inc(apart, 1)
                        pool.wait_ge(x_in[s], 16 * i + 16)
                        pool.sem_inc(apart, 1)
                        for j in range(tiles(g)):
                            pool.indirect_dma_start(
                                out=xt[:, s, j, :], out_offset=None, in_=X1,
                                in_offset=bass.IndirectOffsetOnAxis(ap=idx[:, s, 0, j:j + 1], axis=0),
                                bounds_check=NO_ROW - 1, oob_is_err=False).then_inc(x1_in[s], 16)
                        pool.wait_ge(filled, g + 1)
                        pool.sem_inc(apart, 1)
                        for j in range(tiles(g)):
                            pool.indirect_dma_start(
                                out=gb[:, s, j, :], out_offset=None, in_=GS,
                                in_offset=bass.IndirectOffsetOnAxis(ap=idx[:, s, 1, j:j + 1], axis=0),
                                bounds_check=NO_ROW - 1, oob_is_err=False).then_inc(gs_in[s], 16)

                    pipelined(pool, [(gathers, 0)], STEPS)

                def arrived(eng, signals, g, s, i):
                    eng.wait_ge(signals[s], 16 * NT * i + 16 * tiles(g))

                @block.vector
                def _(dve):
                    def indices(g, s, i):
                        n = tiles(g)
                        if reached(i, 1):
                            dve.wait_ge(gs_in[s], 16 * NT * i)
                        dve.tensor_copy(idx[:, s, 0, 0:n], end_d[:, bass.ds(g * NT, n)])
                        dve.tensor_copy(idx[:, s, 1, 0:n], end_s[:, bass.ds(g * NT, n)]).then_inc(idx_made, 1)

                    def stats(g, s, i):
                        n = tiles(g)
                        arrived(dve, x1_in, g, s, i)
                        for j in range(n):
                            dve.bn_stats(st[:, j, :], xt[:, s, j, :])
                        dve.drain()
                        for j in range(n):
                            last = dve.bn_aggr(mv[:, j, :], st[:, j, :])
                        last.then_inc(stats_made, 1)

                    def norm(g, s, i):
                        n = tiles(g)
                        dve.wait_ge(root_made, g + 1)
                        dve.reciprocal(rstd[:, 0:n], sd[:, 0:n])
                        dve.drain()
                        for j in range(n):
                            last = dve.tensor_scalar(xn[:, s % 2, j, :], xt[:, s, j, :], mv[:, j, 0:1], rstd[:, j:j + 1], ALU.subtract, ALU.mult)
                        last.then_inc(normed, 1)
                        dve.drain()
                        dve.scalar_tensor_tensor(res[:, s, 0:n, :], xn[:, s % 2, 0:n, :], 0.0, xt[:, s, 0:n, :], ALU.max, ALU.add).then_inc(res_made, 1)
                        dve.drain()
                        dve.tensor_tensor(res[:, s, 0:n, :], res[:, s, 0:n, :],
                                          ub2r[:, :].unsqueeze(1).to_broadcast([P, n, D]), ALU.add)

                    def add_messages(g, s, i):
                        n = tiles(g)
                        dve.wait_ge(u_summed, g + 1)
                        arrived(dve, gs_in, g, s, i)
                        if reached(g, 1):
                            dve.wait_ge(u_turned, g)
                        for j in range(n):
                            last = dve.tensor_tensor(ua[:, j, :], U_ps[j][:, :], gb[:, s, j, :], ALU.add)
                        last.then_inc(u_made, 1)

                    def finish(g, s, i):
                        n = tiles(g)
                        dve.wait_ge(o_summed, g + 1)
                        if reached(g, 2):
                            dve.wait_ge(stored[(s + 2) % UN], 16 * (i + (s + 2) // UN))
                        dve.tensor_tensor(ot[:, s % 2, 0:n, :], O_ps[:, 0:n * D].rearrange("p (j d) -> p j d", d=D), res[:, s, 0:n, :],
                                          ALU.add).then_inc(o_made, 1)

                    pipelined(dve, [(stats, 3), (finish, 6), (norm, 3), (add_messages, 4), (indices, 0)], STEPS)

                @block.scalar
                def _(act):
                    def fill(g, s, i):
                        if reached(g, UN):
                            act.wait_ge(u_made, g - UN + 1)
                        for j in range(tiles(g)):
                            last = act.activation(gb[:, s, j, :], ub1r[:, :], ACT.Copy)
                        last.then_inc(filled, 1)

                    def root(g, s, i):
                        n = tiles(g)
                        act.wait_ge(stats_made, g + 1)
                        act.activation(sd[:, 0:n], mv[:, 0:n, 1], ACT.Sqrt, bias=eps[:, :]).then_inc(root_made, 1)

                    def evac_h(g, s, i):
                        n = tiles(g)
                        act.wait_ge(turned, g + 1)
                        act.activation(hT[:, :, 0:n * P], hT_ps[:, :].rearrange("p (k e) -> p k e", k=KD)[:, :, 0:n * P],
                                       ACT.Relu).then_inc(hT_made, 1)

                    def evac_u(g, s, i):
                        act.wait_ge(u_turned, g + 1)
                        for j in range(tiles(g)):
                            last = act.activation(uT[:, j, :, :].rearrange("p k e -> p (k e)"), uT_ps[j][:, :], ACT.Relu)
                        last.then_inc(uT_made, 1)

                    pipelined(act, [(evac_h, 4), (root, 3), (evac_u, 5), (fill, 0)], STEPS)

                @block.tensor
                def _(pe):
                    def turn(g, s, i):
                        pe.wait_ge(normed, g + 1)
                        for j in range(tiles(g)):
                            for k in range(KD):
                                mm = pe.transpose(hT_ps[:, k * NT * P + j * P:k * NT * P + (j + 1) * P],
                                                  xn[:, s % 2, j, k * P:(k + 1) * P], ident[:, :])
                        mm.then_inc(turned, 1)

                    def up(g, s, i):
                        pe.wait_ge(hT_made, g + 1)
                        if reached(g, 1):
                            pe.wait_ge(u_made, g)
                        for j in range(tiles(g)):
                            for k in range(KD):
                                mm = pe.matmul(U_ps[j][:, :], hT[:, k, j * P:(j + 1) * P], uw1[:, k, :],
                                               start=(k == 0), stop=(k == KD - 1))
                        mm.then_inc(u_summed, 1)

                    def turn_u(g, s, i):
                        pe.wait_ge(u_made, g + 1)
                        if reached(g, 1):
                            pe.wait_ge(uT_made, g)
                        for j in range(tiles(g)):
                            for m in range(KH):
                                mm = pe.transpose(uT_ps[j][:, m * P:(m + 1) * P], ua[:, j, m * P:(m + 1) * P], ident[:, :])
                        mm.then_inc(u_turned, 1)

                    def down(g, s, i):
                        pe.wait_ge(uT_made, g + 1)
                        if reached(g, 1):
                            pe.wait_ge(o_made, g)
                        for j in range(tiles(g)):
                            for m in range(KH):
                                mm = pe.matmul(O_ps[:, j * D:(j + 1) * D], uT[:, j, m, :], uw2[:, m, :],
                                               start=(m == 0), stop=(m == KH - 1))
                        mm.then_inc(o_summed, 1)

                    pipelined(pe, [(turn, 0), (turn_u, 1), (up, 0), (down, 1)], STEPS)


_INS = ["x", "src", "dst", "edge_attr_16", "L0_gnn_W1", "L0_gnn_al1", "L0_gnn_ar1", "L0_gnn_W2", "L0_gnn_al2",
        "L0_gnn_ar2", "L1_gnn_mW1", "L1_gnn_mb1", "L1_gnn_mW2", "L1_gnn_mb2", "L1_gnn_uW1", "L1_gnn_ub1",
        "L1_gnn_uW2", "L1_gnn_ub2"]


def kernel(**inputs):
    import numpy as _np
    import concourse.bacc as _bacc
    from concourse import mybir as _mybir
    from concourse.bass_utils import run_bass_kernel_spmd as _run

    nc = _bacc.Bacc("TRN2", target_bir_lowering=False, num_devices=1)
    arrays, args = {}, []
    for name in _INS:
        a = _np.ascontiguousarray(inputs[name])
        arrays[f"in_{name}"] = a
        args.append(nc.dram_tensor(f"in_{name}", a.shape, _mybir.dt.from_np(a.dtype), kind="ExternalInput").ap())
    out = nc.dram_tensor("out_dram", (N_NODES, D), _mybir.dt.float32, kind="ExternalOutput").ap()
    build(nc, *args, out)
    r = _run(nc, [arrays], core_ids=[0])
    return r.results[0]["out_dram"]
```

```python
from contextlib import ExitStack

import numpy as np
import concourse.bass as bass
from concourse import mybir

F32 = mybir.dt.float32
F16 = mybir.dt.float16
BF16 = mybir.dt.bfloat16
I32 = mybir.dt.int32
F32R = mybir.dt.float32r
ALU = mybir.AluOpType
ACT = mybir.ActivationFunctionType
AX = mybir.AxisListType

P = 128
N_NODES, D = 50000, 256
N_EDGES, D_EDGE = 12500, 16
HEADS = 4
D_HEAD = D // HEADS
HIDDEN = 512
KD = D // P
KH = HIDDEN // P
TILES = 100
EDGES = P * TILES
PARTS_USED = N_EDGES // TILES
assert PARTS_USED * TILES == N_EDGES and PARTS_USED < P
NODE_TILES = -(-N_NODES // P)
LAST_ROWS = N_NODES - (NODE_TILES - 1) * P
PAD_KEY = NODE_TILES * P - 1
assert PAD_KEY >= N_NODES
NO_ROW = EDGES
G = 256
GT = G // P
GROUPS = EDGES // G
ROW = 2 + D_EDGE
ATT_HI, ATT_LO, ATT_HI2 = 0, 32, 64
UN = 4
UN_SORT = 10
PARTS = ((0, 1), (1, 0), (0, 0))
EPS = 1e-5
NEG_SLOPE = 0.2
FAR = 1e30


def build(nc, x, src, dst, attr, W1, al1, ar1, W2, al2, ar2, mW1, mb1, mW2, mb2, uW1, ub1, uW2, ub2, out):
    ctx = ExitStack()

    def dram(name, shape, dt):
        return nc.dram_tensor(name, shape, dt, kind="Internal").ap()

    by_dst = dram("by_dst", [EDGES + 1, 2], I32)
    by_src = dram("by_src", [EDGES + 1, ROW], I32)
    end_of = dram("end_of", [P * NODE_TILES, 1], I32)
    H1 = dram("H1", [EDGES + 1, D], F32)
    X1 = dram("X1", [EDGES + 1, D], F32)
    GS = dram("GS", [EDGES, HIDDEN], F32)

    with ctx:
        def sb(name, shape, dt=F32):
            return ctx.enter_context(nc.sbuf_tensor(name, shape, dt))

        def sem(name):
            return ctx.enter_context(nc.semaphore(name))

        ident = sb("ident", [P, P])
        ident16 = sb("ident16", [P, P], F16)
        tri = sb("tri", [P, P])
        trilow = sb("trilow", [P, P])
        ones = sb("ones", [P, P])
        iota_t = sb("iota_t", [P, NODE_TILES], F16)
        eps = sb("eps", [P, 1])
        headsel = sb("headsel", [HEADS, KD, P])
        w1 = sb("w1", [P, KD, D])
        w2 = sb("w2", [P, KD, D])
        wa = sb("wa", [P, 4, KD, HEADS])
        mw1 = [sb(f"mw1_{part}", [P, 2 * KD, HIDDEN], F32R) for part in ("hi", "lo")]
        mw2 = [sb(f"mw2_{part}", [P, KH, D], F32R) for part in ("hi", "lo")]
        uw1 = [sb(f"uw1_{part}", [P, 2 * KD, HIDDEN], F32R) for part in ("hi", "lo")]
        uw2 = [sb(f"uw2_{part}", [P, KH, D], F32R) for part in ("hi", "lo")]
        mw1e = sb("mw1e", [P, HIDDEN], F32R)
        mb2c = sb("mb2c", [P, KD])
        ub1r = sb("ub1r", [P, HIDDEN])
        ub2r = sb("ub2r", [P, D])
        end_d = sb("end_d", [P, NODE_TILES], I32)
        end_s = sb("end_s", [P, NODE_TILES], I32)
        ends = sb("ends", [P, TILES, 3], I32)

        def reached(v, n):
            return not isinstance(v, int) or v >= n

        def pipelined(eng, stages, n, slots=UN):
            lags = [lag for _, lag in stages if lag is not None]

            def step(i, c):
                for stage, lag in stages:
                    if lag is None:
                        stage()
                        continue
                    g = slots * i + c - lag
                    if not isinstance(g, int) or 0 <= g < n:
                        stage(g, (c - lag) % slots, i + (c - lag) // slots)

            first = -(-(max(lags) + slots) // slots)
            for T in range(first * slots):
                step(T // slots, T % slots)
            with eng.Fori(first, (n - 1) // slots) as i:
                for c in range(slots):
                    step(i, c)
            for T in range((n - 1) // slots * slots, n + max(lags)):
                step(T // slots, T % slots)

        apart = sem("apart")
        phase_sems = []

        def phase_sem(name):
            phase_sems.append(nc.alloc_semaphore(name))
            return phase_sems[-1]

        def end_phase():
            nc.clear_and_free_semaphores(list(phase_sems))
            nc.all_engine_barrier()
            phase_sems.clear()


        with ExitStack() as c0:
            def sb0(name, shape, dt=F32):
                return c0.enter_context(nc.sbuf_tensor(name, shape, dt))

            av = sb0("av", [P, 4, D])
            prod = sb0("prod", [P, 4, KD, D])
            key = sb0("key", [P, 2, TILES], I32)
            hi_i = sb0("hi_i", [P, 2, TILES], I32)
            lo_i = sb0("lo_i", [P, 2, TILES], I32)
            keyf = sb0("keyf", [P, 2, TILES])
            hi = sb0("hi", [P, 2, TILES])
            lo = sb0("lo", [P, 2, TILES])
            pay = sb0("pay", [P, TILES, ROW], I32)
            zrow = sb0("zrow", [1, D])
            w_full = {"mw1": sb0("mw1_full", [P, 2 * KD, HIDDEN]), "mw2": sb0("mw2_full", [P, KH, D]),
                      "uw1": sb0("uw1_full", [P, 2 * KD, HIDDEN]), "uw2": sb0("uw2_full", [P, KH, D])}
            mw1e_full = sb0("mw1e_full", [P, HIDDEN])
            sentinel = sb0("sentinel", [1, ROW], I32)
            ohH = sb0("ohH", [P, UN_SORT, 2, NODE_TILES], F16)
            ohL = sb0("ohL", [P, UN_SORT, 2, P], F16)
            cnt = sb0("cnt", [P, 2, NODE_TILES])
            tot = sb0("tot", [P, 2, NODE_TILES])
            cum = sb0("cum", [P, 2, NODE_TILES])
            first = sb0("first", [P, 2, NODE_TILES])
            has = sb0("has", [P, 2, NODE_TILES])
            onesr = sb0("onesr", [P, NODE_TILES])

            w_in, k_in, a_in, cst, prodd, wad = (sem(n) for n in ("weights_in", "keys_in", "attr_in", "consts_made", "prod_made", "wa_made"))
            keyset, pay_set, z_out, z_set = (sem(n) for n in ("keys_preset", "rows_preset", "zeros_out", "zeros_set"))
            W_LOADS = 16 * 18
            with nc.Block() as block:
                @block.sync
                def _(sp):
                    sp.wait_ge(keyset, 1)
                    sp.dma_start(key[0:PARTS_USED, 0, :], dst.rearrange("(p t) -> p t", t=TILES)).then_inc(k_in, 16)
                    sp.dma_start(key[0:PARTS_USED, 1, :], src.rearrange("(p t) -> p t", t=TILES)).then_inc(k_in, 16)
                    sp.wait_ge(pay_set, 1)
                    sp.dma_start(pay[0:PARTS_USED, :, 2:ROW], attr.bitcast(I32).rearrange("(p t) f -> p t f", t=TILES)).then_inc(a_in, 16)
                    sp.wait_ge(z_set, 2)
                    sp.dma_start(H1[NO_ROW:NO_ROW + 1, :], zrow[:, :]).then_inc(z_out, 16)
                    sp.dma_start(X1[NO_ROW:NO_ROW + 1, :], zrow[:, :]).then_inc(z_out, 16)
                    sp.dma_start(by_dst[0:1, :], sentinel[:, 0:2]).then_inc(z_out, 16)
                    sp.dma_start(by_src[0:1, :], sentinel[:, :]).then_inc(z_out, 16)

                @block.gpsimd
                def _(pool):
                    pool.memset(ident[:, :], 0.0)
                    pool.memset(tri[:, :], 1.0)
                    pool.memset(trilow[:, :], 1.0)
                    pool.memset(headsel[:, :, :], 1.0)
                    pool.iota(iota_t[:, :], pattern=[[1, NODE_TILES]], base=0, channel_multiplier=0,
                              allow_small_or_imprecise_dtypes=True)
                    pool.drain()
                    pool.affine_select(out=ident[:, :], in_=ident[:, :], compare_op=ALU.not_equal, fill=1.0,
                                       base=0, pattern=[[-1, P]], channel_multiplier=1)
                    pool.affine_select(out=tri[:, :], in_=tri[:, :], compare_op=ALU.is_ge, fill=0.0,
                                       base=-1, pattern=[[1, P]], channel_multiplier=-1)
                    pool.affine_select(out=trilow[:, :], in_=trilow[:, :], compare_op=ALU.is_ge, fill=0.0,
                                       base=-1, pattern=[[-1, P]], channel_multiplier=1)
                    pool.affine_select(out=headsel[:, :, :], in_=headsel[:, :, :], compare_op=ALU.is_ge, fill=0.0,
                                       base=0, pattern=[[P, KD], [1, P]], channel_multiplier=-D_HEAD)
                    pool.drain()
                    pool.affine_select(out=headsel[:, :, :], in_=headsel[:, :, :], compare_op=ALU.is_ge, fill=0.0,
                                       base=D_HEAD - 1, pattern=[[-P, KD], [-1, P]], channel_multiplier=D_HEAD)
                    pool.tensor_copy(ident16[:, :], ident[:, :])

                @block.vector
                def _(dve):
                    dve.memset(key[:, :, :], PAD_KEY).then_inc(keyset, 1)
                    dve.memset(pay[:, :, :], 0).then_inc(pay_set, 1)
                    dve.memset(mw1e_full[:, :], 0.0)
                    dve.memset(zrow[:, :], 0.0).then_inc(z_set, 1)
                    dve.memset(sentinel[:, :], -1).then_inc(z_set, 1)
                    dve.memset(ones[:, :], 1.0)
                    dve.memset(onesr[:, :], 1.0)
                    dve.memset(eps[:, :], EPS)
                    dve.wait_ge(k_in, 32)
                    dve.tensor_scalar(hi_i[:, :, :], key[:, :, :], 7, None, ALU.arith_shift_right)
                    dve.tensor_scalar(lo_i[:, :, :], key[:, :, :], P - 1, None, ALU.bitwise_and)
                    dve.tensor_copy(keyf[:, :, :], key[:, :, :])
                    dve.drain()
                    dve.tensor_copy(hi[:, :, :], hi_i[:, :, :])
                    dve.tensor_copy(lo[:, :, :], lo_i[:, :, :])
                    dve.tensor_copy(pay[:, :, 0], key[:, 1, :])
                    dve.tensor_copy(pay[:, :, 1], key[:, 0, :])

            cnt_ps = [c0.enter_context(nc.psum_tensor(f"cnt_ps{k}", [P, 512], F32)) for k in range(2)]
            onehot, counted, slot_free, table_up = (sem(n) for n in ("onehot_made", "tile_counted", "onehot_free", "tables_stored"))
            cum_ps, cnt_done, seeded = (sem(n) for n in ("sums_made", "cnt_copied", "starts_seeded"))
            first_done = sem("first_made")
            tot_ps = [c0.enter_context(nc.psum_tensor(f"tot_ps{k}", [P, 512], F32)) for k in range(2)]
            pre_ps = [c0.enter_context(nc.psum_tensor(f"pre_ps{k}", [P, 512], F32)) for k in range(2)]

            def make_onehots(dve, t, slot):
                for k in range(2):
                    dve.tensor_scalar(ohH[:, slot, k, :], iota_t[:, :], hi[:, k, bass.ds(t, 1)], None, ALU.is_equal)
                    last = dve.tensor_scalar(ohL[:, slot, k, :], iota_t[:, 0:P], lo[:, k, bass.ds(t, 1)], None, ALU.is_equal)
                return last

            with nc.Block() as block:
                @block.vector
                def _(dve):
                    for slot in range(UN_SORT):
                        make_onehots(dve, slot, slot).then_inc(onehot, 1)
                    with dve.Fori(1, TILES // UN_SORT) as i:
                        for slot in range(UN_SORT):
                            dve.wait_ge(slot_free, UN_SORT * i + slot - UN_SORT + 1)
                            make_onehots(dve, UN_SORT * i + slot, slot).then_inc(onehot, 1)
                    dve.wait_ge(counted, 1)
                    for k in range(2):
                        dve.tensor_copy(cnt[:, k, :], cnt_ps[k][:, 0:NODE_TILES])
                    dve.drain().then_inc(cnt_done, 1)
                    dve.wait_ge(w_in, W_LOADS)
                    for i in range(4):
                        w = (w1, w1, w2, w2)[i]
                        for k in range(KD):
                            dve.tensor_tensor(prod[:, i, k, :], w[:, k, :], av[:, i, :], ALU.mult)
                    dve.drain()
                    dve.tensor_reduce(wa[:, :, :, :].rearrange("p i k h -> p (i k h)"),
                                      prod[:, :, :, :].rearrange("p i k (h d) -> p (i k h) d", h=HEADS), AX.X, ALU.add)
                    dve.wait_ge(cum_ps, 1)
                    for k in range(2):
                        dve.tensor_copy(tot[:, k, :], tot_ps[k][:, 0:NODE_TILES])
                    dve.drain()
                    for k in range(2):
                        dve.tensor_tensor_scan(cum[:, k, :], onesr[:, :], tot[:, k, :], 0.0, ALU.mult, ALU.add)
                    dve.drain()
                    dve.tensor_tensor(cum[:, :, :], cum[:, :, :], tot[:, :, :], ALU.subtract)
                    dve.tensor_scalar(has[:, :, :], cnt[:, :, :], 0.5, None, ALU.is_gt)
                    dve.drain()
                    for k in range(2):
                        dve.tensor_tensor(first[:, k, :], cum[:, k, :], pre_ps[k][:, 0:NODE_TILES], ALU.add)
                    dve.drain().then_inc(first_done, 1)
                    dve.scalar_tensor_tensor(tot[:, :, :], first[:, :, :], float(-1 - NO_ROW), cnt[:, :, :], ALU.add, ALU.add)
                    dve.drain()
                    dve.tensor_tensor(tot[:, :, :], tot[:, :, :], has[:, :, :], ALU.mult)
                    dve.drain()
                    dve.tensor_scalar(end_d[:, :], tot[:, 0, :], float(NO_ROW), None, ALU.add)
                    dve.tensor_scalar(end_s[:, :], tot[:, 1, :], float(NO_ROW), None, ALU.add)
                    dve.drain().then_inc(table_up, 1)

                @block.tensor
                def _(pe):
                    for slot in range(UN_SORT):
                        pe.wait_ge(onehot, slot + 1)
                        for k in range(2):
                            mm = pe.matmul(cnt_ps[k][:, 0:NODE_TILES], ohL[:, slot, k, :], ohH[:, slot, k, :],
                                           start=(slot == 0), stop=False, skip_group_check=True)
                        mm.then_inc(slot_free, 1)
                    with pe.Fori(1, TILES // UN_SORT) as i:
                        for slot in range(UN_SORT):
                            pe.wait_ge(onehot, UN_SORT * i + slot + 1)
                            for k in range(2):
                                mm = pe.matmul(cnt_ps[k][:, 0:NODE_TILES], ohL[:, slot, k, :], ohH[:, slot, k, :],
                                               start=False, stop=False, skip_group_check=True)
                            mm.then_inc(slot_free, 1)
                    pe.drain().then_inc(counted, 1)
                    pe.wait_ge(cnt_done, 1)
                    for k in range(2):
                        pe.matmul(pre_ps[k][:, 0:NODE_TILES], tri[:, :], cnt[:, k, :], start=True, stop=True)
                        mm = pe.matmul(tot_ps[k][:, 0:NODE_TILES], ones[:, :], cnt[:, k, :], start=True, stop=True)
                    mm.then_inc(cum_ps, 1)
                    pe.wait_ge(first_done, 1)
                    for k in range(2):
                        pe.matmul(cnt_ps[k][:, 0:NODE_TILES], ident[:, :], first[:, k, :], start=True, stop=False,
                                  skip_group_check=True)

                @block.gpsimd
                def _(pool):
                    pool.wait_ge(w_in, W_LOADS)
                    for name, (w_hi, w_lo) in (("mw1", mw1), ("mw2", mw2), ("uw1", uw1), ("uw2", uw2)):
                        pool.tensor_copy(w_hi[:, :, :], w_full[name][:, :, :])
                        pool.drain()
                        pool.tensor_tensor(w_lo[:, :, :], w_full[name][:, :, :], w_hi[:, :, :].bitcast(F32), ALU.subtract)
                    pool.tensor_copy(mw1e[:, :], mw1e_full[:, :])
                    pool.drain()
                    lo_rows = slice(ATT_HI2, ATT_HI2 + 32)
                    pool.tensor_tensor(mw1e[lo_rows, :], mw1e_full[lo_rows, :], mw1e[lo_rows, :].bitcast(F32), ALU.subtract)

                @block.sync
                def _(sp):
                    sp.dma_start(w1[:, :, :], W1.rearrange("(k p) n -> p k n", p=P)).then_inc(w_in, 16)
                    sp.dma_start(w2[:, :, :], W2.rearrange("(k p) n -> p k n", p=P)).then_inc(w_in, 16)
                    for i, a in enumerate((al1, ar1, al2, ar2)):
                        sp.dma_start(av[:, i, :], a.rearrange("h d -> (h d)").partition_broadcast(P)).then_inc(w_in, 16)
                    for part in (ATT_HI, ATT_LO, ATT_HI2):
                        sp.dma_start(mw1e_full[part:part + D_EDGE, :], mW1[2 * D:2 * D + D_EDGE, :]).then_inc(w_in, 16)
                    for part in (ATT_HI, ATT_HI2):
                        sp.dma_start(mw1e_full[part + D_EDGE:part + D_EDGE + 1, :], mb1.unsqueeze(0)).then_inc(w_in, 16)
                    sp.dma_start(w_full["mw1"][:, :, :], mW1[0:2 * D, :].rearrange("(k p) n -> p k n", p=P)).then_inc(w_in, 16)
                    sp.dma_start(w_full["mw2"][:, :, :], mW2.rearrange("(k p) n -> p k n", p=P)).then_inc(w_in, 16)
                    sp.dma_start(w_full["uw1"][:, :, :], uW1.rearrange("(k p) n -> p k n", p=P)).then_inc(w_in, 16)
                    sp.dma_start(w_full["uw2"][:, :, :], uW2.rearrange("(k p) n -> p k n", p=P)).then_inc(w_in, 16)
                    with nc.allow_non_contiguous_dma(reason="bias columns, once"):
                        sp.dma_start(mb2c[:, :], mb2.rearrange("(k p) -> p k", p=P)).then_inc(w_in, 16)
                    sp.dma_start(ub1r[:, :], ub1.partition_broadcast(P)).then_inc(w_in, 16)
                    sp.dma_start(ub2r[:, :], ub2.partition_broadcast(P)).then_inc(w_in, 16)
                    sp.wait_ge(table_up, 1)
                    sp.dma_start(end_of.rearrange("(p n) o -> p (n o)", p=P), end_d[:, :]).then_inc(table_up, 16)
                    sp.wait_ge(table_up, 17)
                    sp.wait_ge(z_out, 64)

            snap = sb0("snap", [P, 2, 2, NODE_TILES])
            diag = sb0("diag", [P, 2, 2, P])
            lT = sb0("lT", [P, 2, 2, P])
            bw = sb0("bw", [P, 2, 2, 2])
            place = sb0("place", [P, UN_SORT, 2], I32)
            row = sb0("row", [P, UN_SORT, ROW], I32)
            junk = sb0("junk", [P, 2, NODE_TILES])
            junk2 = sb0("junk2", [P, 2, P])
            pick_ps = [tot_ps, [c0.enter_context(nc.psum_tensor(f"pick_ps{k}", [P, 512], F32)) for k in range(2)]]
            keyrow_ps = [p[:, 0:2 * P].rearrange("p (k n) -> p k n", k=2) for p in pre_ps]
            lT_ps = [p[:, 2 * P:3 * P].bitcast(F16) for p in pre_ps]
            onehot2, snap_made, diag_made, lT_made, lT_copied, advanced, picked, tile_read, placed = (sem(n) for n in (
                "p2_onehot_made", "p2_snap_made", "p2_diag_made", "p2_lT_made", "p2_lT_copied", "p2_advanced", "p2_picked", "p2_tile_read",
                "p2_placed"))
            row_out = [sem(f"p2_row_out{s}") for s in range(UN_SORT)]
            with nc.Block() as block:
                @block.vector
                def _(dve):
                    def tile_onehots(t, s, i):
                        if reached(t, UN_SORT):
                            dve.wait_ge(picked, t - UN_SORT + 1)
                        make_onehots(dve, t, s).then_inc(onehot2, 1)

                    def counts(t, s, i):
                        dve.wait_ge(picked, t + 1)
                        for k in range(2):
                            dve.scalar_tensor_tensor(junk[:, k, :], pick_ps[s % 2][k][:, 0:NODE_TILES], 1.0,
                                                     ohH[:, s, k, :], ALU.mult, ALU.mult, accum_out=bw[:, s % 2, 0, k:k + 1])
                        for k in range(2):
                            last = dve.scalar_tensor_tensor(junk2[:, k, :], keyrow_ps[s % 2][:, k, :], keyf[:, k, bass.ds(t, 1)],
                                                            trilow[:, :], ALU.is_equal, ALU.mult, accum_out=bw[:, s % 2, 1, k:k + 1])
                        last.then_inc(tile_read, 1)

                    def places(t, s, i):
                        if reached(i, 1):
                            dve.wait_ge(row_out[s], 32 * i)
                        dve.tensor_copy(row[:, s, :], pay[:, bass.ds(t, 1), :].rearrange("p o w -> p (o w)"))
                        dve.scalar_tensor_tensor(place[:, s, :], bw[:, s % 2, 0, :], 1.0, bw[:, s % 2, 1, :], ALU.add, ALU.add).then_inc(placed, 1)

                    def drain():
                        dve.drain()

                    dve.wait_ge(a_in, 16)
                    pipelined(dve, [(places, 3), (tile_onehots, 0), (counts, 2), (drain, None)], TILES, UN_SORT)

                @block.gpsimd
                def _(pool):
                    def write_rows(t, s, i):
                        pool.wait_ge(placed, t + 1)
                        pool.sem_inc(apart, 1)
                        for table, words, k in ((by_dst, 2, 0), (by_src, ROW, 1)):
                            pool.indirect_dma_start(
                                out=table, out_offset=bass.IndirectOffsetOnAxis(ap=place[:, s, k:k + 1], axis=0),
                                in_=row[:, s, 0:words], in_offset=None).then_inc(row_out[s], 16)

                    pipelined(pool, [(write_rows, 0)], TILES, UN_SORT)
                    for s in range(UN_SORT):
                        pool.wait_ge(row_out[s], 32 * (TILES // UN_SORT))

                @block.tensor
                def _(pe):
                    def turn(t, s, i):
                        pe.wait_ge(onehot2, t + 1)
                        if reached(t, 2):
                            pe.wait_ge(tile_read, t - 1)
                        for k in range(2):
                            mm = pe.transpose(lT_ps[s % 2][:, k * P:(k + 1) * P], ohL[:, s, k, :], ident16[:, :])
                        mm.then_inc(lT_made, 1)

                    def advance(t, s, i):
                        pe.wait_ge(snap_made, t + 1)
                        for k in range(2):
                            mm = pe.matmul(cnt_ps[k][:, 0:NODE_TILES], ohL[:, s, k, :], ohH[:, s, k, :],
                                           start=False, stop=False, skip_group_check=True)
                        mm.then_inc(advanced, 1)

                    def pick(t, s, i):
                        s2 = s % 2
                        pe.wait_ge(lT_copied, t + 1)
                        for k in range(2):
                            pe.matmul(pick_ps[s2][k][:, 0:NODE_TILES], lT[:, s2, k, :], snap[:, s2, k, :], start=True, stop=True)
                        pe.wait_ge(diag_made, t + 1)
                        for k in range(2):
                            mm = pe.matmul(keyrow_ps[s2][:, k, :], ones[:, :], diag[:, s2, k, :], start=True, stop=True)
                        mm.then_inc(picked, 1)

                    pipelined(pe, [(advance, 1), (pick, 1), (turn, 0)], TILES, UN_SORT)

                @block.scalar
                def _(act):
                    def tile(t, s, i):
                        s = s % 2
                        if reached(t, 2):
                            act.wait_ge(picked, t - 1)
                        for k in range(2):
                            last = act.activation(diag[:, s, k, :], ident[:, :], ACT.Copy, scale=keyf[:, k, bass.ds(t, 1)])
                        last.then_inc(diag_made, 1)
                        if reached(t, 1):
                            act.wait_ge(advanced, t)
                        for k in range(2):
                            last = act.activation(snap[:, s, k, :], cnt_ps[k][:, 0:NODE_TILES], ACT.Copy)
                        last.then_inc(snap_made, 1)
                        act.wait_ge(lT_made, t + 1)
                        act.activation(lT[:, s, :, :].rearrange("p k n -> p (k n)"), lT_ps[s], ACT.Copy).then_inc(lT_copied, 1)

                    pipelined(act, [(tile, 0)], TILES, UN_SORT)

        def gat(layer, neg):
            nm = f"g{layer}_"
            first_layer = layer == 1
            w = w1 if first_layer else w2
            wal, war = (wa[:, 2 * (layer - 1), :, :], wa[:, 2 * layer - 1, :, :])
            n_in = 2 if first_layer else 3
            SLOTS = UN if first_layer else 2 * UN
            TURN = 6 if first_layer else 3
            with ExitStack() as c:
                def t(name, shape, dt=F32):
                    return c.enter_context(nc.sbuf_tensor(nm + name, shape, dt))

                def ps(name, dt=F32):
                    return c.enter_context(nc.psum_tensor(nm + name, [P, 512], dt))

                def sm(name):
                    return phase_sem(nm + name)

                rows = t("rows", [P, SLOTS, GT, 2], I32)
                keys = t("keys", [HEADS, SLOTS, G + 1, 2], I32) if first_layer else None
                parts = t("parts", [P, SLOTS, GT, 2, 2], I32)
                flat = t("flat", [P, SLOTS, GT, 2], I32)
                found = t("found", [P, SLOTS, GT, 2], I32)
                idx = t("idx", [P, SLOTS, GT, 3], I32)
                same = t("same", [HEADS, 2, G])
                xin = t("xin", [P, SLOTS, GT, n_in, D])
                xn = t("xn", [P, 2, GT, 2, D]) if first_layer else None
                st = t("st", [P, 2 * GT, 6])
                mv = t("mv", [P, 2, 2 * GT, 2])
                sd = t("sd", [P, 2 * GT])
                rstd = t("rstd", [P, 2 * GT])
                nmr = t("nmr", [P, 2 * GT])
                hT = t("hT", [P, 2, KD, G])
                raw = t("raw", [HEADS, 2, G])
                score = t("score", [HEADS, G])
                top = t("top", [HEADS, 2, G + 1])
                dd = t("dd", [HEADS, 2, G])
                ew = t("ew", [HEADS, UN, 2, G])
                den = t("den", [HEADS, 2, G])
                feat = t("feat", [P, UN, KD, G])
                val = t("val", [P, KD, G])
                acc = t("acc", [P, 2, KD, G])
                rden = t("rden", [P, GT * HEADS])
                r = t("r", [P, 2, GT, D])
                exp_r = t("exp_r", [P, GT, D])
                res = t("res", [P, SLOTS, GT, D])
                hT_ps = [ps(f"hT_ps{q}") for q in range(2)]
                F_ps = ps("F_ps")
                S_ps = ps("S_ps")
                B_ps = [ps(f"B_ps{b}") for b in range(2)]
                O_ps = ps("O_ps")
                DT_ps = ps("DT_ps")
                DT = DT_ps[:, 0:GT * HEADS]

                rows_in, keys_in, x_in, found_in, stored = ([sm(f"{n}{s}") for s in range(SLOTS)] for n in (
                    "rows_in", "keys_in", "x_in", "found_in", "stored"))
                (idx_made, stats_made, root_made, scale_made, normed, turned, hT_made, f_summed, feat_made, scored, score_read,
                 same_made, neg_made, dd_made, ew_made, spread, scanned, out_turned, out_read, r_made, exp_made, res_made) = (
                     sm(n) for n in (
                         "idx_made", "stats_made", "root_made", "scale_made", "normed", "turned", "hT_made", "f_summed",
                         "feat_made", "scored", "score_read", "same_made", "neg_made", "dd_made", "ew_made", "spread",
                         "scanned", "out_turned", "out_read", "r_made", "exp_made", "res_made"))
                target = H1 if first_layer else X1

                with nc.Block() as block:
                    @block.sync
                    def _(sp):
                        def load_rows(g, s, i):
                            if reached(g, SLOTS):
                                sp.wait_ge(idx_made, g - SLOTS + 1)
                            sp.dma_start(rows[:, s, :, :], by_dst[bass.ds(g * G + 1, G), :].rearrange("(j p) w -> p j w", p=P)).then_inc(rows_in[s], 16)

                        def load_keys(g, s, i):
                            if reached(g, SLOTS):
                                sp.wait_ge(same_made, g - SLOTS + 1)
                            sp.dma_start(keys[:, s, :, :].rearrange("h e w -> h (e w)"),
                                         by_dst[bass.ds(g * G, G + 1), :].rearrange("e w -> (e w)").partition_broadcast(HEADS)).then_inc(keys_in[s], 16)

                        def store(g, s, i):
                            sp.wait_ge(res_made, g + 1)
                            sp.dma_start(target[bass.ds(g * G, G), :].rearrange("(j p) d -> p j d", p=P), res[:, s, :, :]).then_inc(stored[s], 16)

                        if first_layer:
                            pipelined(sp, [(load_rows, 0), (load_keys, TURN - 2), (store, TURN + 7)], GROUPS, SLOTS)
                        else:
                            pipelined(sp, [(store, TURN + 7)], GROUPS, SLOTS)
                        for s in range(SLOTS):
                            sp.wait_ge(stored[s], 16 * len(range(s, GROUPS, SLOTS)))

                    @block.gpsimd
                    def _(pool):
                        def gathers(g, s, i):
                            pool.wait_ge(idx_made, g + 1)
                            pool.sem_inc(apart, 1)
                            if reached(g, SLOTS):
                                pool.wait_ge(normed if first_layer else res_made, g - SLOTS + 1)
                                pool.sem_inc(apart, 1)
                            for j in range(GT):
                                for q in range(n_in):
                                    source = x if first_layer or q == 2 else H1
                                    pool.indirect_dma_start(
                                        out=xin[:, s, j, q, :], out_offset=None, in_=source,
                                        in_offset=bass.IndirectOffsetOnAxis(ap=idx[:, s, j, q:q + 1], axis=0)).then_inc(x_in[s], 16)
                            if first_layer:
                                for j in range(GT):
                                    for q in range(2):
                                        pool.indirect_dma_start(
                                            out=found[:, s, j, q:q + 1], out_offset=None, in_=end_of,
                                            in_offset=bass.IndirectOffsetOnAxis(ap=flat[:, s, j, q:q + 1], axis=0)).then_inc(found_in[s], 16)

                        pipelined(pool, [(gathers, 0)], GROUPS, SLOTS)

                    @block.vector
                    def _(dve):
                        def prepare(g, s, i):
                            if reached(i, 1):
                                dve.wait_ge(x_in[s], 16 * GT * n_in * i)
                            if first_layer:
                                dve.wait_ge(rows_in[s], 16 * (i + 1))
                                if reached(i, 1):
                                    dve.wait_ge(found_in[s], 16 * GT * 2 * i)
                                dve.tensor_scalar(idx[:, s, :, 0:2], rows[:, s, :, :], float(N_NODES - 1), None, ALU.min)
                                dve.tensor_scalar(parts[:, s, :, :, 0], rows[:, s, :, :], 7, None, ALU.arith_shift_right)
                                dve.tensor_scalar(parts[:, s, :, :, 1], rows[:, s, :, :], P - 1, None, ALU.bitwise_and)
                            else:
                                dve.tensor_copy(idx[:, s, :, :], ends[:, bass.ds(g * GT, GT), :]).then_inc(idx_made, 1)

                        def join_parts(g, s, i):
                            dve.scalar_tensor_tensor(flat[:, s, :, :], parts[:, s, :, :, 1], float(NODE_TILES),
                                                     parts[:, s, :, :, 0], ALU.mult, ALU.add).then_inc(idx_made, 1)

                        def keep(g, s, i):
                            dve.wait_ge(found_in[s], 16 * GT * 2 * (i + 1))
                            dve.tensor_copy(ends[:, bass.ds(g * GT, GT), 0:2], found[:, s, :, :])
                            dve.tensor_copy(ends[:, bass.ds(g * GT, GT), 2:3], idx[:, s, :, 1:2])

                        def stats(g, s, i):
                            dve.wait_ge(x_in[s], 16 * GT * n_in * (i + 1))
                            for j in range(GT):
                                for q in range(2):
                                    dve.bn_stats(st[:, 2 * j + q, :], xin[:, s, j, q, :])

                        def join_stats(g, s, i):
                            for a in range(2 * GT):
                                last = dve.bn_aggr(mv[:, s % 2, a, :], st[:, a, :])
                            last.then_inc(stats_made, 1)

                        def invert_root(g, s, i):
                            dve.wait_ge(root_made, g + 1)
                            if reached(g, 1):
                                dve.wait_ge(normed, g)
                            dve.reciprocal(rstd[:, :], sd[:, :])

                        def shift(g, s, i):
                            dve.scalar_tensor_tensor(nmr[:, :], mv[:, s % 2, :, 0], -1.0, rstd[:, :], ALU.mult, ALU.mult).then_inc(scale_made, 1)

                        def compare_keys(g, s, i):
                            dve.wait_ge(keys_in[s], 16 * (i + 1))
                            if reached(g, 2):
                                dve.wait_ge(neg_made, g - 1)
                            dve.tensor_tensor(same[:, s % 2, :], keys[:, s, 1:G + 1, 1], keys[:, s, 0:G, 1], ALU.is_equal).then_inc(same_made, 1)

                        def leak(g, s, i):
                            s2 = s % 2
                            dve.wait_ge(score_read, g + 1)
                            dve.scalar_tensor_tensor(score[:, :], raw[:, s2, :], NEG_SLOPE, raw[:, s2, :], ALU.mult, ALU.max)
                            dve.tensor_copy(top[:, s2, 0:1], top[:, 1 - s2, G:G + 1])

                        def scan_top(g, s, i):
                            s2 = s % 2
                            if first_layer:
                                dve.wait_ge(neg_made, g + 1)
                            dve.tensor_tensor_scan(top[:, s2, 1:G + 1], neg[:, bass.ds(g * G, G)], score[:, :], top[:, s2, 0:1], ALU.add, ALU.max)

                        def differences(g, s, i):
                            s2 = s % 2
                            if reached(g, 1):
                                dve.wait_ge(ew_made, g)
                            dve.tensor_tensor(dd[:, 0, :], top[:, s2, 0:G], top[:, s2, 1:G + 1], ALU.subtract)
                            dve.tensor_tensor(dd[:, 1, :], score[:, :], top[:, s2, 1:G + 1], ALU.subtract)

                        def cut_segments(g, s, i):
                            dve.tensor_tensor(dd[:, 0, :], dd[:, 0, :], neg[:, bass.ds(g * G, G)], ALU.min).then_inc(dd_made, 1)

                        def weigh_features(g, s, i):
                            s2 = s % 2
                            dve.wait_ge(ew_made, g + 1)
                            if reached(g, 2):
                                dve.wait_ge(out_turned, g - 1)
                            dve.tensor_tensor_scan(den[:, s2, :], ew[:, s % UN, 0, :], ew[:, s % UN, 1, :], den[:, 1 - s2, G - 1:G], ALU.mult, ALU.add)
                            dve.wait_ge(spread, g + 1)
                            dve.wait_ge(feat_made, g + 1)
                            for b in range(KD):
                                dve.tensor_tensor(val[:, b, :], feat[:, s % UN, b, :], B_ps[b][:, G:2 * G], ALU.mult)

                        def scan_sums(g, s, i):
                            s2 = s % 2
                            for b in range(KD):
                                last = dve.tensor_tensor_scan(acc[:, s2, b, :], B_ps[b][:, 0:G], val[:, b, :],
                                                              acc[:, 1 - s2, b, G - 1:G], ALU.mult, ALU.add)
                            last.then_inc(scanned, 1)

                        def invert_den(g, s, i):
                            dve.wait_ge(out_turned, g + 1)
                            dve.reciprocal(rden[:, :], DT)

                        def divide(g, s, i):
                            last = dve.tensor_tensor(r[:, s % 2, :, :].rearrange("p j (h d) -> p (j h) d", h=HEADS),
                                                     O_ps[:, :].rearrange("p (a d) -> p a d", d=D_HEAD),
                                                     rden[:, :].unsqueeze(2).to_broadcast([P, GT * HEADS, D_HEAD]), ALU.mult).then_inc(out_read, 1)

                        def add_residual(g, s, i):
                            dve.tensor_tensor(r[:, s % 2, :, :], r[:, s % 2, :, :], xin[:, s, :, 1, :], ALU.add).then_inc(r_made, 1)

                        def elu(g, s, i):
                            dve.wait_ge(exp_made, g + 1)
                            if reached(i, 1):
                                dve.wait_ge(stored[s], 16 * i)
                            ins = dve.scalar_tensor_tensor(res[:, s, :, :], exp_r[:, :, :], -1.0, r[:, s % 2, :, :], ALU.add, ALU.max)
                            if first_layer:
                                ins.then_inc(res_made, 1)

                        def add_x(g, s, i):
                            dve.tensor_tensor(res[:, s, :, :], res[:, s, :, :], xin[:, s, :, 2, :], ALU.add).then_inc(res_made, 1)

                        def drain():
                            dve.drain()

                        dve.memset(top[:, :, :], 0.0)
                        dve.memset(den[:, :, :], 0.0)
                        dve.memset(acc[:, :, :, :], 0.0)
                        dve.drain()
                        if first_layer:
                            pipelined(dve, [
                                (weigh_features, TURN + 4), (keep, 3), (drain, None),
                                (scan_sums, TURN + 4), (invert_den, TURN + 5), (leak, TURN + 2), (drain, None),
                                (scan_top, TURN + 2), (divide, TURN + 5), (prepare, 0), (compare_keys, TURN + 1), (drain, None),
                                (differences, TURN + 2), (stats, 3), (invert_root, 4), (join_parts, 0), (drain, None),
                                (cut_segments, TURN + 2), (join_stats, 3), (shift, 4), (elu, TURN + 6)], GROUPS, SLOTS)
                        else:
                            pipelined(dve, [
                                (weigh_features, TURN + 4), (drain, None),
                                (scan_sums, TURN + 4), (invert_den, TURN + 5), (leak, TURN + 2), (drain, None),
                                (scan_top, TURN + 2), (elu, TURN + 6), (divide, TURN + 5), (drain, None),
                                (differences, TURN + 2), (add_x, TURN + 6), (add_residual, TURN + 5), (prepare, 0), (drain, None),
                                (cut_segments, TURN + 2)], GROUPS, SLOTS)

                    @block.scalar
                    def _(act):
                        def root(g, s, i):
                            act.wait_ge(stats_made, g + 1)
                            act.activation(sd[:, :], mv[:, s % 2, :, 1], ACT.Sqrt, bias=eps[:, :]).then_inc(root_made, 1)

                        def apply(g, s, i):
                            act.wait_ge(scale_made, g + 1)
                            if reached(g, 2):
                                act.wait_ge(turned, g - 1)
                            for j in range(GT):
                                for q in range(2):
                                    a = 2 * j + q
                                    last = act.activation(xn[:, s % 2, j, q, :], xin[:, s, j, q, :], ACT.Identity,
                                                          scale=rstd[:, a:a + 1], bias=nmr[:, a:a + 1])
                            last.then_inc(normed, 1)

                        def evac_h(g, s, i):
                            act.wait_ge(turned, g + 1)
                            for q in range(2):
                                last = act.activation(hT[:, q, :, :].rearrange("p k e -> p (k e)"), hT_ps[q][:, :],
                                                      ACT.Relu if first_layer else ACT.Copy)
                            last.then_inc(hT_made, 1)

                        def evac_f(g, s, i):
                            act.wait_ge(f_summed, g + 1)
                            if reached(g, UN):
                                act.wait_ge(scanned, g - UN + 1)
                            act.activation(feat[:, s % UN, :, :].rearrange("p k e -> p (k e)"), F_ps[:, :], ACT.Copy).then_inc(feat_made, 1)

                        def evac_score(g, s, i):
                            act.wait_ge(scored, g + 1)
                            if reached(g, 2):
                                act.wait_ge(dd_made, g - 1)
                            act.activation(raw[:, s % 2, :], S_ps[0:HEADS, 0:G], ACT.Copy).then_inc(score_read, 1)

                        def cuts(g, s, i):
                            act.wait_ge(same_made, g + 1)
                            act.activation(neg[:, bass.ds(g * G, G)], same[:, s % 2, :], ACT.Copy, scale=FAR, bias=-FAR).then_inc(neg_made, 1)

                        def weights(g, s, i):
                            act.wait_ge(dd_made, g + 1)
                            if reached(g, UN):
                                act.wait_ge(scanned, g - UN + 1)
                            act.activation(ew[:, s % UN, :, :], dd[:, :, :], ACT.Exp).then_inc(ew_made, 1)

                        def exp_of_r(g, s, i):
                            act.wait_ge(out_read if first_layer else r_made, g + 1)
                            if reached(g, 1):
                                act.wait_ge(res_made, g)
                            act.activation(exp_r[:, :, :], r[:, s % 2, :, :], ACT.Relu, scale=-1.0)
                            act.drain()
                            act.activation(exp_r[:, :, :], exp_r[:, :, :], ACT.Exp, scale=-1.0).then_inc(exp_made, 1)

                        if first_layer:
                            pipelined(act, [(weights, TURN + 3), (exp_of_r, TURN + 6), (root, 4), (apply, 5), (evac_f, TURN + 1),
                                            (evac_score, TURN + 1), (evac_h, TURN), (cuts, TURN + 1)], GROUPS, SLOTS)
                        else:
                            pipelined(act, [(weights, TURN + 3), (exp_of_r, TURN + 6), (evac_f, TURN + 1),
                                            (evac_score, TURN + 1), (evac_h, TURN)], GROUPS, SLOTS)

                    @block.tensor
                    def _(pe):
                        def turn(g, s, i):
                            if first_layer:
                                pe.wait_ge(normed, g + 1)
                            else:
                                pe.wait_ge(x_in[s], 16 * GT * n_in * (i + 1))
                            rows_of = xn[:, s % 2, :, :, :] if first_layer else xin[:, s, :, :, :]
                            for q in range(2):
                                for j in range(GT):
                                    for k in range(KD):
                                        mm = pe.transpose(hT_ps[q][:, k * G + j * P:k * G + (j + 1) * P],
                                                          rows_of[:, j, q, k * P:(k + 1) * P], ident[:, :])
                            mm.then_inc(turned, 1)

                        def products(g, s, i):
                            pe.wait_ge(hT_made, g + 1)
                            if reached(g, 1):
                                pe.wait_ge(feat_made, g)
                            for m in range(KD):
                                for k in range(KD):
                                    mm = pe.matmul(F_ps[:, m * G:(m + 1) * G], w[:, k, m * P:(m + 1) * P], hT[:, 0, k, :],
                                                   start=(k == 0), stop=(k == KD - 1))
                            mm.then_inc(f_summed, 1)
                            if reached(g, 1):
                                pe.wait_ge(score_read, g)
                            for q in range(2):
                                for k in range(KD):
                                    mm = pe.matmul(S_ps[0:HEADS, 0:G], (wal, war)[q][:, k, :], hT[:, q, k, :],
                                                   start=(q == 0 and k == 0), stop=(q == 1 and k == KD - 1))
                            mm.then_inc(scored, 1)

                        def spread_weights(g, s, i):
                            pe.wait_ge(ew_made, g + 1)
                            if reached(g, 1):
                                pe.wait_ge(scanned, g)
                            for b in range(KD):
                                mm = pe.matmul(B_ps[b][:, :], headsel[:, b, :], ew[:, s % UN, :, :].rearrange("h q e -> h (q e)"),
                                               start=True, stop=True)
                            mm.then_inc(spread, 1)

                        def turn_back(g, s, i):
                            pe.wait_ge(scanned, g + 1)
                            if reached(g, 1):
                                pe.wait_ge(out_read, g)
                            for j in range(GT):
                                for b in range(KD):
                                    pe.transpose(O_ps[:, j * D + b * P:j * D + (b + 1) * P],
                                                 acc[:, s % 2, b, j * P:(j + 1) * P], ident[:, :])
                                mm = pe.transpose(DT[:, j * HEADS:(j + 1) * HEADS], den[:, s % 2, j * P:(j + 1) * P], ident[0:HEADS, 0:HEADS])
                            mm.then_inc(out_turned, 1)

                        pipelined(pe, [(products, TURN + 1), (turn, TURN), (spread_weights, TURN + 3), (turn_back, TURN + 4)], GROUPS, SLOTS)

        with nc.sbuf_tensor("neg", [HEADS, EDGES], BF16) as neg:
            gat(1, neg)
            end_phase()
            gat(2, neg)
            end_phase()

        with ExitStack() as c:
            def t(name, shape, dt=F32):
                return c.enter_context(nc.sbuf_tensor("m_" + name, shape, dt))

            def ps(name):
                return c.enter_context(nc.psum_tensor("m_" + name, [P, 512], F32))

            def sm(name):
                return phase_sem("m_" + name)

            rows = t("rows", [P, UN, GT, ROW], I32)
            keys = t("keys", [1, UN, G + 1], I32)
            ones_r = t("ones_r", [1, P], F32R)
            parts = t("parts", [P, UN, GT, 2, 2], I32)
            flat = t("flat", [P, UN, GT, 2], I32)
            found = t("found", [P, UN, GT, 2], I32)
            idx = t("idx", [P, UN, GT], I32)
            att = t("att", [P, 2, GT, P], F32R)
            attT = t("attT", [P, G], F32R)
            same = t("same", [1, UN, G], F32R)
            xin = t("xin", [P, UN, GT, 2, D])
            xn = t("xn", [P, 2, GT, 2, D])
            st = t("st", [P, 2 * GT, 6])
            mv = t("mv", [P, 2 * GT, 2])
            sd = t("sd", [P, 2 * GT])
            rstd = t("rstd", [P, 2 * GT])
            nmr = t("nmr", [P, 2 * GT])
            hT = [t(f"hT_{part}", [P, 2, KD, G], F32R) for part in ("hi", "lo")]
            hid = [t(f"hid_{part}", [P, KH, G], F32R) for part in ("hi", "lo")]
            aggs = [t(f"aggs_{part}", [P, 2, KD, G], F32R) for part in ("hi", "lo")]
            msg = t("msg", [P, KD, G])
            agg = t("agg", [P, 2, KD, G])
            gs = t("gs", [P, 2, GT, HIDDEN])
            hT_ps = [ps(f"hT_ps{q}") for q in range(2)]
            misc_ps = ps("misc_ps")
            hid_ps = [ps(f"hid_ps{b}") for b in range(2)]
            msg_ps = ps("msg_ps")
            gs_ps = [ps(f"gs_ps{j}") for j in range(GT)]
            rows_in, found_in, x_in, x1_in, stored = ([sm(f"{n}{s}") for s in range(UN)] for n in (
                "rows_in", "found_in", "x_in", "x1_in", "stored"))
            (idx_made, stats_made, root_made, normed, turned, hT_made, attT_made, hid_summed, hid_made, msg_summed, msg_made,
             spread, scanned, gs_summed, gs_made, hT_hi_made, hid_hi_made, agg_hi_made, agg_lo_made, att_made,
             scale_made, flagged) = (
                 sm(n) for n in (
                     "idx_made", "stats_made", "root_made", "normed", "turned", "hT_made", "attT_made", "hid_summed", "hid_made",
                     "msg_summed", "msg_made", "spread", "scanned", "gs_summed", "gs_made", "hT_hi_made", "hid_hi_made",
                     "agg_hi_made", "agg_lo_made", "att_made", "scale_made", "flagged"))
            with nc.Block() as block:
                @block.sync
                def _(sp):
                    def load(g, s, i):
                        if reached(g, UN):
                            sp.wait_ge(att_made, g - UN + 1)
                            sp.wait_ge(flagged, g - UN + 1)
                        sp.dma_start(rows[:, s, :, :], by_src[bass.ds(g * G + 1, G), :].rearrange("(j p) w -> p j w", p=P)).then_inc(rows_in[s], 16)
                        with nc.allow_non_contiguous_dma(reason="the sources alone, of rows"):
                            sp.dma_start(keys[:, s, :], by_src[bass.ds(g * G, G + 1), 0:1].rearrange("e o -> o e")).then_inc(rows_in[s], 16)

                    def store(g, s, i):
                        sp.wait_ge(gs_made, g + 1)
                        sp.dma_start(GS[bass.ds(g * G, G), :].rearrange("(j p) d -> p j d", p=P), gs[:, s % 2, :, :]).then_inc(stored[s], 16)

                    pipelined(sp, [(load, 0), (store, 9)], GROUPS)
                    for s in range(UN):
                        sp.wait_ge(stored[s], 16 * len(range(s, GROUPS, UN)))

                @block.gpsimd
                def _(pool):
                    def first_gathers(g, s, i):
                        pool.wait_ge(idx_made, g + 1)
                        pool.sem_inc(apart, 1)
                        if reached(g, UN):
                            pool.wait_ge(normed, g - UN + 1)
                            pool.sem_inc(apart, 1)
                        for j in range(GT):
                            for q in range(2):
                                pool.indirect_dma_start(
                                    out=found[:, s, j, q:q + 1], out_offset=None, in_=end_of,
                                    in_offset=bass.IndirectOffsetOnAxis(ap=flat[:, s, j, q:q + 1], axis=0)).then_inc(found_in[s], 16)
                        for j in range(GT):
                            pool.indirect_dma_start(
                                out=xin[:, s, j, 0, :], out_offset=None, in_=x,
                                in_offset=bass.IndirectOffsetOnAxis(ap=idx[:, s, j:j + 1], axis=0)).then_inc(x_in[s], 16)

                    def second_gathers(g, s, i):
                        pool.wait_ge(found_in[s], 16 * GT * 2 * (i + 1))
                        pool.sem_inc(apart, 1)
                        for j in range(GT):
                            pool.indirect_dma_start(
                                out=xin[:, s, j, 1, :], out_offset=None, in_=X1,
                                in_offset=bass.IndirectOffsetOnAxis(ap=found[:, s, j, 1:2], axis=0)).then_inc(x1_in[s], 16)
                        pool.wait_ge(x_in[s], 16 * GT * (i + 1))
                        pool.sem_inc(apart, 1)
                        for j in range(GT):
                            pool.indirect_dma_start(
                                out=xin[:, s, j, 0, :], out_offset=None, in_=X1,
                                in_offset=bass.IndirectOffsetOnAxis(ap=found[:, s, j, 0:1], axis=0),
                                bounds_check=NO_ROW - 1, oob_is_err=False).then_inc(x1_in[s], 16)

                    pipelined(pool, [(first_gathers, 0), (second_gathers, 1)], GROUPS)

                @block.vector
                def _(dve):
                    def prepare(g, s, i):
                        dve.wait_ge(rows_in[s], 32 * i + 32)
                        if reached(i, 1):
                            dve.wait_ge(x1_in[s], 32 * GT * i)
                        dve.tensor_scalar(idx[:, s, :], rows[:, s, :, 0], float(N_NODES - 1), None, ALU.min)
                        dve.tensor_scalar(parts[:, s, :, :, 0], rows[:, s, :, 0:2], 7, None, ALU.arith_shift_right)
                        dve.tensor_scalar(parts[:, s, :, :, 1], rows[:, s, :, 0:2], P - 1, None, ALU.bitwise_and)
                        dve.drain()
                        dve.scalar_tensor_tensor(flat[:, s, :, :], parts[:, s, :, :, 1], float(NODE_TILES),
                                                 parts[:, s, :, :, 0], ALU.mult, ALU.add).then_inc(idx_made, 1)

                    def stats(g, s, i):
                        dve.wait_ge(x1_in[s], 32 * GT * (i + 1))
                        for j in range(GT):
                            for q in range(2):
                                dve.bn_stats(st[:, 2 * j + q, :], xin[:, s, j, q, :])
                        dve.drain()
                        for a in range(2 * GT):
                            last = dve.bn_aggr(mv[:, a, :], st[:, a, :])
                        last.then_inc(stats_made, 1)

                    def scale(g, s, i):
                        dve.wait_ge(root_made, g + 1)
                        if reached(g, 1):
                            dve.wait_ge(normed, g)
                        dve.reciprocal(rstd[:, :], sd[:, :])
                        dve.drain()
                        dve.scalar_tensor_tensor(nmr[:, :], mv[:, :, 0], -1.0, rstd[:, :], ALU.mult, ALU.mult).then_inc(scale_made, 1)

                    def flags(g, s, i):
                        if reached(g, UN):
                            dve.wait_ge(spread, g - UN + 1)
                        dve.tensor_tensor(same[:, s, :], keys[:, s, 1:G + 1], keys[:, s, 0:G], ALU.is_equal).then_inc(flagged, 1)

                    def split_att(g, s, i):
                        s2 = s % 2
                        if reached(g, 2):
                            dve.wait_ge(turned, g - 1)
                        full = rows[:, s, :, 2:ROW].bitcast(F32)
                        dve.tensor_copy(att[:, s2, :, ATT_HI:ATT_HI + D_EDGE], full)
                        dve.tensor_copy(att[:, s2, :, ATT_HI2:ATT_HI2 + D_EDGE], full)
                        dve.drain()
                        dve.tensor_tensor(att[:, s2, :, ATT_LO:ATT_LO + D_EDGE], full,
                                          att[:, s2, :, ATT_HI:ATT_HI + D_EDGE].bitcast(F32), ALU.subtract).then_inc(att_made, 1)

                    def evac_att(g, s, i):
                        dve.wait_ge(turned, g + 1)
                        dve.tensor_copy(attT[:, :], misc_ps[:, 0:G]).then_inc(attT_made, 1)

                    def lo_h(g, s, i):
                        for q in range(2):
                            dve.wait_ge(hT_hi_made, 2 * g + q + 1)
                            last = dve.scalar_tensor_tensor(hT[1][:, q, :, :].rearrange("p k e -> p (k e)"), hT_ps[q][:, :], 0.0,
                                                            hT[0][:, q, :, :].rearrange("p k e -> p (k e)").bitcast(F32),
                                                            ALU.max, ALU.subtract)
                        last.then_inc(hT_made, 1)

                    def lo_hid(g, s, i):
                        for b in range(2):
                            dve.wait_ge(hid_hi_made, 2 * g + b + 1)
                            last = dve.scalar_tensor_tensor(hid[1][:, 2 * b:2 * b + 2, :].rearrange("p k e -> p (k e)"),
                                                            hid_ps[b][:, :], 0.0,
                                                            hid[0][:, 2 * b:2 * b + 2, :].rearrange("p k e -> p (k e)").bitcast(F32),
                                                            ALU.max, ALU.subtract)
                        last.then_inc(hid_made, 1)

                    def lo_agg(g, s, i):
                        s2 = s % 2
                        dve.wait_ge(agg_hi_made, g + 1)
                        dve.tensor_tensor(aggs[1][:, s2, :, :], agg[:, s2, :, :], aggs[0][:, s2, :, :].bitcast(F32),
                                          ALU.subtract).then_inc(agg_lo_made, 1)

                    def scan(g, s, i):
                        dve.wait_ge(msg_made, g + 1)
                        dve.wait_ge(spread, g + 1)
                        for b in range(KD):
                            last = dve.tensor_tensor_scan(agg[:, s % 2, b, :], misc_ps[:, G:2 * G], msg[:, b, :],
                                                          agg[:, 1 - s % 2, b, G - 1:G], ALU.mult, ALU.add)
                        last.then_inc(scanned, 1)

                    def add_bias(g, s, i):
                        dve.wait_ge(gs_summed, g + 1)
                        if reached(g, 2):
                            dve.wait_ge(stored[(s + 2) % UN], 16 * (i + (s + 2) // UN))
                        for j in range(GT):
                            last = dve.tensor_tensor(gs[:, s % 2, j, :], gs_ps[j][:, :], ub1r[:, :], ALU.add)
                        last.then_inc(gs_made, 1)

                    dve.memset(agg[:, :, :, :], 0.0)
                    dve.memset(att[:, :, :, :].bitcast(F32), 0.0)
                    dve.memset(ones_r[:, :].bitcast(F32), 1.0)
                    dve.drain()
                    for part in (ATT_HI, ATT_HI2):
                        dve.memset(att[:, :, :, part + D_EDGE:part + D_EDGE + 1].bitcast(F32), 1.0)
                    dve.drain()
                    pipelined(dve, [(prepare, 1), (scale, 5), (stats, 4), (split_att, 4), (flags, 4), (scan, 7), (lo_agg, 7), (lo_hid, 6), (evac_att, 5),
                                    (lo_h, 5), (add_bias, 8)], GROUPS)

                @block.scalar
                def _(act):
                    def root(g, s, i):
                        act.wait_ge(stats_made, g + 1)
                        act.activation(sd[:, :], mv[:, :, 1], ACT.Sqrt, bias=eps[:, :]).then_inc(root_made, 1)

                    def evac_h(g, s, i):
                        act.wait_ge(turned, g + 1)
                        for q in range(2):
                            act.activation(hT[0][:, q, :, :].rearrange("p k e -> p (k e)"), hT_ps[q][:, :],
                                           ACT.Relu).then_inc(hT_hi_made, 1)

                    def apply(g, s, i):
                        act.wait_ge(scale_made, g + 1)
                        if reached(g, 2):
                            act.wait_ge(turned, g - 1)
                        for j in range(GT):
                            for q in range(2):
                                a = 2 * j + q
                                last = act.activation(xn[:, s % 2, j, q, :], xin[:, s, j, q, :], ACT.Identity,
                                                      scale=rstd[:, a:a + 1], bias=nmr[:, a:a + 1])
                        last.then_inc(normed, 1)

                    def evac_hid(g, s, i):
                        act.wait_ge(hid_summed, g + 1)
                        for b in range(2):
                            act.activation(hid[0][:, 2 * b:2 * b + 2, :].rearrange("p k e -> p (k e)"), hid_ps[b][:, :],
                                           ACT.Relu).then_inc(hid_hi_made, 1)

                    def hi_agg(g, s, i):
                        act.wait_ge(scanned, g + 1)
                        if reached(g, 2):
                            act.wait_ge(gs_summed, g - 1)
                        act.activation(aggs[0][:, s % 2, :, :], agg[:, s % 2, :, :], ACT.Copy).then_inc(agg_hi_made, 1)

                    def evac_msg(g, s, i):
                        act.wait_ge(msg_summed, g + 1)
                        if reached(g, 1):
                            act.wait_ge(scanned, g)
                        for m in range(KD):
                            last = act.activation(msg[:, m, :], msg_ps[:, m * G:(m + 1) * G], ACT.Identity, bias=mb2c[:, m:m + 1])
                        last.then_inc(msg_made, 1)

                    pipelined(act, [(evac_msg, 7), (apply, 5), (hi_agg, 7), (evac_hid, 6), (evac_h, 5), (root, 4)], GROUPS)

                @block.tensor
                def _(pe):
                    def turn(g, s, i):
                        pe.wait_ge(normed, g + 1)
                        if reached(g, 2):
                            pe.wait_ge(scanned, g - 1)
                        for q in range(2):
                            for j in range(GT):
                                for k in range(KD):
                                    pe.transpose(hT_ps[q][:, k * G + j * P:k * G + (j + 1) * P],
                                                 xn[:, s % 2, j, q, k * P:(k + 1) * P], ident[:, :])
                        pe.wait_ge(att_made, g + 1)
                        for j in range(GT):
                            mm = pe.transpose(misc_ps[:, j * P:(j + 1) * P], att[:, s % 2, j, :].bitcast(F32), ident[:, :])
                        mm.then_inc(turned, 1)

                    def hidden(g, s, i):
                        pe.wait_ge(hT_made, g + 1)
                        pe.wait_ge(attT_made, g + 1)
                        for m in range(KH):
                            o = hid_ps[m // 2][:, (m % 2) * G:(m % 2 + 1) * G]
                            mm = pe.matmul(o, mw1e[:, m * P:(m + 1) * P], attT[:, :], start=True, stop=False)
                            for w_part, h_part in PARTS:
                                for q in range(2):
                                    for k in range(KD):
                                        mm = pe.matmul(o, mw1[w_part][:, q * KD + k, m * P:(m + 1) * P], hT[h_part][:, q, k, :],
                                                       start=False, stop=((w_part, h_part) == PARTS[-1] and q == 1 and k == KD - 1))
                        mm.then_inc(hid_summed, 1)

                    def messages(g, s, i):
                        pe.wait_ge(hid_made, g + 1)
                        if reached(g, 1):
                            pe.wait_ge(msg_made, g)
                        for m in range(KD):
                            for w_part, h_part in PARTS:
                                for k in range(KH):
                                    mm = pe.matmul(msg_ps[:, m * G:(m + 1) * G], mw2[w_part][:, k, m * P:(m + 1) * P],
                                                   hid[h_part][:, k, :], start=((w_part, h_part) == PARTS[0] and k == 0),
                                                   stop=((w_part, h_part) == PARTS[-1] and k == KH - 1))
                        mm.then_inc(msg_summed, 1)
                        pe.wait_ge(flagged, g + 1)
                        pe.wait_ge(attT_made, g + 2 if not isinstance(g, int) else min(g + 2, GROUPS))
                        pe.matmul(misc_ps[:, G:2 * G], ones_r[:, :], same[:, s, :], start=True, stop=True).then_inc(spread, 1)

                    def aggregate(g, s, i):
                        pe.wait_ge(agg_lo_made, g + 1)
                        if reached(g, 1):
                            pe.wait_ge(gs_made, g)
                        for j in range(GT):
                            for w_part, a_part in PARTS:
                                for k in range(KD):
                                    mm = pe.matmul(gs_ps[j][:, :], aggs[a_part][:, s % 2, k, j * P:(j + 1) * P], uw1[w_part][:, KD + k, :],
                                                   start=((w_part, a_part) == PARTS[0] and k == 0),
                                                   stop=((w_part, a_part) == PARTS[-1] and k == KD - 1))
                        mm.then_inc(gs_summed, 1)

                    pipelined(pe, [(messages, 2), (hidden, 1), (turn, 0), (aggregate, 3)], GROUPS)

        end_phase()

        NT = 2
        STEPS = (NODE_TILES + NT - 1) // NT
        with ExitStack() as c:
            def t(name, shape, dt=F32):
                return c.enter_context(nc.sbuf_tensor("u_" + name, shape, dt))

            def ps(name):
                return c.enter_context(nc.psum_tensor("u_" + name, [P, 512], F32))

            def sm(name):
                return phase_sem("u_" + name)

            idx = t("idx", [P, UN, 2, NT], I32)
            xt = t("xt", [P, UN, NT, D])
            gb = t("gb", [P, UN, NT, HIDDEN])
            xn = t("xn", [P, 2, NT, D])
            st = t("st", [P, NT, 6])
            mv = t("mv", [P, NT, 2])
            sd = t("sd", [P, NT])
            rstd = t("rstd", [P, NT])
            res = t("res", [P, UN, NT, D])
            nmr = t("nmr", [P, NT])
            hT = [t(f"hT_{part}", [P, KD, NT * P], F32R) for part in ("hi", "lo")]
            ua = t("ua", [P, NT, HIDDEN])
            uT = [t(f"uT_{part}", [P, NT, KH, P], F32R) for part in ("hi", "lo")]
            ot = t("ot", [P, UN, NT, D])
            hT_ps = ps("hT_ps")
            U_ps = [ps(f"U_ps{j}") for j in range(NT)]
            uT_ps = [ps(f"uT_ps{j}") for j in range(NT)]
            O_ps = ps("O_ps")
            x_in, x1_in, gs_in, stored = ([sm(f"{n}{s}") for s in range(UN)] for n in ("x_in", "x1_in", "gs_in", "stored"))
            (idx_made, filled, stats_made, root_made, normed, res_made, turned, hT_made, u_summed, u_made, u_turned, uT_made,
             o_summed, o_made, scale_made, biased, hT_hi_made, uT_hi_made) = (sm(n) for n in (
                 "idx_made", "filled", "stats_made", "root_made", "normed", "res_made", "turned", "hT_made", "u_summed",
                 "u_made", "u_turned", "uT_made", "o_summed", "o_made", "scale_made", "biased", "hT_hi_made", "uT_hi_made"))
            last_step = STEPS - 1
            assert NODE_TILES - last_step * NT == 1

            def tiles(g):
                return 1 if isinstance(g, int) and g == last_step else NT

            with nc.Block() as block:
                @block.sync
                def _(sp):
                    def load(g, s, i):
                        if reached(g, UN):
                            sp.wait_ge(res_made, g - UN + 1)
                        if tiles(g) == NT:
                            sp.dma_start(xt[:, s, :, :], x[bass.ds(g * (NT * P), NT * P), :].rearrange("(j p) d -> p j d", p=P)).then_inc(x_in[s], 16)
                        else:
                            sp.dma_start(xt[0:LAST_ROWS, s, 0, :], x[g * NT * P:N_NODES, :]).then_inc(x_in[s], 16)

                    def store(g, s, i):
                        sp.wait_ge(o_made, g + 1)
                        if tiles(g) == NT:
                            sp.dma_start(out[bass.ds(g * (NT * P), NT * P), :].rearrange("(j p) d -> p j d", p=P), ot[:, s, :, :]).then_inc(stored[s], 16)
                        else:
                            sp.dma_start(out[g * NT * P:N_NODES, :], ot[0:LAST_ROWS, s, 0, :]).then_inc(stored[s], 16)

                    pipelined(sp, [(store, 8), (load, 0)], STEPS)
                    for s in range(UN):
                        sp.wait_ge(stored[s], 16 * len(range(s, STEPS, UN)))

                @block.gpsimd
                def _(pool):
                    def gathers(g, s, i):
                        pool.wait_ge(idx_made, g + 1)
                        pool.sem_inc(apart, 1)
                        pool.wait_ge(x_in[s], 16 * i + 16)
                        pool.sem_inc(apart, 1)
                        for j in range(tiles(g)):
                            pool.indirect_dma_start(
                                out=xt[:, s, j, :], out_offset=None, in_=X1,
                                in_offset=bass.IndirectOffsetOnAxis(ap=idx[:, s, 0, j:j + 1], axis=0),
                                bounds_check=NO_ROW - 1, oob_is_err=False).then_inc(x1_in[s], 16)

                    def message_gathers(g, s, i):
                        pool.wait_ge(filled, g + 1)
                        pool.sem_inc(apart, 1)
                        for j in range(tiles(g)):
                            pool.indirect_dma_start(
                                out=gb[:, s, j, :], out_offset=None, in_=GS,
                                in_offset=bass.IndirectOffsetOnAxis(ap=idx[:, s, 1, j:j + 1], axis=0),
                                bounds_check=NO_ROW - 1, oob_is_err=False).then_inc(gs_in[s], 16)

                    def bias(g, s, i):
                        n = tiles(g)
                        pool.wait_ge(res_made, g + 1)
                        pool.tensor_tensor(res[:, s, 0:n, :], res[:, s, 0:n, :],
                                           ub2r[:, :].unsqueeze(1).to_broadcast([P, n, D]), ALU.add).then_inc(biased, 1)

                    pipelined(pool, [(gathers, 0), (message_gathers, 2), (bias, 5)], STEPS)

                def arrived(eng, signals, g, s, i):
                    eng.wait_ge(signals[s], 16 * NT * i + 16 * tiles(g))

                @block.vector
                def _(dve):
                    def indices(g, s, i):
                        n = tiles(g)
                        if reached(i, 1):
                            dve.wait_ge(gs_in[s], 16 * NT * i)
                        dve.tensor_copy(idx[:, s, 0, 0:n], end_d[:, bass.ds(g * NT, n)])
                        dve.tensor_copy(idx[:, s, 1, 0:n], end_s[:, bass.ds(g * NT, n)]).then_inc(idx_made, 1)

                    def stats(g, s, i):
                        n = tiles(g)
                        arrived(dve, x1_in, g, s, i)
                        for j in range(n):
                            dve.bn_stats(st[:, j, :], xt[:, s, j, :])
                        dve.drain()
                        for j in range(n):
                            last = dve.bn_aggr(mv[:, j, :], st[:, j, :])
                        last.then_inc(stats_made, 1)

                    def scale(g, s, i):
                        n = tiles(g)
                        dve.wait_ge(root_made, g + 1)
                        dve.reciprocal(rstd[:, 0:n], sd[:, 0:n])
                        dve.drain()
                        dve.scalar_tensor_tensor(nmr[:, 0:n], mv[:, 0:n, 0], -1.0, rstd[:, 0:n], ALU.mult, ALU.mult).then_inc(scale_made, 1)

                    def residual(g, s, i):
                        n = tiles(g)
                        dve.wait_ge(normed, g + 1)
                        dve.scalar_tensor_tensor(res[:, s, 0:n, :], xn[:, s % 2, 0:n, :], 0.0, xt[:, s, 0:n, :], ALU.max, ALU.add).then_inc(res_made, 1)

                    def lo_h(g, s, i):
                        n = tiles(g)
                        dve.wait_ge(hT_hi_made, g + 1)
                        dve.scalar_tensor_tensor(hT[1][:, :, 0:n * P], hT_ps[:, :].rearrange("p (k e) -> p k e", k=KD)[:, :, 0:n * P], 0.0,
                                                 hT[0][:, :, 0:n * P].bitcast(F32), ALU.max, ALU.subtract).then_inc(hT_made, 1)

                    def lo_u(g, s, i):
                        for j in range(tiles(g)):
                            dve.wait_ge(uT_hi_made, 2 * g + j + 1)
                            last = dve.scalar_tensor_tensor(uT[1][:, j, :, :].rearrange("p k e -> p (k e)"), uT_ps[j][:, :], 0.0,
                                                            uT[0][:, j, :, :].rearrange("p k e -> p (k e)").bitcast(F32),
                                                            ALU.max, ALU.subtract)
                        last.then_inc(uT_made, 1)

                    def add_messages(g, s, i):
                        n = tiles(g)
                        dve.wait_ge(u_summed, g + 1)
                        arrived(dve, gs_in, g, s, i)
                        if reached(g, 1):
                            dve.wait_ge(u_turned, g)
                        for j in range(n):
                            last = dve.tensor_tensor(ua[:, j, :], U_ps[j][:, :], gb[:, s, j, :], ALU.add)
                        last.then_inc(u_made, 1)

                    def finish(g, s, i):
                        n = tiles(g)
                        dve.wait_ge(o_summed, g + 1)
                        dve.wait_ge(biased, g + 1)
                        if reached(i, 1):
                            dve.wait_ge(stored[s], 16 * i)
                        dve.tensor_tensor(ot[:, s, 0:n, :], O_ps[:, 0:n * D].rearrange("p (j d) -> p j d", d=D), res[:, s, 0:n, :],
                                          ALU.add).then_inc(o_made, 1)

                    pipelined(dve, [(finish, 8), (lo_u, 7), (scale, 4), (stats, 3), (add_messages, 6), (lo_h, 5), (residual, 4), (indices, 0)], STEPS)

                @block.scalar
                def _(act):
                    def fill(g, s, i):
                        if reached(g, UN):
                            act.wait_ge(u_made, g - UN + 1)
                        for j in range(tiles(g)):
                            last = act.activation(gb[:, s, j, :], ub1r[:, :], ACT.Copy)
                        last.then_inc(filled, 1)

                    def root(g, s, i):
                        n = tiles(g)
                        act.wait_ge(stats_made, g + 1)
                        act.activation(sd[:, 0:n], mv[:, 0:n, 1], ACT.Sqrt, bias=eps[:, :]).then_inc(root_made, 1)

                    def evac_h(g, s, i):
                        n = tiles(g)
                        act.wait_ge(turned, g + 1)
                        act.activation(hT[0][:, :, 0:n * P], hT_ps[:, :].rearrange("p (k e) -> p k e", k=KD)[:, :, 0:n * P],
                                       ACT.Relu).then_inc(hT_hi_made, 1)

                    def apply(g, s, i):
                        act.wait_ge(scale_made, g + 1)
                        if reached(g, 2):
                            act.wait_ge(turned, g - 1)
                            act.wait_ge(res_made, g - 1)
                        for j in range(tiles(g)):
                            last = act.activation(xn[:, s % 2, j, :], xt[:, s, j, :], ACT.Identity, scale=rstd[:, j:j + 1], bias=nmr[:, j:j + 1])
                        last.then_inc(normed, 1)

                    def evac_u(g, s, i):
                        act.wait_ge(u_turned, g + 1)
                        for j in range(tiles(g)):
                            act.activation(uT[0][:, j, :, :].rearrange("p k e -> p (k e)"), uT_ps[j][:, :], ACT.Relu).then_inc(uT_hi_made, 1)

                    pipelined(act, [(evac_u, 7), (apply, 4), (root, 3), (evac_h, 5), (fill, 2)], STEPS)

                @block.tensor
                def _(pe):
                    def turn(g, s, i):
                        pe.wait_ge(normed, g + 1)
                        for j in range(tiles(g)):
                            for k in range(KD):
                                mm = pe.transpose(hT_ps[:, k * NT * P + j * P:k * NT * P + (j + 1) * P],
                                                  xn[:, s % 2, j, k * P:(k + 1) * P], ident[:, :])
                        mm.then_inc(turned, 1)

                    def up(g, s, i):
                        pe.wait_ge(hT_made, g + 1)
                        if reached(g, 1):
                            pe.wait_ge(u_made, g)
                        for j in range(tiles(g)):
                            for w_part, h_part in PARTS:
                                for k in range(KD):
                                    mm = pe.matmul(U_ps[j][:, :], hT[h_part][:, k, j * P:(j + 1) * P], uw1[w_part][:, k, :],
                                                   start=((w_part, h_part) == PARTS[0] and k == 0),
                                                   stop=((w_part, h_part) == PARTS[-1] and k == KD - 1))
                        mm.then_inc(u_summed, 1)

                    def turn_u(g, s, i):
                        pe.wait_ge(u_made, g + 1)
                        if reached(g, 1):
                            pe.wait_ge(uT_made, g)
                        for j in range(tiles(g)):
                            for m in range(KH):
                                mm = pe.transpose(uT_ps[j][:, m * P:(m + 1) * P], ua[:, j, m * P:(m + 1) * P], ident[:, :])
                        mm.then_inc(u_turned, 1)

                    def down(g, s, i):
                        pe.wait_ge(uT_made, g + 1)
                        if reached(g, 1):
                            pe.wait_ge(o_made, g)
                        for j in range(tiles(g)):
                            for w_part, u_part in PARTS:
                                for m in range(KH):
                                    mm = pe.matmul(O_ps[:, j * D:(j + 1) * D], uT[u_part][:, j, m, :], uw2[w_part][:, m, :],
                                                   start=((w_part, u_part) == PARTS[0] and m == 0),
                                                   stop=((w_part, u_part) == PARTS[-1] and m == KH - 1))
                        mm.then_inc(o_summed, 1)

                    pipelined(pe, [(up, 1), (turn, 0), (down, 2), (turn_u, 1)], STEPS)


_INS = ["x", "src", "dst", "edge_attr_16", "L0_gnn_W1", "L0_gnn_al1", "L0_gnn_ar1", "L0_gnn_W2", "L0_gnn_al2",
        "L0_gnn_ar2", "L1_gnn_mW1", "L1_gnn_mb1", "L1_gnn_mW2", "L1_gnn_mb2", "L1_gnn_uW1", "L1_gnn_ub1",
        "L1_gnn_uW2", "L1_gnn_ub2"]


def kernel(**inputs):
    import numpy as _np
    import concourse.bacc as _bacc
    from concourse import mybir as _mybir
    from concourse.bass_utils import run_bass_kernel_spmd as _run

    nc = _bacc.Bacc("TRN2", target_bir_lowering=False, num_devices=1)
    arrays, args = {}, []
    for name in _INS:
        a = _np.ascontiguousarray(inputs[name])
        arrays[f"in_{name}"] = a
        args.append(nc.dram_tensor(f"in_{name}", a.shape, _mybir.dt.from_np(a.dtype), kind="ExternalInput").ap())
    out = nc.dram_tensor("out_dram", (N_NODES, D), _mybir.dt.float32, kind="ExternalOutput").ap()
    build(nc, *args, out)
    r = _run(nc, [arrays], core_ids=[0])
    return r.results[0]["out_dram"]
```
